# Optimizing a Trainium2 kernel written in Bass

```python
import numpy as np
import jax
import jax.numpy as jnp

def _softmax(x, axis=-1):
    return jax.nn.softmax(x, axis=axis)

def _gelu(x):
    return jax.nn.gelu(x, approximate=True)

def _silu(x):
    return jax.nn.silu(x)

def _sigmoid(x):
    return jax.nn.sigmoid(x)

def _layernorm(x, axis=-1, eps=1e-05):
    m = jnp.mean(x, axis=axis, keepdims=True)
    v = jnp.var(x, axis=axis, keepdims=True)
    return (x - m) / jnp.sqrt(v + eps)

def _scatter_add(tgt, idx, src, axis=0):
    return tgt.at[idx].add(src)

def _segment_sum(src, seg, n):
    return jax.ops.segment_sum(src, seg, n)
kernel_name = 'mk_decoder_preln_d1_seqx_r4_97a4d4'

def setup_inputs(seed: int=0):
    np.random.seed(seed)
    _w = jnp.asarray

    def _rec_inputs():
        import jax
        import jax.numpy as jnp
        _rk = jax.random.key(seed)
        x = -0.0003929 + 0.9999 * jax.random.normal(jax.random.fold_in(_rk, 1), (1, 2048, 256), jnp.float32)
        _lenS = 2048 - jax.random.randint(jax.random.fold_in(_rk, 7), (1,), 0, max(1, 2048 // 4) + 1, jnp.int32)
        _lenS2 = 1601 - jax.random.randint(jax.random.fold_in(_rk, 8), (1,), 0, max(1, 1601 // 4) + 1, jnp.int32)
        _ctx_768P = jax.random.normal(jax.random.fold_in(_rk, 11), (1, 16, 192), jnp.float32)
        _ctx_768c = jax.random.dirichlet(jax.random.fold_in(_rk, 511), 0.3 * jnp.ones((16,), jnp.float32), (1, 1601))
        _ctx_768t = jnp.einsum('bsk,bkd->bsd', _ctx_768c, _ctx_768P)
        _ctx_768t = _ctx_768t * jax.lax.rsqrt(jnp.mean(jnp.square(_ctx_768t)) + 1e-12) * 0.953939
        ctx_768 = -0.00055796 + 0.999787 * (_ctx_768t + 0.3 * jax.random.normal(jax.random.fold_in(_rk, 611), (1, 1601, 192), jnp.float32))
        return (x, ctx_768)
    x, ctx_768 = _rec_inputs()

    def _L0_attn_setup():
        import jax, jax.numpy as jnp
        import numpy as np
        import math
        D_MODEL = 256
        HEAD_DIM = 128
        BATCH, SEQ = (4, 1024)
        key = jax.random.key(seed)
        ks = jax.random.split(key, 10)
        s_in = 1.0 / math.sqrt(D_MODEL)
        s_out = 1.0 / math.sqrt(HEAD_DIM)
        x = jax.random.normal(ks[0], (BATCH, SEQ, D_MODEL), dtype=jnp.float32)
        wavelengths = jnp.arange(1, HEAD_DIM + 1, dtype=jnp.float32) * 2.0 * math.pi / HEAD_DIM
        phase_bias = jnp.zeros((HEAD_DIM,), dtype=jnp.float32)
        Wq = jax.random.uniform(ks[1], (HEAD_DIM, D_MODEL), jnp.float32, -s_in, s_in)
        bq = jax.random.uniform(ks[2], (HEAD_DIM,), jnp.float32, -s_in, s_in)
        Wk = jax.random.uniform(ks[3], (HEAD_DIM, D_MODEL), jnp.float32, -s_in, s_in)
        bk = jax.random.uniform(ks[4], (HEAD_DIM,), jnp.float32, -s_in, s_in)
        Wv = jax.random.uniform(ks[5], (HEAD_DIM, D_MODEL), jnp.float32, -s_in, s_in)
        bv = jax.random.uniform(ks[6], (HEAD_DIM,), jnp.float32, -s_in, s_in)
        Wo = jax.random.uniform(ks[7], (D_MODEL, HEAD_DIM), jnp.float32, -s_out, s_out)
        bo = jax.random.uniform(ks[8], (D_MODEL,), jnp.float32, -s_out, s_out)
        return {'x': x, 'wavelengths': wavelengths, 'phase_bias': phase_bias, 'Wq': Wq, 'bq': bq, 'Wk': Wk, 'bk': bk, 'Wv': Wv, 'bv': bv, 'Wo': Wo, 'bo': bo}
    _L0_attn_all = _L0_attn_setup()
    _L0_attn_in = {k: v for k, v in _L0_attn_all.items() if k in ('wavelengths', 'phase_bias', 'Wq', 'bq', 'Wk', 'bk', 'Wv', 'bv', 'Wo', 'bo')}
    del _L0_attn_all

    def _L0_xattn_setup():
        import jax, jax.numpy as jnp
        import numpy as np
        IMAGE_DIM = 256
        TEXT_DIM = 192
        NUM_HEADS = 16
        HEAD_DIM = IMAGE_DIM // NUM_HEADS
        key = jax.random.key(seed)
        ks = jax.random.split(key, 14)
        B, N, M = (4, 1024, 128)
        s_img = 1.0 / np.sqrt(IMAGE_DIM)
        s_txt = 1.0 / np.sqrt(TEXT_DIM)
        s_ff = 1.0 / np.sqrt(2 * IMAGE_DIM)
        return {'x': jax.random.normal(ks[0], (B, N, IMAGE_DIM), jnp.float32), 'y': jax.random.normal(ks[1], (B, M, TEXT_DIM), jnp.float32), 'Wq': jax.random.normal(ks[2], (IMAGE_DIM, IMAGE_DIM), jnp.float32) * s_img, 'bq': jax.random.normal(ks[3], (IMAGE_DIM,), jnp.float32) * s_img, 'Wk': jax.random.normal(ks[4], (TEXT_DIM, IMAGE_DIM), jnp.float32) * s_txt, 'bk': jax.random.normal(ks[5], (IMAGE_DIM,), jnp.float32) * s_txt, 'Wv': jax.random.normal(ks[6], (TEXT_DIM, IMAGE_DIM), jnp.float32) * s_txt, 'bv': jax.random.normal(ks[7], (IMAGE_DIM,), jnp.float32) * s_txt, 'W1': jax.random.normal(ks[8], (IMAGE_DIM, 2 * IMAGE_DIM), jnp.float32) * s_img, 'b1': jax.random.normal(ks[9], (2 * IMAGE_DIM,), jnp.float32) * s_img, 'W2': jax.random.normal(ks[10], (2 * IMAGE_DIM, IMAGE_DIM), jnp.float32) * s_ff, 'b2': jax.random.normal(ks[11], (IMAGE_DIM,), jnp.float32) * s_ff}
    _L0_xattn_all = _L0_xattn_setup()
    _L0_xattn_in = {k: v for k, v in _L0_xattn_all.items() if k in ('Wq', 'bq', 'Wk', 'bk', 'Wv', 'bv', 'W1', 'b1', 'W2', 'b2')}
    del _L0_xattn_all

    def _L0_ffn_setup():
        import jax, jax.numpy as jnp
        import numpy as np
        B, S, D, F, E = (4, 512, 256, 1024, 8)
        key = jax.random.key(seed)
        ks = jax.random.split(key, 7)
        s1 = 1.0 / np.sqrt(D)
        s2 = 1.0 / np.sqrt(F)
        x = jax.random.normal(ks[0], (B, S, D), dtype=jnp.float32)
        W1 = jax.random.uniform(ks[1], (E, D, F), jnp.float32, -s1, s1)
        b1 = jax.random.uniform(ks[2], (E, F), jnp.float32, -s1, s1)
        W2 = jax.random.uniform(ks[3], (E, F, D), jnp.float32, -s2, s2)
        b2 = jax.random.uniform(ks[4], (E, D), jnp.float32, -s2, s2)
        Wr = jax.random.uniform(ks[5], (D, E), jnp.float32, -s1, s1)
        br = jax.random.uniform(ks[6], (E,), jnp.float32, -s1, s1)
        return {'x': x, 'W1': W1, 'b1': b1, 'W2': W2, 'b2': b2, 'Wr': Wr, 'br': br}
    _L0_ffn_all = _L0_ffn_setup()
    _L0_ffn_in = {k: v for k, v in _L0_ffn_all.items() if k in ('W1', 'b1', 'W2', 'b2', 'Wr', 'br')}
    del _L0_ffn_all
    return {'x': x, 'ctx_768': ctx_768, 'L0_attn_wavelengths': _L0_attn_in['wavelengths'], 'L0_attn_phase_bias': _L0_attn_in['phase_bias'], 'L0_attn_Wq': _L0_attn_in['Wq'], 'L0_attn_bq': _L0_attn_in['bq'], 'L0_attn_Wk': _L0_attn_in['Wk'], 'L0_attn_bk': _L0_attn_in['bk'], 'L0_attn_Wv': _L0_attn_in['Wv'], 'L0_attn_bv': _L0_attn_in['bv'], 'L0_attn_Wo': _L0_attn_in['Wo'], 'L0_attn_bo': _L0_attn_in['bo'], 'L0_xattn_Wq': _L0_xattn_in['Wq'], 'L0_xattn_bq': _L0_xattn_in['bq'], 'L0_xattn_Wk': _L0_xattn_in['Wk'], 'L0_xattn_bk': _L0_xattn_in['bk'], 'L0_xattn_Wv': _L0_xattn_in['Wv'], 'L0_xattn_bv': _L0_xattn_in['bv'], 'L0_xattn_W1': _L0_xattn_in['W1'], 'L0_xattn_b1': _L0_xattn_in['b1'], 'L0_xattn_W2': _L0_xattn_in['W2'], 'L0_xattn_b2': _L0_xattn_in['b2'], 'L0_ffn_W1': _L0_ffn_in['W1'], 'L0_ffn_b1': _L0_ffn_in['b1'], 'L0_ffn_W2': _L0_ffn_in['W2'], 'L0_ffn_b2': _L0_ffn_in['b2'], 'L0_ffn_Wr': _L0_ffn_in['Wr'], 'L0_ffn_br': _L0_ffn_in['br']}

def reference(x, ctx_768, L0_attn_wavelengths, L0_attn_phase_bias, L0_attn_Wq, L0_attn_bq, L0_attn_Wk, L0_attn_bk, L0_attn_Wv, L0_attn_bv, L0_attn_Wo, L0_attn_bo, L0_xattn_Wq, L0_xattn_bq, L0_xattn_Wk, L0_xattn_bk, L0_xattn_Wv, L0_xattn_bv, L0_xattn_W1, L0_xattn_b1, L0_xattn_W2, L0_xattn_b2, L0_ffn_W1, L0_ffn_b1, L0_ffn_W2, L0_ffn_b2, L0_ffn_Wr, L0_ffn_br):
    import jax
    import jax.numpy as jnp

    def _L0_attn_ref(x, wavelengths, phase_bias, Wq, bq, Wk, bk, Wv, bv, Wo, bo):
        import jax, jax.numpy as jnp
        import numpy as np
        import math
        D_MODEL = 256
        HEAD_DIM = 128
        BATCH, SEQ = (4, 1024)
        Q = jnp.einsum('bsd,hd->bsh', x, Wq) + bq
        K = jnp.einsum('bsd,hd->bsh', x, Wk) + bk
        V = jnp.einsum('bsd,hd->bsh', x, Wv) + bv
        inv_w = 1.0 / (wavelengths + 1e-08)
        theta_q = Q * inv_w + phase_bias
        theta_k = K * inv_w + phase_bias
        sim = jnp.einsum('bqh,bkh->bqk', jnp.cos(theta_q), jnp.cos(theta_k)) + jnp.einsum('bqh,bkh->bqk', jnp.sin(theta_q), jnp.sin(theta_k))
        weights = jax.nn.softmax(sim / math.sqrt(HEAD_DIM), axis=-1)
        out = jnp.einsum('bqk,bkh->bqh', weights, V)
        return jnp.einsum('bqh,dh->bqd', out, Wo) + bo

    def _L0_xattn_ref(x, y, Wq, bq, Wk, bk, Wv, bv, W1, b1, W2, b2):
        import jax, jax.numpy as jnp
        import numpy as np
        IMAGE_DIM = 256
        TEXT_DIM = 192
        NUM_HEADS = 16
        HEAD_DIM = IMAGE_DIM // NUM_HEADS
        B, N, _ = x.shape
        M = y.shape[1]
        q = (x @ Wq + bq).reshape(B, N, NUM_HEADS, HEAD_DIM)
        k = (y @ Wk + bk).reshape(B, M, NUM_HEADS, HEAD_DIM)
        v = (y @ Wv + bv).reshape(B, M, NUM_HEADS, HEAD_DIM)
        scale = 1.0 / np.sqrt(HEAD_DIM)
        scores = jnp.einsum('bnhd,bmhd->bhnm', q, k) * scale
        attn = jax.nn.softmax(scores, axis=-1)
        out = jnp.einsum('bhnm,bmhd->bnhd', attn, v).reshape(B, N, IMAGE_DIM)
        h = jax.nn.relu(out @ W1 + b1)
        return h @ W2 + b2

    def _L0_ffn_ref(x, W1, b1, W2, b2, Wr, br):
        import jax, jax.numpy as jnp
        import numpy as np
        B, S, D, F, E = (4, 512, 256, 1024, 8)
        b, s, d = x.shape
        e = Wr.shape[1]
        logits = x @ Wr + br
        idx = jnp.argmax(logits, axis=-1)
        probs = jax.nn.softmax(logits, axis=-1)
        gates = jnp.take_along_axis(probs, idx[..., None], axis=-1)[..., 0]
        xf = x.reshape(-1, d)
        idxf = idx.reshape(-1)
        gf = gates.reshape(-1)
        out = jnp.zeros_like(xf)
        for ei in range(e):
            h = jax.nn.gelu(xf @ W1[ei] + b1[ei], approximate=False)
            y = h @ W2[ei] + b2[ei]
            mask = (idxf == ei).astype(xf.dtype)
            out = out + y * (gf * mask)[:, None]
        return out.reshape(b, s, d)
    x = x + _L0_attn_ref(_layernorm(x, axis=-1), L0_attn_wavelengths, L0_attn_phase_bias, L0_attn_Wq, L0_attn_bq, L0_attn_Wk, L0_attn_bk, L0_attn_Wv, L0_attn_bv, L0_attn_Wo, L0_attn_bo)
    x = x + _L0_xattn_ref(_layernorm(x, axis=-1), ctx_768, L0_xattn_Wq, L0_xattn_bq, L0_xattn_Wk, L0_xattn_bk, L0_xattn_Wv, L0_xattn_bv, L0_xattn_W1, L0_xattn_b1, L0_xattn_W2, L0_xattn_b2)
    x = x + _L0_ffn_ref(_layernorm(x, axis=-1), L0_ffn_W1, L0_ffn_b1, L0_ffn_W2, L0_ffn_b2, L0_ffn_Wr, L0_ffn_br)
    return x

_drawn_inputs = setup_inputs


def setup_inputs(seed=0):
    import zlib

    import numpy as np

    out = dict(_drawn_inputs(seed))
    spreads = {'L0_attn_phase_bias': (0.0, 2.0)}
    factors = {'L0_attn_wavelengths': 8.0,
     'L0_attn_Wq': 8.0,
     'L0_attn_bq': 43.484,
     'L0_attn_Wk': 8.0,
     'L0_attn_bk': 64.0,
     'L0_attn_Wv': 6.613,
     'L0_attn_bv': 2.719,
     'L0_attn_Wo': 2.706,
     'L0_xattn_bq': 5.908,
     'L0_xattn_bk': 64.0,
     'L0_ffn_b1': 8.0,
     'L0_ffn_b2': 8.0,
     'L0_ffn_br': 4.907}
    for name, (base, spread) in spreads.items():
        noise = np.random.default_rng([zlib.crc32(name.encode()), seed]).standard_normal(out[name].shape)
        drawn = base * np.exp(spread * noise) if base else spread * noise
        out[name] = jnp.asarray(drawn.astype(out[name].dtype))
    for name, factor in factors.items():
        out[name] = (out[name] * factor).astype(out[name].dtype)
    return out
```

```python
from contextlib import ExitStack
import math

import concourse.bass as bass
from concourse import mybir

F32 = mybir.dt.float32
BF16 = mybir.dt.bfloat16
I32 = mybir.dt.int32
U32 = mybir.dt.uint32
ALU = mybir.AluOpType
ACT = mybir.ActivationFunctionType
AX = mybir.AxisListType
ds = bass.ds

P = 128
T = 2048
D = 256
KD = D // P
NT = T // P
QC = 512
NQ = T // QC
TPC = QC // P
HD = 128
S_PAIRS = NT // 2
M = 1601
YD = 192
YC = YD // 2
NH = 16
DH = D // NH
G = 4
NG = NH // G
MT = -(-M // P)
MLAST = M - (MT - 1) * P
VW = DH + 1
F1 = 512
NF1 = F1 // P
E = 8
F = 1024
NF = F // P
NB = (T + E * (P - 1)) // P
KCH = [(0, 400), (400, 400), (800, 400), (1200, 401)]
PARTS_Q = [0, 0, 0, 1, 1, 2]
PARTS_K = [0, 1, 2, 0, 1, 0]
RS = 6 * DH
RK = RS + 3
EPS = 1e-5
TWO_PI = 2.0 * math.pi
C1 = 6.28125
C2 = TWO_PI - C1
MAGIC = 1.5 * 2.0 ** 23
PI_IN = 3.14159250


TAIL_LINKS = 34


LEAST_RECIPROCAL = 1e-30


class Chain:

    def __init__(self, eng, sem):
        self.eng, self.sem, self.base, self.n = eng, sem, 0, 0

    def inc(self, ins):
        self.n += 1
        ins.then_inc(self.sem, 1)

    def wait(self):
        self.eng.wait_ge(self.sem, self.base + self.n)

    def link(self, ins):
        self.inc(ins)
        self.wait()

    def enter(self, i, per):
        self.saved = (self.base + self.n, per)
        self.base, self.n = i * per + (self.base + self.n), 0

    def leave(self, count):
        start, per = self.saved
        assert self.n == per, (self.n, per)
        self.base, self.n = start + count * per, 0


def layer(nc, a, out):
    ctx = ExitStack()
    with ctx:
        def sb(name, shape, dt=F32):
            return ctx.enter_context(nc.sbuf_tensor(name, shape, dt))

        def sem(name):
            return ctx.enter_context(nc.semaphore(name))

        k_parts = nc.dram_tensor("k_parts", [3, D, M], BF16, kind="Internal").ap()
        q_parts = nc.dram_tensor("q_parts", [3, D, T], BF16, kind="Internal").ap()
        b1_parts = nc.dram_tensor("b1_parts", [3, E * F], BF16, kind="Internal").ap()
        x_slots = nc.dram_tensor("x_slots", [NB * P, D], F32, kind="Internal").ap()
        y_slots = nc.dram_tensor("y_slots", [NB * P, D], F32, kind="Internal").ap()

        res = sb("res", [P, NT, D])
        w1e = sb("w1e", [P, KD * E * F])
        arena = sb("arena", [P, 16384])
        duo = sb("duo", [P, 4096 + 2048])
        pbuf = sb("pbuf", [P, 4, 1024])
        vbuf = sb("vbuf", [P, 3600])
        ident = sb("ident", [P, P])
        ones = sb("ones", [P, P])
        tri = sb("tri", [P, P])
        cols = sb("cols", [P, 13])
        rows = sb("rows", [P, D + E])
        b1f = sb("b1f", [P, E * F // P])
        b1r = sb("b1r", [P, E * F // P])
        b1s = sb("b1s", [P, 3, E * F // P], BF16)
        ones_b = sb("ones_b", [3, P], BF16)
        w1_x = sb("w1_x", [P, KD, F1])
        wr = sb("wr", [P, KD, E])
        inv_w = sb("inv_w", [P, 2])
        bqk = sb("bqk", [P, 2])
        half_pi = sb("half_pi", [P, 1])
        ksum = sb("ksum", [P, KD, 4])
        kneg = sb("kneg", [P, KD])
        stats = sb("stats", [P, TPC, 6])
        mv = sb("mv", [P, TPC, 2])
        rstd = sb("rstd", [P, TPC])
        nt1 = sb("nt1", [P, TPC])
        nv = sb("nv", [P, TPC])
        rden_x = sb("rden_x", [P, TPC, G])
        rmin = sb("rmin", [P, TPC, G])
        small = sb("small", [P, 2])
        again = sb("again", [P, 1], I32)

        yT = w1e[0:YC, 0:2 * M].rearrange("p (c m) -> p c m", c=2)
        wk_x = w1e[0:YC, 3328:3840].rearrange("p (c n) -> p c n", c=2)
        wv_x = w1e[0:YC, 3840:4352].rearrange("p (c n) -> p c n", c=2)
        wqkv = w1e[:, 4352:5120].rearrange("p (w c n) -> p w c n", w=3, c=KD)
        bo_b = w1e[:, 9984:10240]
        wq_x = w1e[:, 15360:15872].rearrange("p (c n) -> p c n", c=KD)
        wo_s = w1e[:, 15872:16128]
        bv_b = w1e[:, 16128:16384]
        k_bf = w1e[:, 5120:5120 + 4864].bitcast(BF16)[:, 0:3 * KD * M].rearrange("p (j c m) -> p j c m", j=3, c=KD)
        kr = w1e[:, 10240:10240 + KD * M].rearrange("p (c m) -> p c m", c=KD)
        xo = duo[:, 0:4096].rearrange("p (t n) -> p t n", t=NT)
        kf = duo[:, 0:KD * M].rearrange("p (c m) -> p c m", c=KD)
        b1p = duo[0:3, 0:4096].bitcast(BF16)
        xT = [duo[:, 4096 + 1024 * b:5120 + 1024 * b].rearrange("p (k t) -> p k t", k=KD) for b in range(2)]
        sc = [arena[:, 4096 * w:4096 * w + 4096].rearrange("p (c t) -> p c t", c=2) for w in range(2)]
        v_s = arena[:, 8192:10240].rearrange("p (t n) -> p t n", t=NT)
        aT = arena[:, 10240:10752]
        o_raw = arena[:, 10752:11264]
        th = arena[:, 11264:12288].rearrange("p (w n) -> p w n", w=2)
        tn = arena[:, 12288:13312].rearrange("p (w n) -> p w n", w=2)
        acc = arena[:, 11264:12288]
        acc1 = arena[:, 12288:12800]
        rden = arena[:, 12800:13312]
        xn2 = arena[:, 13312:14336].rearrange("p (t n) -> p t n", t=TPC)
        qf = arena[:, 14336:15360].rearrange("p (c n) -> p c n", c=KD)
        q_bf = w1e[:, 13824:13824 + 1536].bitcast(BF16).rearrange("p (j c n) -> p j c n", j=3, c=KD)
        zero = arena[:, 14848:14848 + D]
        w2_x = arena[:, 15360:16384].rearrange("p (f n) -> p f n", f=NF1)
        qr = w1e[:, 12800:13824].rearrange("p (c n) -> p c n", c=KD)
        qst = [arena[0:RK, 4096 * b:4096 * b + 4096].bitcast(BF16).rearrange("p (h t) -> p h t", h=G) for b in range(2)]
        kst = [arena[0:RK, 8192 + 3204 * b:8192 + 3204 * b + 3202].bitcast(BF16).rearrange("p (h m) -> p h m", h=G)
               for b in range(2)]
        gp = pbuf[:, :, :].rearrange("p a n -> p (a n)")[:, 0:M]
        gpT = pbuf[:, 2:4, :].rearrange("p a n -> p (a n)")[:, 0:MT * P].rearrange("p (t n) -> p t n", n=P)
        gq, gk = qst[0][0:RS, 0, :], kst[0][0:RS, 0, :]
        oT = arena[:, 14848:14848 + QC]
        w2e = arena[:, :].rearrange("p (e n) -> p e n", e=E)
        w1v = w1e[:, :].rearrange("p (k n) -> p k n", k=KD)
        xn = pbuf[:, :, :].rearrange("p a (t n) -> p (a t) n", n=D)
        hs = [pbuf[:, b, :] for b in range(2)]
        hT = [pbuf[:, 2 + b, :].rearrange("p (f n) -> p f n", f=NF) for b in range(2)]
        vx = vbuf[:, 0:MT * NH * VW].rearrange("p (t n) -> p t n", t=MT)
        h_x = vbuf[:, 0:NF1 * QC].rearrange("p (f n) -> p f n", f=NF1)
        xn3T = vbuf[:, 2048:3072].rearrange("p (k n) -> p k n", k=KD)
        b2e = vbuf[:, 0:2048]
        xg = [vbuf[:, 2048 + 256 * b:2304 + 256 * b] for b in range(2)]
        xgT = [vbuf[:, 2560 + 256 * b:2816 + 256 * b].rearrange("p (k n) -> p k n", k=KD) for b in range(2)]
        ys = [vbuf[:, 3072 + 256 * b:3328 + 256 * b] for b in range(2)]
        lg, l2, rank, tot, oneh, *incl = [vbuf[:, P * i:P * i + P].rearrange("p (t e) -> p t e", e=E) for i in range(7)]
        revi = sb("revi", [P, E])
        lmax = sb("lmax", [P, NT])
        gate = sb("gate", [P, NT])
        top = sb("top", [P, NT])
        nb = sb("nb", [P, E])
        cum = [sb(f"cum{i}", [P, E]) for i in range(2)]
        slot_f = sb("slot_f", [P, NT])
        slot = sb("slot", [P, NT], U32)
        bl_i = sb("bl_i", [P, 24])
        bl_c = vbuf[:, 1024:1024 + 24 * E].rearrange("p (b e) -> p b e", e=E)
        bl_f = sb("bl_f", [P, 24])
        bl_e = sb("bl_e", [P, 24], I32)
        yt = xn

        psum = ctx.enter_context(nc.psum_tensor("psum", [P, 8, 512], F32))

        ld_y = sem("ld_y"); ld_small = sem("ld_small"); ld_x = [sem(f"ld_x{q}") for q in range(NQ)]
        ld_ws = sem("ld_ws"); ld_w1e = sem("ld_w1e"); ld_w2e = sem("ld_w2e"); ld_b1e = sem("ld_b1e"); ld_b2e = sem("ld_b2e")
        consts = sem("consts"); zero_ok = sem("zero_ok"); zeroed = sem("zeroed")
        dve_own = sem("dve_own"); pool_own = sem("pool_own"); act_own = sem("act_own")
        k_proj = sem("k_proj"); k_evac = sem("k_evac"); k_split = sem("k_split"); k_stored = sem("k_stored")
        v_proj = sem("v_proj"); v_evac = sem("v_evac"); o_clear = sem("o_clear")
        col_ok = sem("col_ok"); xn_ok = sem("xn_ok"); xn_T = sem("xn_T"); xT_ok = sem("xT_ok")
        qkv_mm = sem("qkv_mm"); th_ok = sem("th_ok"); v_ok = sem("v_ok"); ang_ok = sem("ang_ok"); sc_ok = sem("sc_ok")
        bo_added = sem("bo_added")
        s_mm = sem("s_mm"); s_exp = sem("s_exp"); s_pv = sem("s_pv"); s_acc = sem("s_acc"); o_evac = sem("o_evac")
        acc_ok = sem("acc_ok"); den_mm = sem("den_mm"); aT_ok = sem("aT_ok"); wo_mm = sem("wo_mm"); res_ok = sem("res_ok")
        xn2_ok = sem("xn2_ok"); xn2_T = sem("xn2_T"); x2T_ok = sem("x2T_ok"); q_mm = sem("q_mm"); q_ok = sem("q_ok")
        q_split = sem("q_split"); q_stored = sem("q_stored")
        st_rows = sem("st_rows"); st_ld = [sem(f"st_ld{g}") for g in range(NG)]
        c_mm = sem("c_mm"); c_exp = sem("c_exp"); c_pv = sem("c_pv"); c_evac = sem("c_evac"); c_tr = sem("c_tr"); c_xo = sem("c_xo")
        bad_ok = sem("bad_ok"); bad_mm = sem("bad_mm"); flag_ok = sem("flag_ok")
        m_ld = sem("m_ld"); m_mm = sem("m_mm"); m_max = sem("m_max"); m_exp = sem("m_exp"); m_tr = sem("m_tr")
        m_pT = sem("m_pT"); m_pv = sem("m_pv"); m_out = sem("m_out"); m_red = sem("m_red")
        b2_added = sem("b2_added"); b1_stored = sem("b1_stored")
        f_tr = sem("f_tr"); f_xT = sem("f_xT"); f_h = sem("f_h"); f_relu = sem("f_relu"); f_y = sem("f_y"); f_res = sem("f_res")
        xn3_ok = sem("xn3_ok"); r_tr = sem("r_tr"); r_xT = sem("r_xT"); r_lg = sem("r_lg")
        r_sub = sem("r_sub"); r_exp = sem("r_exp"); r_one = sem("r_one"); r_rank = sem("r_rank"); r_slot = sem("r_slot"); r_blk = sem("r_blk")
        dispatched = sem("dispatched")
        g_ld = [sem(f"g_ld{b}") for b in range(2)]; g_tr = sem("g_tr"); g_xT = sem("g_xT"); g_h = sem("g_h")
        g_act = sem("g_act"); g_ht = sem("g_ht"); g_hTa = sem("g_hTa"); g_hTd = sem("g_hTd"); g_y = sem("g_y"); g_ys = sem("g_ys")
        g_st = [sem(f"g_st{b}") for b in range(2)]
        y_in = [sem(f"y_in{t}") for t in range(NT)]; o_ok = sem("o_ok"); o_st = sem("o_st")

        block = ctx.enter_context(nc.Block())

        BQ, PH, WL, BV = 0, 1, 2, 4
        BK = 3
        XBQ, XBK, XB1 = 5, 7, 9
        b2_b, br_b = rows[:, 0:D], rows[:, D:D + E]

        @block.sync
        def _(sp):
            sp.dma_start(yT, a["yT"].rearrange("(c p) m -> p c m", c=2)).then_inc(ld_y, 16)
            sp.dma_start(wk_x, a["xwk"].rearrange("(c p) n -> p c n", c=2)).then_inc(ld_y, 16)
            sp.dma_start(wv_x, a["xwv"].rearrange("(c p) n -> p c n", c=2)).then_inc(ld_y, 16)
            sp.dma_start(wqkv, a["wqkv"].rearrange("w (c p) n -> p w c n", c=KD)).then_inc(ld_ws, 16)
            sp.dma_start(wo_s, a["wo"]).then_inc(ld_ws, 16)
            sp.dma_start(wq_x, a["xwq"].rearrange("(c p) n -> p c n", c=KD)).then_inc(ld_ws, 16)
            sp.dma_start(w1_x[:, :, :], a["xw1"].rearrange("(c p) n -> p c n", c=KD)).then_inc(ld_ws, 16)
            sp.dma_start(w2_x, a["xw2"].rearrange("(c p) n -> p c n", c=NF1)).then_inc(ld_ws, 16)
            sp.dma_start(wr[:, :, :], a["wr"].rearrange("(c p) n -> p c n", c=KD)).then_inc(ld_ws, 16)
            sp.wait_ge(zero_ok, 1)
            for b in range(NB):
                sp.dma_start(x_slots[b * P:b * P + P, :], zero).then_inc(zeroed, 16)
            sp.wait_ge(k_split, 1)
            for j in range(3):
                sp.dma_start(k_parts[j].rearrange("(c p) m -> p c m", c=KD), k_bf[:, j]).then_inc(k_stored, 16)
            for j in range(3):
                sp.dma_start(b1_parts[j].rearrange("(p n) -> p n", p=P), b1s[:, j]).then_inc(b1_stored, 16)
            for u in range(NQ):
                sp.wait_ge(q_split, u + 1)
                for j in range(3):
                    sp.dma_start(q_parts[j, :, u * QC:u * QC + QC].rearrange("(c p) t -> p c t", c=KD),
                                 q_bf[:, j]).then_inc(q_stored, 16)
            for g in range(NG):
                if g == 0:
                    sp.wait_ge(v_proj, MT)
                    sp.wait_ge(k_stored, 48)
                    sp.wait_ge(q_stored, 48 * NQ)
                    sp.wait_ge(s_pv, NT // 2 * NQ)
                if g >= 2:
                    sp.wait_ge(c_mm, 2 * MT * NQ * (g - 1))
                for r in range(6):
                    sp.dma_start(kst[g % 2][r * DH:(r + 1) * DH, :, :],
                                 k_parts[PARTS_K[r], g * G * DH:(g + 1) * G * DH, :].rearrange("(h d) m -> d h m", d=DH)
                                 ).then_inc(st_ld[g], 16)
                    sp.dma_start(qst[g % 2][r * DH:(r + 1) * DH, :, :],
                                 q_parts[PARTS_Q[r], g * G * DH:(g + 1) * G * DH, :].rearrange("(h d) t -> d h t", d=DH)
                                 ).then_inc(st_ld[g], 16)
                if g == 0:
                    for k in range(KD):
                        sp.dma_start(w1v[:, k, :].rearrange("p (e f) -> p e f", e=E),
                                     a["w1"][:, k * P:k * P + P, :].rearrange("e p f -> p e f")).then_inc(ld_w1e, 16)
            sp.wait_ge(flag_ok, 1)
            with sp.If(sp.value_load(again[0:1, 0:1], min_val=0, max_val=P) > 0):
                with sp.Fori(0, NH) as h:
                    sp.wait_ge(m_out, NT * h + 1)
                    for r in range(6):
                        sp.dma_start(gk[r * DH:(r + 1) * DH, :], k_parts[PARTS_K[r], ds(h * DH, DH), :]).then_inc(m_ld, 16)
                        sp.dma_start(gq[r * DH:(r + 1) * DH, :], q_parts[PARTS_Q[r], ds(h * DH, DH), :]).then_inc(m_ld, 16)
                sp.wait_ge(m_pv, NT * NH)
            sp.wait_ge(c_mm, 2 * MT * NQ * NG)
            sp.wait_ge(c_tr, NQ * NG)
            for e in range(E):
                if e == E - 1:
                    sp.wait_ge(f_tr, KD * NQ)
                    sp.wait_ge(b1_stored, 48)
                    sp.dma_start(b1p, b1_parts).then_inc(ld_b1e, 16)
                    sp.wait_ge(f_y, NQ)
                sp.dma_start(w2e[:, e, :].rearrange("p (f n) -> p f n", f=NF),
                             a["w2"][e].rearrange("(f p) n -> p f n", f=NF)).then_inc(ld_w2e, 16)
            sp.wait_ge(r_blk, 1)
            sp.dma_start(b2e, a["b2"].partition_broadcast(P)).then_inc(ld_b2e, 16)

            sp.wait_ge(dispatched, 16 * NT)
            sp.wait_ge(r_lg, NT)

            def load(b, j):
                sp.dma_start(xg[j], x_slots[ds(b * P, P), :]).then_inc(g_ld[j], 16)

            def store(b, j):
                sp.wait_ge(g_ys, b + 1)
                sp.dma_start(y_slots[ds(b * P, P), :], ys[j]).then_inc(g_st[j], 16)

            load(0, 0)
            load(1, 1)
            with sp.Fori(0, (NB - 3) // 2) as i:
                for j in range(2):
                    b = 2 * i + j
                    sp.wait_ge(g_tr, b + 1)
                    load(b + 2, j)
                    store(b, j)
            sp.wait_ge(g_tr, NB - 2)
            load(NB - 1, 0)
            for b in range(NB - 3, NB):
                store(b, b % 2)
            for t in range(NT):
                sp.wait_ge(o_ok, t + 1)
                sp.dma_start(out.rearrange("b (t p) n -> p (b t) n", p=P)[:, t, :], res[:, t, :]).then_inc(o_st, 16)
            sp.wait_ge(o_st, 16 * NT)

        @block.gpsimd
        def _(pool):
            ch = Chain(pool, pool_own)
            pool.memset(zero, 0.0).then_inc(zero_ok, 1)
            pool.memset(half_pi[:, :], math.pi / 2).then_inc(consts, 1)
            pool.memset(ones[:, :], 1.0).then_inc(consts, 1)
            pool.memset(ones_b[:, :], 1.0).then_inc(consts, 1)
            ch.inc(pool.memset(ident[:, :], 0.0))
            ch.inc(pool.memset(tri[:, :], 1.0))
            ch.wait()
            pool.affine_select(out=ident[:, :], in_=ident[:, :], compare_op=ALU.not_equal, fill=1.0, base=0,
                               pattern=[[-1, P]], channel_multiplier=1).then_inc(consts, 1)
            pool.affine_select(out=tri[:, :], in_=tri[:, :], compare_op=ALU.is_gt, fill=0.0, base=0,
                               pattern=[[1, P]], channel_multiplier=-1).then_inc(consts, 1)
            pool.iota(revi[:, :], [[-1, E]], base=E, channel_multiplier=0,
                      allow_small_or_imprecise_dtypes=True).then_inc(consts, 1)
            pool.iota(bl_i[:, :], [[1, 24]], base=0, channel_multiplier=0,
                      allow_small_or_imprecise_dtypes=True).then_inc(consts, 1)

            pool.wait_ge(k_evac, 2 * len(KCH))
            pool.wait_ge(ld_small, 80)
            ch.link(pool.tensor_tensor(ksum[:, :, 0:2], ksum[:, :, 0:2], ksum[:, :, 2:4], ALU.add))
            ch.link(pool.tensor_tensor(ksum[:, :, 0:1], ksum[:, :, 0:1], ksum[:, :, 1:2], ALU.add))
            ch.link(pool.tensor_scalar(kneg[:, :], ksum[:, :, 0], -1.0 / M, None, ALU.mult))
            for c in range(KD):
                ch.inc(pool.tensor_scalar(kf[:, c], kf[:, c], kneg[:, c:c + 1], None, ALU.add))
            ch.wait()
            ch.link(pool.tensor_copy(k_bf[:, 0], kf[:, :, :]))
            ch.link(pool.tensor_tensor(kr, kf, k_bf[:, 0], ALU.subtract))
            ch.link(pool.tensor_copy(k_bf[:, 1], kr))
            ch.link(pool.tensor_tensor(kf, kr, k_bf[:, 1], ALU.subtract))
            ch.inc(pool.tensor_copy(k_bf[:, 2], kf))
            ch.link(pool.tensor_copy(b1s[:, 0], b1f[:, :]))
            ch.link(pool.tensor_tensor(b1r[:, :], b1f[:, :], b1s[:, 0], ALU.subtract))
            ch.link(pool.tensor_copy(b1s[:, 1], b1r[:, :]))
            ch.link(pool.tensor_tensor(b1r[:, :], b1r[:, :], b1s[:, 1], ALU.subtract))
            pool.tensor_copy(b1s[:, 2], b1r[:, :]).then_inc(k_split, 1)

            for q in range(NQ):
                pool.wait_ge(xn_ok, q + 1)
                r = res[:, q * TPC:(q + 1) * TPC, :]
                pool.tensor_tensor(r, r, bo_b.unsqueeze(1).to_broadcast([P, TPC, D]), ALU.add).then_inc(bo_added, 1)

            for u in range(NQ):
                pool.wait_ge(q_ok, 2 * u + 2)
                if u:
                    pool.wait_ge(q_stored, 48 * u)
                ch.link(pool.tensor_copy(q_bf[:, 0], qf))
                ch.link(pool.tensor_tensor(qr, qf, q_bf[:, 0], ALU.subtract))
                ch.link(pool.tensor_copy(q_bf[:, 1], qr))
                ch.link(pool.tensor_tensor(qr, qr, q_bf[:, 1], ALU.subtract))
                pool.tensor_copy(q_bf[:, 2], qr).then_inc(q_split, 1)

            pool.wait_ge(s_pv, NT // 2 * NQ)
            pool.wait_ge(q_split, NQ)
            for b in range(2):
                pool.memset(kst[b][RS:RK, :, :], 1.0).then_inc(st_rows, 1)
                pool.memset(qst[b][RS:RK, :, :], 0.0).then_inc(st_rows, 1)
            pool.wait_ge(xn2_ok, NQ)
            pool.wait_ge(st_rows, 4)
            pool.tensor_tensor(res[:, :, :], res[:, :, :], b2_b.unsqueeze(1).to_broadcast([P, NT, D]), ALU.add).then_inc(b2_added, 1)

            pool.wait_ge(zeroed, 16 * NB)
            pool.wait_ge(r_slot, 1)
            for t in range(NT):
                pool.indirect_dma_start(out=x_slots[:, :], out_offset=bass.IndirectOffsetOnAxis(ap=slot[:, t:t + 1], axis=0),
                                        in_=xn[:, t, :], in_offset=None).then_inc(dispatched, 16)
            pool.wait_ge(g_st[0], 16 * ((NB + 1) // 2))
            pool.wait_ge(g_st[1], 16 * (NB // 2))
            for t in range(NT):
                pool.indirect_dma_start(out=yt[:, t, :], out_offset=None, in_=y_slots[:, :],
                                        in_offset=bass.IndirectOffsetOnAxis(ap=slot[:, t:t + 1], axis=0)).then_inc(y_in[t], 16)

        @block.tensor
        def _(pe):
            def bank(i, n=512, p=P):
                return psum[0:p, i, 0:n]

            pe.wait_ge(ld_y, 48)
            for j, (m0, mn) in enumerate(KCH):
                for c in range(KD):
                    i = 2 * j + c
                    if i >= 4:
                        pe.wait_ge(k_evac, i - 3)
                    for y in range(2):
                        mm = pe.matmul(bank(i % 4, mn), wk_x[:, y, c * P:c * P + P], yT[:, y, m0:m0 + mn], start=(y == 0), stop=(y == 1))
                    mm.then_inc(k_proj, 1)
            for t in range(MT):
                n = P if t < MT - 1 else MLAST
                if t >= 2:
                    pe.wait_ge(v_evac, t - 1)
                for y in range(2):
                    mm = pe.matmul(bank(4 + t % 2, D, n), yT[:, y, t * P:t * P + n], wv_x[:, y, :], start=(y == 0), stop=(y == 1))
                mm.then_inc(v_proj, 1)

            pe.wait_ge(consts, 7)
            pe.wait_ge(ld_ws, 96)
            for q in range(NQ):
                pe.wait_ge(xn_ok, q + 1)
                for k in range(KD):
                    if q:
                        pe.wait_ge(xT_ok, 2 * (q - 1) + k + 1)
                    for t in range(TPC):
                        mm = pe.transpose(psum[:, 6 + k, t * P:t * P + P], xn[:, q * TPC + t, k * P:k * P + P], ident[:, :])
                    mm.then_inc(xn_T, 1)
                pe.wait_ge(xT_ok, 2 * q + 2)
                b0 = 0 if q % 2 == 0 else 3
                if q < 1:
                    pe.wait_ge(k_evac, 8)
                if q == 1:
                    pe.wait_ge(v_evac, MT)
                for w in range(2):
                    if q >= 2:
                        pe.wait_ge(th_ok, 2 * (q - 2) + w + 1)
                    for k in range(KD):
                        mm = pe.matmul(bank(b0 + w), wqkv[:, w, k, :], xT[q % 2][:, k, :], start=(k == 0), stop=(k == KD - 1))
                    mm.then_inc(qkv_mm, 1)
                if q >= 2:
                    pe.wait_ge(v_ok, q - 1)
                for t in range(TPC):
                    for k in range(KD):
                        mm = pe.matmul(psum[:, b0 + 2, t * P:t * P + P], xT[q % 2][:, k, t * P:t * P + P], wqkv[:, 2, k, :],
                                       start=(k == 0), stop=(k == KD - 1))
                mm.then_inc(qkv_mm, 1)

            def scores(u, i):
                n = S_PAIRS * u + i
                if not (isinstance(u, int) and n < 2):
                    pe.wait_ge(s_exp, n - 1)
                for h in range(2):
                    kt = 2 * i + h
                    for c in range(2):
                        mm = pe.matmul(bank(2 * (i % 2) + h), sc[1][:, c, kt * P:kt * P + P], sc[0][:, c, ds(u * QC, QC)],
                                       start=(c == 0), stop=(c == 1))
                mm.then_inc(s_mm, 1)

            def pv(u, i):
                n = S_PAIRS * u + i
                pe.wait_ge(s_exp, n + 1)
                if i == 0 and not (isinstance(u, int) and u == 0):
                    pe.wait_ge(o_evac, u)
                for h in range(2):
                    kt = 2 * i + h
                    mm = pe.matmul(bank(4), v_s[:, kt, :], pbuf[:, i % 4, h * QC:h * QC + QC], start=(kt == 0), stop=(kt == NT - 1))
                mm.then_inc(s_pv, 1)

            def tail_den(u):
                pe.wait_ge(acc_ok, u + 1)
                pe.matmul(bank(5), ones[:, :], acc1, start=True, stop=True).then_inc(den_mm, 1)

            def tail_wo(u):
                pe.wait_ge(aT_ok, u + 1)
                for t in range(TPC):
                    mm = pe.matmul(psum[:, 6 + t // 2, (t % 2) * D:(t % 2) * D + D], aT[:, t * P:t * P + P], wo_s, start=True, stop=True)
                mm.then_inc(wo_mm, 1)

            def tail_turn(u):
                pe.wait_ge(xn2_ok, u + 1)
                for k in range(KD):
                    for t in range(TPC):
                        mm = pe.transpose(psum[:, 6 + k, t * P:t * P + P], xn2[:, t, k * P:k * P + P], ident[:, :])
                    mm.then_inc(xn2_T, 1)

            def tail_q(u):
                pe.wait_ge(x2T_ok, 2 * u + 2)
                for c in range(KD):
                    for k in range(KD):
                        mm = pe.matmul(bank(5 + c), wq_x[:, k, c * P:c * P + P], xT[0][:, k, :], start=(k == 0), stop=(k == KD - 1))
                    mm.then_inc(q_mm, 1)

            def self_unit(u, first):
                for i in range(S_PAIRS):
                    if i == S_PAIRS - 1 and not first:
                        pe.wait_ge(q_ok, 2 * u)
                    scores(u, i)
                    if i:
                        pv(u, i - 1)
                    elif not first:
                        pv(u - 1, S_PAIRS - 1)
                    if not first:
                        if i == 1:
                            tail_den(u - 1)
                        if i == 2:
                            tail_wo(u - 1)
                        if i == 4:
                            tail_turn(u - 1)
                        if i == 5:
                            tail_q(u - 1)

            pe.wait_ge(sc_ok, 4 * NQ)
            pe.wait_ge(v_ok, NQ)
            self_unit(0, True)
            with pe.Fori(1, NQ) as u:
                self_unit(u, False)
            pv(NQ - 1, S_PAIRS - 1)
            tail_den(NQ - 1)
            tail_wo(NQ - 1)
            tail_turn(NQ - 1)
            tail_q(NQ - 1)

            def c_scores(u, g, qc, t):
                n = P if t < MT - 1 else MLAST
                for hf in range(2):
                    i = 2 * t + hf
                    first = isinstance(u, int) and u == 0
                    if i >= 3:
                        pe.wait_ge(c_exp, 2 * MT * u + i - 2)
                    elif not first:
                        pe.wait_ge(c_exp, 2 * MT * u - (2 * MT - 1 - [24, 25, 23][i]))
                    for h in range(2):
                        hh = 2 * hf + h
                        mm = pe.matmul(bank(2 * (i % 3) + h, QC, n), kst[g % 2][:, hh, t * P:t * P + n], qst[g % 2][:, hh, ds(qc * QC, QC)],
                                       start=True, stop=True)
                    mm.then_inc(c_mm, 1)

            def c_values(u, g, t):
                n = P if t < MT - 1 else MLAST
                pe.wait_ge(c_exp, 2 * MT * u + 2 * t + 2)
                if t == 0 and not (isinstance(u, int) and u == 0):
                    pe.wait_ge(c_evac, u)
                for h in range(G):
                    hh = g * G + h
                    mm = pe.matmul(psum[32 * h:32 * h + VW, 6, :], vx[0:n, t, hh * VW:(hh + 1) * VW],
                                   pbuf[0:n, (2 * t + h // 2) % 4, (h % 2) * QC:(h % 2) * QC + QC], start=(t == 0), stop=(t == MT - 1),
                                   tile_position=(0, 32 * h))
                mm.then_inc(c_pv, 1)

            def c_turn(u):
                pe.wait_ge(c_evac, u + 1)
                if not (isinstance(u, int) and u == 0):
                    pe.wait_ge(c_xo, u)
                for t in range(TPC):
                    mm = pe.transpose(psum[:, 7, t * P:t * P + P], oT[:, t * P:t * P + P], ident[:, :])
                mm.then_inc(c_tr, 1)

            def cross_unit(u, g, qc, first):
                for t in range(MT):
                    c_scores(u, g, qc, t)
                    if t:
                        c_values(u, g, t - 1)
                    elif not first:
                        c_values(u - 1, g if not isinstance(qc, int) else g - 1, MT - 1)
                    if t == 2 and not first:
                        c_turn(u - 1)

            for g in range(NG):
                if g == 0:
                    pe.wait_ge(st_rows, 4)
                    pe.wait_ge(q_ok, 2 * NQ)
                    pe.wait_ge(o_clear, 1)
                pe.wait_ge(st_ld[g], 12 * 16)
                cross_unit(NQ * g, g, 0, g == 0)
                with pe.Fori(1, NQ) as qc:
                    cross_unit(qc + NQ * g, g, qc, False)
            c_values(NQ * NG - 1, NG - 1, MT - 1)
            c_turn(NQ * NG - 1)

            pe.wait_ge(bad_ok, 1)
            pe.matmul(psum[:, 7, 0:1], ones[:, :], small[:, 0:1], start=True, stop=True).then_inc(bad_mm, 1)
            pe.wait_ge(flag_ok, 1)
            with pe.If(pe.value_load(again[0:1, 0:1], min_val=0, max_val=P) > 0):
                with pe.Fori(0, NH) as h:
                    with pe.Fori(0, NT) as t:
                        i = h * NT + t
                        pe.wait_ge(m_ld, 12 * 16 * (h + 1))
                        pe.wait_ge(m_out, i + 1)
                        for c, (m0, mn) in enumerate(KCH):
                            mm = pe.matmul(bank(c, 401), gq[:, ds(t * P, P)], gk[:, m0:m0 + 401], start=True, stop=True)
                        mm.then_inc(m_mm, 1)
                        pe.wait_ge(m_exp, 2 * i + 2)
                        for k in range(MT):
                            n = P if k < MT - 1 else MLAST
                            mm = pe.transpose(psum[0:n, 4 + k // 4, (k % 4) * P:(k % 4) * P + P], gp[:, k * P:k * P + n], ident[:, :])
                        mm.then_inc(m_tr, 1)
                        pe.wait_ge(m_pT, 2 * i + 2)
                        for k in range(MT):
                            n = P if k < MT - 1 else MLAST
                            mm = pe.matmul(psum[:, 0, 0:VW], gpT[0:n, k, :], vx[0:n, k, ds(h * VW, VW)], start=(k == 0), stop=(k == MT - 1))
                        mm.then_inc(m_pv, 1)
                pe.wait_ge(m_out, NT * NH + 1)

            def f_turn(q):
                if q == 0:
                    pe.wait_ge(c_exp, 2 * MT * NQ * NG)
                    pe.wait_ge(c_xo, NQ * NG)
                for k in range(KD):
                    if q >= 2:
                        pe.wait_ge(r_xT, 2 * (q - 2) + k + 1)
                    for t in range(TPC):
                        mm = pe.transpose(bank(k)[:, t * P:t * P + P], xo[:, q * TPC + t, k * P:k * P + P], ident[:, :])
                    mm.then_inc(f_tr, 1)

            def f_up(q):
                pe.wait_ge(f_xT, 2 * q + 2)
                for f in range(NF1):
                    i = NF1 * q + f
                    if i >= 3:
                        pe.wait_ge(f_relu, i - 2)
                    for k in range(KD):
                        mm = pe.matmul(bank(2 + i % 3), w1_x[:, k, f * P:f * P + P], xT[q % 2][:, k, :], start=(k == 0), stop=(k == KD - 1))
                    mm.then_inc(f_h, 1)

            def f_down(q):
                pe.wait_ge(f_relu, NF1 * (q + 1))
                if q:
                    pe.wait_ge(f_res, q)
                for t in range(TPC):
                    for f in range(NF1):
                        mm = pe.matmul(psum[:, 6 + t // 2, (t % 2) * D:(t % 2) * D + D], h_x[:, f, t * P:t * P + P], w2_x[:, f, :],
                                       start=(f == 0), stop=(f == NF1 - 1))
                mm.then_inc(f_y, 1)

            def f_router(q):
                pe.wait_ge(xn3_ok, q + 1)
                for k in range(KD):
                    for t in range(TPC):
                        mm = pe.transpose(bank(k)[:, t * P:t * P + P], xn[:, q * TPC + t, k * P:k * P + P], ident[:, :])
                    mm.then_inc(r_tr, 1)
                pe.wait_ge(r_xT, 2 * q + 2)
                for t in range(TPC):
                    for k in range(KD):
                        mm = pe.matmul(psum[:, 5, (q * TPC + t) * E:(q * TPC + t + 1) * E], xn3T[:, k, t * P:t * P + P], wr[:, k, :],
                                       start=(k == 0), stop=(k == KD - 1))
                    mm.then_inc(r_lg, 1)

            for q in range(NQ):
                f_turn(q)
                f_up(q)
                if q:
                    f_router(q - 1)
                f_down(q)
            f_router(NQ - 1)

            pe.wait_ge(r_one, 1)
            pe.matmul(psum[:, 6, 0:P], tri[:, :], oneh.rearrange("p t e -> p (t e)"), start=True, stop=True)
            pe.matmul(psum[:, 7, 0:P], ones[:, :], oneh.rearrange("p t e -> p (t e)"), start=True, stop=True).then_inc(r_rank, 1)

            def expert(b):
                return pe.value_load(bl_e[0:1, ds(b, 1)], min_val=0, max_val=E - 1)

            def g_turn(b, j, half):
                pe.wait_ge(g_ld[j], 16 * (half + 1))
                if not (isinstance(b, int) and b == 0):
                    pe.wait_ge(g_xT, b)
                for k in range(KD):
                    mm = pe.transpose(psum[:, 6, k * P:k * P + P], xg[j][:, k * P:k * P + P], ident[:, :])
                mm.then_inc(g_tr, 1)

            def g_up(b, j):
                e = expert(b)
                pe.wait_ge(g_xT, b + 1)
                if not (isinstance(b, int) and b < 2):
                    pe.wait_ge(g_act, b - 1)
                for n in range(2):
                    pe.matmul(bank(2 * j + n), ones_b[:, :], b1p[:, ds(e * F + n * 512, 512)], start=True, stop=False)
                    for k in range(KD):
                        mm = pe.matmul(bank(2 * j + n), xgT[j][:, k, :], w1v[:, k, ds(e * F + n * 512, 512)], start=False, stop=(k == KD - 1))
                mm.then_inc(g_h, 1)

            def g_hidden(b, j):
                pe.wait_ge(g_act, b + 1)
                if not (isinstance(b, int) and b == 0):
                    pe.wait_ge(g_hTa, b)
                    pe.wait_ge(g_hTd, b)
                for f in range(NF):
                    mm = pe.transpose(psum[:, 4 + f // 4, (f % 4) * P:(f % 4) * P + P], hs[j][:, f * P:f * P + P], ident[:, :])
                mm.then_inc(g_ht, 1)

            def g_down(b, j):
                e = expert(b)
                pe.wait_ge(g_hTa, b + 1)
                pe.wait_ge(g_hTd, b + 1)
                if not (isinstance(b, int) and b == 0):
                    pe.wait_ge(g_ys, b)
                for f in range(NF):
                    mm = pe.matmul(psum[:, 7, 0:D], hT[j][:, f, :], arena[:, ds(e * (NF * D) + f * D, D)], start=(f == 0), stop=(f == NF - 1))
                mm.then_inc(g_y, 1)

            pe.wait_ge(r_blk, 1)
            pe.wait_ge(ld_w1e, 32)
            pe.wait_ge(ld_b1e, 16)
            pe.wait_ge(ld_w2e, 16 * E)
            g_turn(0, 0, 0)
            g_turn(1, 1, 0)
            g_up(0, 0)
            with pe.Fori(0, (NB - 3) // 2) as i:
                for j in range(2):
                    b = 2 * i + j
                    g_hidden(b, j)
                    g_up(b + 1, 1 - j)
                    g_turn(b + 2, j, i + 1)
                    g_down(b, j)
            for b in range(NB - 3, NB):
                g_hidden(b, b % 2)
                if b + 1 < NB:
                    g_up(b + 1, (b + 1) % 2)
                if b + 2 < NB:
                    g_turn(b + 2, b % 2, (b + 2) // 2)
                g_down(b, b % 2)

        @block.scalar
        def _(act):
            act.dma_start(cols[:, :], a["cols"]).then_inc(ld_small, 16)
            act.dma_start(rows[:, :], a["rows"].partition_broadcast(P)).then_inc(ld_small, 16)
            act.dma_start(bo_b, a["bo"].partition_broadcast(P)).then_inc(ld_small, 16)
            act.dma_start(bv_b, a["bv"].partition_broadcast(P)).then_inc(ld_small, 16)
            act.dma_start(b1f[:, :], a["b1"].rearrange("(p n) -> p n", p=P)).then_inc(ld_small, 16)
            xv = a["x"].rearrange("b (t p) n -> p (b t) n", p=P)
            for q in range(NQ):
                act.dma_start(res[:, q * TPC:(q + 1) * TPC, :], xv[:, q * TPC:(q + 1) * TPC, :]).then_inc(ld_x[q], 16)
            act.wait_ge(ld_small, 80)
            for j, (m0, mn) in enumerate(KCH):
                for c in range(KD):
                    i = 2 * j + c
                    act.wait_ge(k_proj, i + 1)
                    act.activation(kf[:, c, m0:m0 + mn], psum[:, i % 4, 0:mn], ACT.Identity, bias=cols[:, XBK + c:XBK + c + 1],
                                   accum_out=ksum[:, c, j:j + 1]).then_inc(k_evac, 1)
            act.wait_ge(col_ok, 1)
            act.wait_ge(consts, 7)
            for q in range(NQ):
                for k in range(KD):
                    act.wait_ge(xn_T, 2 * q + k + 1)
                    if q >= 2:
                        act.wait_ge(qkv_mm, 3 * (q - 1))
                    act.copy(xT[q % 2][:, k, :], psum[:, 6 + k, :]).then_inc(xT_ok, 1)
                b0 = 0 if q % 2 == 0 else 3
                for w in range(2):
                    act.wait_ge(qkv_mm, 3 * q + w + 1)
                    if q:
                        act.wait_ge(act_own, 2 * (q - 1) + w + 1)
                        act.wait_ge(sc_ok, 4 * (q - 1) + 2 * w + 2)
                    act.activation(th[:, w], psum[:, b0 + w, :], ACT.Identity, bias=bqk[:, w:w + 1], scale=inv_w[:, 0:1]).then_inc(th_ok, 1)
                for w in range(2):
                    act.wait_ge(ang_ok, 2 * q + w + 1)
                    act.activation(sc[w][:, 1, q * QC:q * QC + QC], th[:, w], ACT.Sin).then_inc(sc_ok, 1)
                    act.activation(tn[:, w], th[:, w], ACT.Abs).then_inc(act_own, 1)
                    act.wait_ge(act_own, 2 * q + w + 1)
                    act.activation(sc[w][:, 0, q * QC:q * QC + QC], tn[:, w], ACT.Sin, bias=half_pi[:, 0:1], scale=-1.0).then_inc(sc_ok, 1)

            def exp_self(u, i):
                n = S_PAIRS * u + i
                act.wait_ge(s_mm, n + 1)
                first = isinstance(u, int) and u == 0
                if i >= 4:
                    act.wait_ge(s_pv, n - 3)
                    act.wait_ge(s_acc, (S_PAIRS - 1) * u + max(i - 4, 1))
                elif not first:
                    act.wait_ge(s_pv, n - 3)
                    act.wait_ge(s_acc, (S_PAIRS - 1) * (u - 1) + i + 4)
                act.activation(pbuf[:, i % 4, :], psum[:, 2 * (i % 2):2 * (i % 2) + 2, :].rearrange("p b n -> p (b n)"),
                               ACT.Exp, scale=1.0 / math.sqrt(HD)).then_inc(s_exp, 1)

            def tail_xT(u):
                for k in range(KD):
                    act.wait_ge(xn2_T, 2 * u + k + 1)
                    act.copy(xT[0][:, k, :], psum[:, 6 + k, :]).then_inc(x2T_ok, 1)

            def tail_q(u):
                for c in range(KD):
                    if isinstance(u, int) or c == 0:
                        act.wait_ge(zeroed, 16 * NB)
                    act.wait_ge(q_mm, 2 * u + c + 1)
                    if c == 0 and not (isinstance(u, int) and u == 0):
                        act.wait_ge(q_split, u)
                    act.activation(qf[:, c], psum[:, 5 + c, :], ACT.Identity, bias=cols[:, XBQ + c:XBQ + c + 1]).then_inc(q_ok, 1)

            for i in range(S_PAIRS):
                exp_self(0, i)
            with act.Fori(1, NQ) as u:
                for i in range(S_PAIRS):
                    exp_self(u, i)
                    if i == 4:
                        tail_xT(u - 1)
                    if i == 5:
                        tail_q(u - 1)
            tail_xT(NQ - 1)
            tail_q(NQ - 1)

            def exp_cross(u):
                for i in range(2 * MT):
                    t = i // 2
                    n = P if t < MT - 1 else MLAST
                    act.wait_ge(c_mm, 2 * MT * u + i + 1)
                    if t >= 2:
                        act.wait_ge(c_pv, MT * u + t - 1)
                    elif not isinstance(u, int):
                        act.wait_ge(c_pv, MT * u - t)
                    act.activation(pbuf[0:n, i % 4, :], psum[0:n, 2 * (i % 3):2 * (i % 3) + 2, :].rearrange("p b n -> p (b n)"),
                                   ACT.Exp, scale=1.0 / math.sqrt(DH)).then_inc(c_exp, 1)

            exp_cross(0)
            with act.Fori(1, NQ * NG) as u:
                exp_cross(u)

            act.wait_ge(flag_ok, 1)
            with act.If(act.value_load(again[0:1, 0:1], min_val=0, max_val=P) > 0):
                with act.Fori(0, NT * NH) as i:
                    act.wait_ge(m_max, i + 1)
                    sc_m = 1.0 / math.sqrt(DH)
                    act.activation(gp[:, 0:1600].rearrange("p (c n) -> p c n", c=4), psum[:, 0:4, 0:400], ACT.Exp,
                                   bias=small[:, 1:2], scale=sc_m).then_inc(m_exp, 1)
                    act.activation(gp[:, 1600:M], psum[:, 3, 400:401], ACT.Exp, bias=small[:, 1:2], scale=sc_m).then_inc(m_exp, 1)
                    act.wait_ge(m_tr, i + 1)
                    act.copy(gpT[:, 0:MT - 1, :], psum[:, 4:7, :].rearrange("p b (k n) -> p (b k) n", n=P)).then_inc(m_pT, 1)
                    act.copy(gpT[0:MLAST, MT - 1, :], psum[0:MLAST, 7, 0:P]).then_inc(m_pT, 1)

            def xn3_turned(q):
                for k in range(KD):
                    act.wait_ge(r_tr, 2 * q + k + 1)
                    if q:
                        act.wait_ge(r_lg, NT // NQ * q)
                    act.copy(xn3T[:, k, :], psum[:, k, :]).then_inc(r_xT, 1)

            for q in range(NQ):
                for f in range(NF1):
                    i = NF1 * q + f
                    act.wait_ge(f_h, i + 1)
                    if q:
                        act.wait_ge(f_y, q)
                    act.activation(h_x[:, f, :], psum[:, 2 + i % 3, :], ACT.Relu, bias=cols[:, XB1 + f:XB1 + f + 1]).then_inc(f_relu, 1)
                if q:
                    xn3_turned(q - 1)
            xn3_turned(NQ - 1)

            act.wait_ge(r_sub, 1)
            act.activation(rank[:, :, :], l2[:, :, :], ACT.Exp).then_inc(r_exp, 1)

            act.wait_ge(dispatched, 16 * NT)

            def rows_turned(b, j):
                act.wait_ge(g_tr, b + 1)
                if not (isinstance(b, int) and b < 2):
                    act.wait_ge(g_h, b - 1)
                act.copy(xgT[j], psum[:, 6, 0:KD * P].rearrange("p (k n) -> p k n", k=KD)).then_inc(g_xT, 1)

            def gelu(b, j):
                act.wait_ge(g_h, b + 1)
                if not (isinstance(b, int) and b < 2):
                    act.wait_ge(g_ht, b - 1)
                act.activation(hs[j], psum[:, 2 * j:2 * j + 2, :].rearrange("p b n -> p (b n)"), ACT.Gelu).then_inc(g_act, 1)

            def hidden_turned(b, j):
                act.wait_ge(g_ht, b + 1)
                if not (isinstance(b, int) and b < 2):
                    act.wait_ge(g_y, b - 1)
                act.copy(hT[j][:, 0:4, :], psum[:, 4, :].rearrange("p (f n) -> p f n", f=4)).then_inc(g_hTa, 1)

            rows_turned(0, 0)
            rows_turned(1, 1)
            gelu(0, 0)
            hidden_turned(0, 0)
            rows_turned(2, 0)
            gelu(1, 1)
            hidden_turned(1, 1)
            rows_turned(3, 1)
            gelu(2, 0)
            with act.Fori(1, (NB - 3) // 2) as i:
                for j in range(2):
                    b = 2 * i + j
                    hidden_turned(b, j)
                    rows_turned(b + 2, j)
                    gelu(b + 1, 1 - j)
            for b in range(NB - 3, NB):
                hidden_turned(b, b % 2)
                if b + 2 < NB:
                    rows_turned(b + 2, b % 2)
                if b + 1 < NB:
                    gelu(b + 1, (b + 1) % 2)

        @block.vector
        def _(dve):
            ch = Chain(dve, dve_own)

            def rsqrt_norm(src, dst, signal):
                ch.inc(dve.memset(nv[:, :], 0.0))
                for t in range(TPC):
                    ch.inc(dve.bn_stats(stats[:, t, :], src[:, t, :]))
                ch.wait()
                ch.inc(dve.memset(nt1[:, :], 0.0))
                for t in range(TPC):
                    ch.inc(dve.bn_aggr(mv[:, t, :], stats[:, t, :]))
                ch.wait()
                ch.link(dve.tensor_scalar(nv[:, :], mv[:, :, 1], EPS, None, ALU.add))
                ch.link(dve.tensor_scalar(rstd[:, :].bitcast(I32), nv[:, :].bitcast(I32), -0.5, float(0x5F3759DF), ALU.mult, ALU.add))
                for _ in range(4):
                    ch.link(dve.tensor_tensor(nt1[:, :], rstd[:, :], rstd[:, :], ALU.mult))
                    ch.link(dve.tensor_tensor(nt1[:, :], nt1[:, :], nv[:, :], ALU.mult))
                    ch.link(dve.tensor_scalar(nt1[:, :], nt1[:, :], -0.5, 1.5, ALU.mult, ALU.add))
                    ch.link(dve.tensor_tensor(rstd[:, :], rstd[:, :], nt1[:, :], ALU.mult))
                for t in range(TPC):
                    ins = dve.tensor_scalar(dst[:, t, :], src[:, t, :], mv[:, t, 0:1], rstd[:, t:t + 1], ALU.subtract, ALU.mult)
                    if t < TPC - 1:
                        ch.inc(ins)
                ins.then_inc(signal, 1)

            vxh = vx.rearrange("p t (h w) -> p t h w", w=VW)
            ch.inc(dve.memset(vbuf[:, :], 1.0))
            ch.wait()
            dve.wait_ge(ld_small, 80)
            ch.link(dve.tensor_scalar(inv_w[:, 1:2], cols[:, WL:WL + 1], 1e-8, None, ALU.add))
            ch.link(dve.reciprocal(inv_w[:, 0:1], inv_w[:, 1:2]))
            dve.tensor_scalar(bqk[:, 0:1], cols[:, BQ:BQ + 1], inv_w[:, 0:1], cols[:, PH:PH + 1], ALU.mult, ALU.add).then_inc(col_ok, 1)
            dve.tensor_scalar(bqk[:, 1:2], cols[:, BK:BK + 1], inv_w[:, 0:1], cols[:, PH:PH + 1], ALU.mult, ALU.add).then_inc(col_ok, 1)
            for t in range(MT):
                n = P if t < MT - 1 else MLAST
                dve.wait_ge(v_proj, t + 1)
                dve.tensor_tensor(vxh[0:n, t, :, 0:DH], psum[0:n, 4 + t % 2, 0:D].rearrange("p (h d) -> p h d", d=DH),
                                  bv_b[0:n].rearrange("p (h d) -> p h d", d=DH), ALU.add).then_inc(v_evac, 1)

            def norm1(q):
                dve.wait_ge(ld_x[q], 16)
                rsqrt_norm(res[:, q * TPC:(q + 1) * TPC, :], xn[:, q * TPC:(q + 1) * TPC, :], xn_ok)

            def angles(q):
                for w in range(2):
                    dve.wait_ge(th_ok, 2 * q + w + 1)
                    ch.link(dve.tensor_scalar(turns, th[:, w], 1.0 / TWO_PI, MAGIC, ALU.mult, ALU.add))
                    ch.link(dve.tensor_scalar(turns, turns, MAGIC, None, ALU.subtract))
                    ch.link(dve.scalar_tensor_tensor(out=th[:, w], in0=turns, scalar=-C1, in1=th[:, w], op0=ALU.mult, op1=ALU.add))
                    ch.link(dve.scalar_tensor_tensor(out=th[:, w], in0=turns, scalar=-C2, in1=th[:, w], op0=ALU.mult, op1=ALU.add))
                    dve.tensor_scalar(th[:, w], th[:, w], PI_IN, -PI_IN, ALU.min, ALU.max).then_inc(ang_ok, 1)

            turns = arena[:, 13312:13824]
            norm1(0)
            norm1(1)
            for q in range(NQ):
                angles(q)
                b0 = 0 if q % 2 == 0 else 3
                dve.wait_ge(qkv_mm, 3 * q + 3)
                dve.tensor_copy(v_s[:, q * TPC:(q + 1) * TPC, :], psum[:, b0 + 2, :].rearrange("p (t n) -> p t n", n=P)).then_inc(v_ok, 1)
                if q + 2 < NQ:
                    norm1(q + 2)

            dve.wait_ge(sc_ok, 4 * NQ)
            dve.wait_ge(bo_added, NQ)

            def accumulate(u, i):
                dve.wait_ge(s_exp, S_PAIRS * u + i + 1)
                if i == 1:
                    dve.tensor_tensor(acc, pbuf[:, 0, :], pbuf[:, 1, :], ALU.add).then_inc(s_acc, 1)
                else:
                    dve.wait_ge(s_acc, (S_PAIRS - 1) * u + i - 1)
                    dve.tensor_tensor(acc, acc, pbuf[:, i % 4, :], ALU.add).then_inc(s_acc, 1)

            def total(u):
                dve.wait_ge(s_acc, (S_PAIRS - 1) * (u + 1))
                dve.tensor_tensor(acc1, acc[:, 0:QC], acc[:, QC:2 * QC], ALU.add).then_inc(acc_ok, 1)
                dve.wait_ge(acc_ok, u + 1)

            def tail_out(u):
                dve.wait_ge(s_pv, S_PAIRS * (u + 1))
                dve.tensor_copy(o_raw, psum[:, 4, :]).then_inc(o_evac, 1)

            def tail_norm(u):
                dve.wait_ge(den_mm, u + 1)
                ch.inc(dve.reciprocal(rden, psum[:, 5, :]))
                ch.wait()
                dve.wait_ge(o_evac, u + 1)
                ch.link(dve.tensor_tensor(aT, o_raw, rden, ALU.mult))
                dve.tensor_scalar(aT, aT, cols[:, BV:BV + 1], None, ALU.add).then_inc(aT_ok, 1)

            def tail_res(u):
                dve.wait_ge(wo_mm, u + 1)
                r = res[:, ds(u * TPC, TPC), :]
                ch.link(dve.tensor_tensor(r.rearrange("p t n -> p (t n)"), r.rearrange("p t n -> p (t n)"),
                                          psum[:, 6:8, :].rearrange("p b n -> p (b n)"), ALU.add))
                rsqrt_norm(r, xn2, xn2_ok)

            for i in range(1, S_PAIRS):
                accumulate(0, i)
            total(0)
            with dve.Fori(0, NQ - 1) as v:
                ch.enter(v, TAIL_LINKS)
                tail_out(v)
                for i in range(1, S_PAIRS):
                    accumulate(v + 1, i)
                    if i == 1:
                        tail_norm(v)
                    if i == 3:
                        tail_res(v)
                total(v + 1)
                ch.leave(NQ - 1)
            tail_out(NQ - 1)
            tail_norm(NQ - 1)
            tail_res(NQ - 1)

            dve.wait_ge(q_ok, 2 * NQ)
            dve.memset(psum[:, 6, :], 0.0).then_inc(o_clear, 1)
            ch.link(dve.memset(rmin[:, :, :], 1.0))
            for g in range(NG):
                with dve.Fori(0, NQ) as qc:
                    ch.enter(qc, 2)
                    u = qc + NQ * g
                    dve.wait_ge(c_pv, MT * u + MT)
                    dve.tensor_copy(oT, psum[:, 6, :]).then_inc(c_evac, 1)
                    dve.wait_ge(c_tr, u + 1)
                    o_v = psum[:, 7, :].rearrange("p (t h w) -> p t h w", t=TPC, h=G)
                    ch.link(dve.reciprocal(rden_x[:, :, :], o_v[:, :, :, DH]))
                    ch.inc(dve.tensor_tensor(rmin[:, :, :], rmin[:, :, :], rden_x[:, :, :], ALU.min))
                    dve.tensor_tensor(xo[:, ds(qc * TPC, TPC), g * G * DH:(g + 1) * G * DH].rearrange("p t (h d) -> p t h d", d=DH),
                                      o_v[:, :, :, 0:DH], rden_x[:, :, :].unsqueeze(3).to_broadcast([P, TPC, G, DH]), ALU.mult).then_inc(c_xo, 1)
                    ch.leave(NQ)

            ch.wait()
            dve.wait_ge(c_xo, NQ * NG)
            ch.link(dve.tensor_reduce(small[:, 1:2], rmin[:, :, :], AX.XY, ALU.min))
            dve.tensor_scalar(small[:, 0:1], small[:, 1:2], LEAST_RECIPROCAL, None, ALU.is_lt).then_inc(bad_ok, 1)
            dve.wait_ge(bad_mm, 1)
            dve.tensor_copy(again[:, :], psum[:, 7, 0:1]).then_inc(flag_ok, 1)
            dve.wait_ge(flag_ok, 1)
            with dve.If(dve.value_load(again[0:1, 0:1], min_val=0, max_val=P) > 0):
                dve.memset(small[:, 0:1], 0.0).then_inc(m_out, 1)
                with dve.Fori(0, NH) as h:
                    with dve.Fori(0, NT) as t:
                        i = h * NT + t
                        dve.wait_ge(m_out, i + 1)
                        dve.wait_ge(m_mm, i + 1)
                        dve.tensor_reduce(small[:, 0:1], psum[:, 0:4, 0:401], AX.XY, ALU.max).then_inc(m_red, 1)
                        dve.wait_ge(m_red, 2 * i + 1)
                        dve.tensor_scalar(small[:, 1:2], small[:, 0:1], -1.0 / math.sqrt(DH), None, ALU.mult).then_inc(m_max, 1)
                        dve.wait_ge(m_pv, i + 1)
                        dve.reciprocal(rden_x[:, 0, 0:1], psum[:, 0, DH:VW]).then_inc(m_red, 1)
                        dve.wait_ge(m_red, 2 * i + 2)
                        dve.tensor_scalar(duo[:, ds(t * D + h * DH, DH)], psum[:, 0, 0:DH], rden_x[:, 0, 0:1], None, ALU.mult).then_inc(m_out, 1)

            dve.wait_ge(b2_added, 1)

            def turned(q):
                for k in range(KD):
                    dve.wait_ge(f_tr, 2 * q + k + 1)
                    if q == 0:
                        dve.wait_ge(q_mm, 2 * NQ)
                    dve.tensor_copy(xT[q % 2][:, k, :], psum[:, k, :]).then_inc(f_xT, 1)

            turned(0)
            for q in range(NQ):
                if q + 1 < NQ:
                    pass
                dve.wait_ge(f_y, q + 1)
                r = res[:, q * TPC:(q + 1) * TPC, :]
                dve.tensor_tensor(r.rearrange("p t n -> p (t n)"), r.rearrange("p t n -> p (t n)"),
                                  psum[:, 6:8, :].rearrange("p b n -> p (b n)"), ALU.add).then_inc(f_res, 1)
                if q + 1 < NQ:
                    turned(q + 1)
                dve.wait_ge(f_res, q + 1)
                rsqrt_norm(r, xn[:, q * TPC:(q + 1) * TPC, :], xn3_ok)

            dve.wait_ge(r_lg, NT)
            ch.link(dve.tensor_tensor(lg[:, :, :], psum[:, 5, 0:P].rearrange("p (t e) -> p t e", e=E), br_b.unsqueeze(1).to_broadcast([P, NT, E]), ALU.add))
            ch.link(dve.tensor_reduce(lmax[:, :], lg[:, :, :], AX.X, ALU.max))
            lmax_b = lmax[:, :].unsqueeze(2).to_broadcast([P, NT, E])
            dve.tensor_tensor(l2[:, :, :], lg[:, :, :], lmax_b, ALU.subtract).then_inc(r_sub, 1)
            ch.link(dve.tensor_tensor(oneh[:, :, :], lg[:, :, :], lmax_b, ALU.is_equal))
            dve.wait_ge(consts, 7)
            revi_b = revi[:, :].unsqueeze(1).to_broadcast([P, NT, E])
            ch.link(dve.tensor_tensor(oneh[:, :, :], oneh[:, :, :], revi_b, ALU.mult))
            ch.link(dve.tensor_reduce(top[:, :], oneh[:, :, :], AX.X, ALU.max))
            dve.tensor_tensor(oneh[:, :, :], revi_b, top[:, :].unsqueeze(2).to_broadcast([P, NT, E]), ALU.is_equal).then_inc(r_one, 1)
            dve.wait_ge(r_exp, 1)
            ch.link(dve.tensor_reduce(gate[:, :], rank[:, :, :], AX.X, ALU.add))
            ch.inc(dve.reciprocal(gate[:, :], gate[:, :]))
            dve.wait_ge(r_rank, 1)
            psb = lambda b: psum[:, b, 0:P].rearrange("p (t e) -> p t e", e=E)
            ch.inc(dve.tensor_copy(tot[:, :, :], psb(7)))
            ch.link(dve.tensor_copy(incl[0][:, :, :], psb(7)))
            cur = 0
            for s_ in (1, 2, 4, 8):
                ch.inc(dve.tensor_copy(incl[1 - cur][:, 0:s_, :], incl[cur][:, 0:s_, :]))
                ch.link(dve.tensor_tensor(incl[1 - cur][:, s_:, :], incl[cur][:, s_:, :], incl[cur][:, 0:NT - s_, :], ALU.add))
                cur = 1 - cur
            ch.link(dve.tensor_scalar(nb[:, :], incl[cur][:, NT - 1, :], 1.0 / P, (P - 1.0) / P - (P - 1.0) / (2 * P), ALU.mult, ALU.add))
            ch.link(dve.tensor_scalar(nb[:, :], nb[:, :], MAGIC, None, ALU.add))
            ch.link(dve.tensor_scalar(nb[:, :], nb[:, :], MAGIC, None, ALU.subtract))
            ch.link(dve.tensor_copy(cum[0][:, :], nb[:, :]))
            cc = 0
            for s_ in (1, 2, 4):
                ch.inc(dve.tensor_copy(cum[1 - cc][:, 0:s_], cum[cc][:, 0:s_]))
                ch.link(dve.tensor_tensor(cum[1 - cc][:, s_:], cum[cc][:, s_:], cum[cc][:, 0:E - s_], ALU.add))
                cc = 1 - cc
            ch.link(dve.tensor_tensor(nb[:, :], cum[cc][:, :], nb[:, :], ALU.subtract))
            ch.link(dve.tensor_tensor(tot[:, :, :], incl[cur][:, :, :], tot[:, :, :], ALU.subtract))
            ch.link(dve.tensor_tensor(tot[:, :, :], tot[:, :, :], psb(6), ALU.add))
            ch.link(dve.scalar_tensor_tensor(out=tot[:, :, :].rearrange("p t e -> p e t"), in0=nb[:, :].unsqueeze(2).to_broadcast([P, E, NT]),
                                             scalar=float(P), in1=tot[:, :, :].rearrange("p t e -> p e t"), op0=ALU.mult, op1=ALU.add))
            ch.link(dve.tensor_tensor(tot[:, :, :], tot[:, :, :], oneh[:, :, :], ALU.mult))
            ch.link(dve.tensor_reduce(slot_f[:, :], tot[:, :, :], AX.X, ALU.add))
            dve.tensor_copy(slot[:, :], slot_f[:, :]).then_inc(r_slot, 1)
            ch.link(dve.tensor_tensor(bl_c[:, :, :], bl_i[:, :].unsqueeze(2).to_broadcast([P, 24, E]), cum[cc][:, :].unsqueeze(1).to_broadcast([P, 24, E]), ALU.is_ge))
            ch.link(dve.tensor_reduce(bl_f[:, :], bl_c[:, :, 0:E - 1], AX.X, ALU.add))
            dve.tensor_copy(bl_e[:, :], bl_f[:, :]).then_inc(r_blk, 1)
            dve.wait_ge(r_blk, 1)

            def expert(b):
                return dve.value_load(bl_e[0:1, ds(b, 1)], min_val=0, max_val=E - 1)

            def hidden_turned(b, j):
                dve.wait_ge(g_ht, b + 1)
                dve.tensor_copy(hT[j][:, 4:8, :], psum[:, 5, :].rearrange("p (f n) -> p f n", f=4)).then_inc(g_hTd, 1)

            def result(b, j, half):
                e = expert(b)
                dve.wait_ge(g_y, b + 1)
                if not (isinstance(b, int) and b < 2):
                    dve.wait_ge(g_st[j], 16 * half)
                dve.tensor_tensor(ys[j], psum[:, 7, 0:D], b2e[:, ds(e * D, D)], ALU.add).then_inc(g_ys, 1)

            dve.wait_ge(dispatched, 16 * NT)
            dve.wait_ge(ld_b2e, 16)
            for b in range(2):
                hidden_turned(b, b % 2)
                result(b, b % 2, 0)
            with dve.Fori(1, (NB - 3) // 2) as i:
                for j in range(2):
                    b = 2 * i + j
                    hidden_turned(b, j)
                    result(b, j, i)
            for b in range(NB - 3, NB):
                hidden_turned(b, b % 2)
                result(b, b % 2, b // 2)
            for t in range(NT):
                dve.wait_ge(y_in[t], 16)
                dve.scalar_tensor_tensor(out=res[:, t, :], in0=yt[:, t, :], scalar=gate[:, t:t + 1], in1=res[:, t, :],
                                         op0=ALU.mult, op1=ALU.add).then_inc(o_ok, 1)


def kernel(**inputs):
    import numpy as np
    import concourse.bacc as bacc
    from concourse.bass_utils import run_bass_kernel_spmd

    v = {k: np.ascontiguousarray(x) for k, x in inputs.items()}
    c = lambda x, n: x.reshape(n, P).T
    arrays = {
        "x": v["x"],
        "yT": v["ctx_768"][0].T,
        "wqkv": np.stack([v["L0_attn_Wq"].T, v["L0_attn_Wk"].T, v["L0_attn_Wv"].T]),
        "wo": v["L0_attn_Wo"].T,
        "xwq": v["L0_xattn_Wq"], "xwk": v["L0_xattn_Wk"], "xwv": v["L0_xattn_Wv"], "xw1": v["L0_xattn_W1"], "xw2": v["L0_xattn_W2"],
        "wr": v["L0_ffn_Wr"], "w1": v["L0_ffn_W1"], "w2": v["L0_ffn_W2"],
        "b1": v["L0_ffn_b1"].reshape(-1), "b2": v["L0_ffn_b2"].reshape(-1),
        "cols": np.concatenate([c(v["L0_attn_bq"], 1), c(v["L0_attn_phase_bias"], 1), c(v["L0_attn_wavelengths"], 1), c(v["L0_attn_bk"], 1),
                                c(v["L0_attn_bv"], 1), c(v["L0_xattn_bq"], 2), c(v["L0_xattn_bk"], 2), c(v["L0_xattn_b1"], 4)], axis=1),
        "rows": np.concatenate([v["L0_xattn_b2"], v["L0_ffn_br"]]), "bo": v["L0_attn_bo"], "bv": v["L0_xattn_bv"],
    }
    nc = bacc.Bacc("TRN2", target_bir_lowering=False, num_devices=1)
    feeds, args = {}, {}
    for name, x in arrays.items():
        x = np.ascontiguousarray(x)
        feeds[f"in_{name}"] = x
        args[name] = nc.dram_tensor(f"in_{name}", x.shape, mybir.dt.from_np(x.dtype), kind="ExternalInput").ap()
    out = nc.dram_tensor("out_0", (1, T, D), F32, kind="ExternalOutput").ap()
    layer(nc, args, out)
    r = run_bass_kernel_spmd(nc, [feeds], core_ids=[0])
    return r.results[0]["out_0"]
```

```python
from contextlib import ExitStack
import math

import concourse.bass as bass
from concourse import mybir

F32 = mybir.dt.float32
BF16 = mybir.dt.bfloat16
F16 = mybir.dt.float16
I32 = mybir.dt.int32
U32 = mybir.dt.uint32
ALU = mybir.AluOpType
ACT = mybir.ActivationFunctionType
AX = mybir.AxisListType
ds = bass.ds

P = 128
T = 2048
D = 256
KD = D // P
NT = T // P
QC = 512
NQ = T // QC
TPC = QC // P
HD = 128
S_PAIRS = NT // 2
M = 1601
YD = 192
YC = YD // 2
NH = 16
DH = D // NH
G = 4
NG = NH // G
MT = -(-M // P)
MLAST = M - (MT - 1) * P
VW = DH + 1
F1 = 512
NF1 = F1 // P
E = 8
F = 1024
NF = F // P
NB = (T + E * (P - 1)) // P
NB_LOOP = 18
NB_TAIL = [[b] for b in range(NB_LOOP, NB)]
KCH = [(0, 400), (400, 400), (800, 400), (1200, 401)]
PARTS_Q = [0, 0, 0, 1, 1, 2]
PARTS_K = [0, 1, 2, 0, 1, 0]
RS = 6 * DH
EPS = 1e-5
TWO_PI = 2.0 * math.pi
C1 = 6.28125
C2 = TWO_PI - C1
MAGIC = 1.5 * 2.0 ** 23
PI_IN = 3.14159250


TAIL_LINKS = 34


LEAST_RECIPROCAL = 1e-30


class Chain:

    def __init__(self, eng, sem):
        self.eng, self.sem, self.base, self.n = eng, sem, 0, 0

    def inc(self, ins):
        self.n += 1
        ins.then_inc(self.sem, 1)

    def wait(self):
        self.eng.wait_ge(self.sem, self.base + self.n)

    def link(self, ins):
        self.inc(ins)
        self.wait()

    def enter(self, i, per):
        self.saved = (self.base + self.n, per)
        self.base, self.n = i * per + (self.base + self.n), 0

    def leave(self, count):
        start, per = self.saved
        assert self.n == per, (self.n, per)
        self.base, self.n = start + count * per, 0


def layer(nc, a, out):
    ctx = ExitStack()
    with ctx:
        def sb(name, shape, dt=F32):
            return ctx.enter_context(nc.sbuf_tensor(name, shape, dt))

        def sem(name):
            return ctx.enter_context(nc.semaphore(name))

        k_parts = nc.dram_tensor("k_parts", [3, D, M], BF16, kind="Internal").ap()
        q_parts = nc.dram_tensor("q_parts", [3, D, T], BF16, kind="Internal").ap()
        b1_parts = nc.dram_tensor("b1_parts", [3, E * F], BF16, kind="Internal").ap()
        x_rows = nc.dram_tensor("x_rows", [T, 2 * D], F32, kind="Internal").ap()
        out_rows = out.rearrange("b t n -> (b t) n")

        res = sb("res", [P, NT, D])
        w1e = sb("w1e", [P, KD * E * F])
        arena = sb("arena", [P, 16384])
        duo = sb("duo", [P, 4096 + 2048])
        pbuf = sb("pbuf", [P, 4, 1024])
        vbuf = sb("vbuf", [P, 3584])
        ident = sb("ident", [P, P])
        ones = sb("ones", [P, P])
        tri = sb("tri", [P, P])
        cols = sb("cols", [P, 13])
        rows = sb("rows", [P, 2 * D + E])
        b1_buf = sb("b1_buf", [P, 160])
        b1f = b1_buf[:, 0:E * F // P]
        b1s = b1_buf[:, 64:160].bitcast(BF16).rearrange("p (j n) -> p j n", j=3)
        lane = b1_buf[:, 0:P]
        ones_b = sb("ones_b", [3, P], BF16)
        w1_x = sb("w1_x", [P, KD, F1])
        wr = sb("wr", [P, KD, E])
        inv_w = sb("inv_w", [P, 2])
        bqk = sb("bqk", [P, 2])
        half_pi = sb("half_pi", [P, 1])
        ksum = sb("ksum", [P, KD, 4])
        kneg = sb("kneg", [P, KD])
        stats = sb("stats", [P, TPC, 6])
        mv = sb("mv", [P, TPC, 2])
        rstd = sb("rstd", [P, TPC])
        nt1 = sb("nt1", [P, TPC])
        nv = sb("nv", [P, TPC])
        rden_x = sb("rden_x", [P, TPC, G])
        rmin = sb("rmin", [P, TPC, G])
        small = sb("small", [P, 2])
        again = sb("again", [P, 1], I32)

        yT = w1e[0:YC, 0:2 * M].rearrange("p (c m) -> p c m", c=2)
        wk_x = w1e[0:YC, 3328:3840].rearrange("p (c n) -> p c n", c=2)
        wv_x = w1e[0:YC, 3840:4352].rearrange("p (c n) -> p c n", c=2)
        wqkv = w1e[:, 4352:5120].rearrange("p (w c n) -> p w c n", w=3, c=KD)
        bo_b = w1e[:, 9984:10240]
        wq_x = w1e[:, 15360:15872].rearrange("p (c n) -> p c n", c=KD)
        wo_s = w1e[:, 15872:16128]
        k_bf = w1e[:, 5120:5120 + 4864].bitcast(BF16)[:, 0:3 * KD * M].rearrange("p (j c m) -> p j c m", j=3, c=KD)
        xo = duo[:, 0:4096].rearrange("p (t n) -> p t n", t=NT)
        kf = duo[:, 0:KD * M].rearrange("p (c m) -> p c m", c=KD)
        b1p = duo[0:3, 0:4096].bitcast(BF16)
        xT = [duo[:, 4096 + 1024 * b:5120 + 1024 * b].rearrange("p (k t) -> p k t", k=KD) for b in range(2)]
        sc_hi = [arena[:, 4096 * w:4096 * w + 2048].bitcast(F16).rearrange("p (c t) -> p c t", c=2) for w in range(2)]
        sc_lo = [arena[:, 4096 * w + 2048:4096 * w + 4096].bitcast(BF16).rearrange("p (c t) -> p c t", c=2) for w in range(2)]
        v_s = arena[:, 8192:10240].rearrange("p (t n) -> p t n", t=NT)
        aT = arena[:, 10240:10752]
        o_raw = arena[:, 10752:11264]
        th, tn = ([arena[:, c:c + 1024].rearrange("p (w n) -> p w n", w=2) for c in places] for places in ((11264, 14336), (12288, 10240)))
        acc0 = w1e[:, 12420:13444]
        stats_late, mv_late = (w1e[:, c:c + 2 * TPC * n].rearrange("p (t n) -> p t n", n=n) for c, n in ((13508, 6), (13556, 2)))
        rstd_late, nt_late, nv_late = (w1e[:, c:c + 2 * TPC] for c in (13572, 13580, 13588))
        b1r = w1e[:, 13444:13444 + E * F // P]
        acc = arena[:, 11264:12288]
        acc1 = arena[:, 12288:12800]
        rden = arena[:, 12800:13312]
        turns = arena[:, 13312:13824]
        xn2 = arena[:, 13312:14336].rearrange("p (t n) -> p t n", t=TPC)
        qf = arena[:, 14336:15360].rearrange("p (c n) -> p c n", c=KD)
        w2_x = arena[:, 15360:16384].rearrange("p (f n) -> p f n", f=NF1)
        q_bf = w1e[:, 13824:13824 + 1536].bitcast(BF16).rearrange("p (j c n) -> p j c n", j=3, c=KD)

        def stack(base, width):
            return base[0:RS].bitcast(BF16).rearrange("p (h n) -> p h n", h=G)[:, :, 0:width]

        qst = [stack(w1e[:, 8324:12420], T), stack(arena[:, 4096:8192], T), stack(arena[:, 0:4096], T), stack(arena[:, 4096:8192], T)]
        kst = [stack(w1e[:, 5120:8322], M), stack(arena[:, 11396:14598], M), stack(arena[:, 8192:11394], M), stack(arena[:, 11396:14598], M)]
        gp = pbuf[:, :, :].rearrange("p a n -> p (a n)")[:, 0:M]
        gpT = pbuf[:, 2:4, :].rearrange("p a n -> p (a n)")[:, 0:MT * P].rearrange("p (t n) -> p t n", n=P)
        gq, gk = qst[2][:, 0, :], kst[2][:, 0, :]
        def p_slot(i):
            return pbuf[:, i % 4, :] if i < 2 * MT - 2 else duo[:, 4096 + 1024 * (i % 2):5120 + 1024 * (i % 2)]

        oT = arena[:, 14848:14848 + QC]
        w2e = arena[:, :].rearrange("p (e n) -> p e n", e=E)
        w1v = w1e[:, :].rearrange("p (k n) -> p k n", k=KD)
        xn1 = w1e[:, 5120:9216].rearrange("p (t n) -> p t n", n=D)
        xn = pbuf[:, :, :].rearrange("p a (t n) -> p (a t) n", n=D)
        hs = [pbuf[:, b, :] for b in range(2)]
        hT = [pbuf[:, 2 + b, :].rearrange("p (f n) -> p f n", f=NF) for b in range(2)]
        vx = vbuf[:, 0:MT * NH * VW].rearrange("p (t n) -> p t n", t=MT)
        h_x = vbuf[:, 0:NF1 * QC].rearrange("p (f n) -> p f n", f=NF1)
        xn3T = vbuf[:, 2048:3072].rearrange("p (k n) -> p k n", k=KD)
        xgT = [vbuf[:, 2560 + 256 * b:2816 + 256 * b].rearrange("p (k n) -> p k n", k=KD) for b in range(2)]
        flat = res[:, :, :].rearrange("p t n -> p (t n)")
        b2e = flat[:, 0:E * D]
        xg = [flat[:, 2048 + 512 * b:2560 + 512 * b] for b in range(2)]
        rs = [flat[:, 3072 + D * b:3072 + D * b + D] for b in range(2)]
        ys = [flat[:, 3584 + D * b:3584 + D * b + D] for b in range(2)]
        RV = 3072
        l2, oneh = [vbuf[:, RV + P * i:RV + P * i + P].rearrange("p (t e) -> p t e", e=E) for i in range(2)]
        base = vbuf[:, RV + 256:RV + 392].rearrange("p (t e) -> p t e", e=E)
        lg = vbuf[:, RV + 392:RV + 424].rearrange("p (t e) -> p t e", e=E)
        tok, bl_i = vbuf[:, RV + 424:RV + 440], vbuf[:, RV + 440:RV + 464]
        cum = [vbuf[:, RV + 464 + 12 * i:RV + 476 + 12 * i] for i in range(2)]
        nb, pad_row, lmax = vbuf[:, RV + 488:RV + 496], vbuf[:, RV + 496:RV + 497], vbuf[:, RV + 500:RV + 504]
        in_block = pbuf[:, 0:2, :].rearrange("p a (t n) -> p (a t) n", n=P)
        to_block = vbuf[:, 0:NT * 3 * 24].rearrange("p (t w b) -> p t w b", w=3, b=24)
        prod = vbuf[:, 1152:1152 + NT * E].rearrange("p (t e) -> p t e", e=E)
        bl_c = vbuf[:, 1280:1280 + 24 * E].rearrange("p (b e) -> p b e", e=E)
        probs = vbuf[:, 1472:1472 + NT * E].rearrange("p (t e) -> p t e", e=E)
        bl_f = vbuf[:, 1600:1624]
        revi = sb("revi", [P, E])
        gate = sb("gate", [P, NT])
        top = sb("top", [P, TPC])
        top_all = vbuf[:, 1624:1640]
        rank = sb("rank", [P, NT])
        full = sb("full", [P, NT])
        after = lambda i, n: duo[:, 4096 + 24 * i:4096 + 24 * i + n]
        token_in = after(0, 24).bitcast(U32)
        token_out = after(1, 24).bitcast(U32)
        slot_gate = after(2, 24)
        bl_e = after(3, 24).bitcast(I32)
        gate_b = after(4, 1)
        n_blocks = after(5, 1).bitcast(I32)[0:1, :]

        psum = ctx.enter_context(nc.psum_tensor("psum", [P, 8, 512], F32))

        ld_y = sem("ld_y"); ld_small = sem("ld_small"); ld_x = [sem(f"ld_x{q}") for q in range(NQ)]
        ld_ws = sem("ld_ws"); ld_wqkv = sem("ld_wqkv"); ld_w1e = sem("ld_w1e"); ld_w2e = sem("ld_w2e"); ld_b1e = sem("ld_b1e"); ld_b2e = sem("ld_b2e")
        consts = sem("consts"); late_consts = sem("late_consts")
        dve_own = sem("dve_own"); pool_own = sem("pool_own"); act_own = sem("act_own")
        k_proj = sem("k_proj"); k_evac = sem("k_evac"); k_split = sem("k_split"); k_stored = sem("k_stored")
        v_proj = sem("v_proj"); v_evac = sem("v_evac"); o_clear = sem("o_clear")
        col_ok = sem("col_ok"); xn_ok = sem("xn_ok"); norm_ok = sem("norm_ok"); xn_T = sem("xn_T"); xT_ok = sem("xT_ok")
        qkv_mm = sem("qkv_mm"); th_ok = sem("th_ok"); lo_ok = sem("lo_ok"); abs_ok = sem("abs_ok"); v_ok = sem("v_ok"); ones_ok = sem("ones_ok"); ang_ok = sem("ang_ok"); sc_ok = sem("sc_ok")
        bo_added = sem("bo_added")
        s_mm = sem("s_mm"); s_exp = sem("s_exp"); s_pv = sem("s_pv"); s_acc = sem("s_acc"); o_evac = sem("o_evac")
        acc_ok = sem("acc_ok"); den_mm = sem("den_mm"); aT_ok = sem("aT_ok"); wo_mm = sem("wo_mm"); res_ok = sem("res_ok")
        xn2_ok = sem("xn2_ok"); xn2_T = sem("xn2_T"); x2T_ok = sem("x2T_ok"); q_mm = sem("q_mm"); q_ok = sem("q_ok")
        q_split = sem("q_split"); q_stored = sem("q_stored")
        st_k0 = sem("st_k0"); st_q0 = sem("st_q0"); st_ld = [sem(f"st_ld{g}") for g in range(NG)]
        c_mm = sem("c_mm"); c_exp = sem("c_exp"); c_pv = sem("c_pv"); c_evac = sem("c_evac"); c_tr = sem("c_tr"); c_xo = sem("c_xo")
        bad_ok = sem("bad_ok"); bad_mm = sem("bad_mm"); flag_ok = sem("flag_ok")
        m_ld = sem("m_ld"); m_mm = sem("m_mm"); m_max = sem("m_max"); m_exp = sem("m_exp"); m_tr = sem("m_tr")
        m_pT = sem("m_pT"); m_pv = sem("m_pv"); m_out = sem("m_out"); m_red = sem("m_red")
        b2_added = sem("b2_added"); b1_stored = sem("b1_stored")
        f_tr = sem("f_tr"); f_xT = sem("f_xT"); f_h = sem("f_h"); f_relu = sem("f_relu"); f_y = sem("f_y"); f_res = sem("f_res")
        xn3_ok = sem("xn3_ok"); r_tr = sem("r_tr"); r_xT = sem("r_xT"); r_lg = sem("r_lg")
        r_sub = sem("r_sub"); r_exp = sem("r_exp"); r_one = sem("r_one"); r_rank = sem("r_rank"); r_used = sem("r_used"); r_blk = sem("r_blk")
        r_to = sem("r_to"); r_table = sem("r_table"); r_slots = sem("r_slots"); row_st = [sem(f"row_st{q}") for q in range(NQ)]
        g_ld = [sem(f"g_ld{b}") for b in range(2)]; g_tr = sem("g_tr"); g_xT = sem("g_xT"); g_h = sem("g_h")
        g_act = sem("g_act"); g_ht = sem("g_ht"); g_hTa = sem("g_hTa"); g_hTd = sem("g_hTd"); g_y = sem("g_y"); g_ys = sem("g_ys")
        g_st = [sem(f"g_st{b}") for b in range(2)]
        g_rs = sem("g_rs"); g_sum = sem("g_sum"); g_gate = sem("g_gate")

        block = ctx.enter_context(nc.Block())

        BQ, PH, WL, BV = 0, 1, 2, 4
        BK = 3
        XBQ, XBK, XB1 = 5, 7, 9
        b2_b, bv_b, br_b = rows[:, 0:D], rows[:, D:2 * D], rows[:, 2 * D:]

        def k_stack(eng, g, r):
            return eng.dma_start(kst[g][r * DH:(r + 1) * DH, :, :],
                                 k_parts[PARTS_K[r], g * G * DH:(g + 1) * G * DH, :].rearrange("(h d) m -> d h m", d=DH))

        @block.sync
        def _(sp):
            xv = a["x"].rearrange("b (t p) n -> p (b t) n", p=P)
            for q in range(NQ):
                sp.dma_start(res[:, q * TPC:(q + 1) * TPC, :], xv[:, q * TPC:(q + 1) * TPC, :]).then_inc(ld_x[q], 16)
                if q == 0:
                    sp.dma_start(wqkv, a["wqkv"].rearrange("w (c p) n -> p w c n", c=KD)).then_inc(ld_wqkv, 16)

            def q_stack(g, r, c0, cn, signal):
                sp.dma_start(qst[g][r * DH:(r + 1) * DH, :, c0:c0 + cn],
                             q_parts[PARTS_Q[r], g * G * DH:(g + 1) * G * DH, c0:c0 + cn].rearrange("(h d) t -> d h t", d=DH)
                             ).then_inc(signal, 16)

            for u in range(NQ):
                sp.wait_ge(q_split, u + 1)
                for j in range(3):
                    sp.dma_start(q_parts[j, :, u * QC:u * QC + QC].rearrange("(c p) t -> p c t", c=KD),
                                 q_bf[:, j]).then_inc(q_stored, 16)
                sp.wait_ge(q_stored, 48 * (u + 2))
                if u:
                    sp.wait_ge(st_q0, 96 * u)
                else:
                    sp.wait_ge(k_stored, 48)
                for r in range(6):
                    q_stack(0, r, u * QC, QC, st_q0)
            for g in range(1, NG):
                if g == 1:
                    sp.wait_ge(q_mm, 2 * NQ)
                    sp.wait_ge(q_split, NQ)
                if g == 3:
                    sp.wait_ge(c_mm, 2 * MT * NQ * 2)
                for r in range(6):
                    k_stack(sp, g, r).then_inc(st_ld[g], 16)
                    q_stack(g, r, 0, T, st_ld[g])
                if g == 2:
                    sp.wait_ge(c_mm, 2 * MT * NQ)
                    sp.wait_ge(v_proj, MT)
                    for k in range(KD):
                        sp.dma_start(w1v[:, k, :].rearrange("p (e f) -> p e f", e=E),
                                     a["w1"][:, k * P:k * P + P, :].rearrange("e p f -> p e f")).then_inc(ld_w1e, 16)
            sp.wait_ge(flag_ok, 1)
            with sp.If(sp.value_load(again[0:1, 0:1], min_val=0, max_val=P) > 0):
                with sp.Fori(0, NH) as h:
                    sp.wait_ge(m_out, NT * h + 1)
                    for r in range(6):
                        sp.dma_start(gk[r * DH:(r + 1) * DH, :], k_parts[PARTS_K[r], ds(h * DH, DH), :]).then_inc(m_ld, 16)
                        sp.dma_start(gq[r * DH:(r + 1) * DH, :], q_parts[PARTS_Q[r], ds(h * DH, DH), :]).then_inc(m_ld, 16)
                sp.wait_ge(m_pv, NT * NH)
            sp.wait_ge(c_mm, 2 * MT * NQ * NG)
            sp.wait_ge(c_tr, NQ * NG)

            def w2(e):
                sp.dma_start(w2e[:, e, :].rearrange("p (f n) -> p f n", f=NF),
                             a["w2"][e].rearrange("(f p) n -> p f n", f=NF)).then_inc(ld_w2e, 16)

            def tokens(q):
                rows_v = x_rows.rearrange("(t p) n -> p t n", p=P)
                tiles = slice(q * TPC, (q + 1) * TPC)
                sp.wait_ge(xn3_ok, q + 1)
                sp.dma_start(rows_v[:, tiles, 0:D], xn[:, tiles, :]).then_inc(row_st[q], 16)
                sp.dma_start(rows_v[:, tiles, D:2 * D], res[:, tiles, :]).then_inc(row_st[q], 16)

            for e in range(E - 1):
                w2(e)
            for q in range(NQ - 1):
                tokens(q)
            sp.wait_ge(f_tr, KD * NQ)
            sp.wait_ge(b1_stored, 48)
            sp.dma_start(b1p, b1_parts).then_inc(ld_b1e, 16)
            tokens(NQ - 1)
            sp.wait_ge(f_y, NQ)
            w2(E - 1)
            for q in range(NQ):
                sp.wait_ge(row_st[q], 32)
            sp.dma_start(b2e, a["b2"].partition_broadcast(P)).then_inc(ld_b2e, 16)
            sp.wait_ge(ld_b2e, 16)

        @block.gpsimd
        def _(pool):
            ch = Chain(pool, pool_own)
            pool.memset(half_pi[:, :], math.pi / 2).then_inc(consts, 1)
            pool.memset(ones[:, :], 1.0).then_inc(consts, 1)
            pool.memset(ones_b[:, :], 1.0).then_inc(consts, 1)
            ch.inc(pool.memset(ident[:, :], 0.0))
            ch.inc(pool.memset(tri[:, :], 1.0))
            ch.wait()
            pool.affine_select(out=ident[:, :], in_=ident[:, :], compare_op=ALU.not_equal, fill=1.0, base=0,
                               pattern=[[-1, P]], channel_multiplier=1).then_inc(consts, 1)
            pool.affine_select(out=tri[:, :], in_=tri[:, :], compare_op=ALU.is_gt, fill=0.0, base=0,
                               pattern=[[1, P]], channel_multiplier=-1).then_inc(consts, 1)

            def low_parts(q):
                for w in range(2):
                    for c, src in ((1, th[q % 2]), (0, tn[q % 2])):
                        pool.wait_ge(sc_ok, 4 * q + 2 * w + 2 - c)
                        pool.tensor_tensor(sc_lo[w][:, c, q * QC:q * QC + QC], src[:, w], sc_hi[w][:, c, q * QC:q * QC + QC],
                                           ALU.subtract).then_inc(lo_ok, 1)

            def add_bo(q):
                pool.wait_ge(xn_ok, q + 1)
                r = res[:, q * TPC:(q + 1) * TPC, :]
                pool.tensor_tensor(r, r, bo_b.unsqueeze(1).to_broadcast([P, TPC, D]), ALU.add).then_inc(bo_added, 1)

            low_parts(0)
            pool.wait_ge(norm_ok, 1)
            for t in range(2 * TPC, NT):
                ins = pool.tensor_scalar(xn1[:, t, :], res[:, t, :], mv_late[:, t - 2 * TPC, 0:1], rstd_late[:, t - 2 * TPC:t - 2 * TPC + 1],
                                         ALU.subtract, ALU.mult)
                if t % TPC == TPC - 1:
                    ins.then_inc(xn_ok, 1)
            for q in range(1, NQ):
                low_parts(q)
            pool.wait_ge(ld_small, 64)
            for q in range(NQ):
                add_bo(q)

            pool.wait_ge(k_evac, 2 * len(KCH))
            ch.link(pool.tensor_tensor(ksum[:, :, 0:2], ksum[:, :, 0:2], ksum[:, :, 2:4], ALU.add))
            ch.link(pool.tensor_tensor(ksum[:, :, 0:1], ksum[:, :, 0:1], ksum[:, :, 1:2], ALU.add))
            ch.link(pool.tensor_scalar(kneg[:, :], ksum[:, :, 0], -1.0 / M, None, ALU.mult))
            for c in range(KD):
                ch.inc(pool.tensor_scalar(kf[:, c], kf[:, c], kneg[:, c:c + 1], None, ALU.add))
            ch.wait()
            pool.wait_ge(xn_T, 2 * NQ)
            ch.link(pool.tensor_copy(k_bf[:, 0], kf[:, :, :]))
            ch.link(pool.tensor_tensor(kf, kf, k_bf[:, 0], ALU.subtract))
            ch.link(pool.tensor_copy(k_bf[:, 1], kf))
            ch.link(pool.tensor_tensor(kf, kf, k_bf[:, 1], ALU.subtract))
            ch.inc(pool.tensor_copy(k_bf[:, 2], kf))
            ch.link(pool.tensor_copy(b1s[:, 0], b1f[:, :]))
            ch.link(pool.tensor_tensor(b1r[:, :], b1f[:, :], b1s[:, 0], ALU.subtract))
            ch.link(pool.tensor_copy(b1s[:, 1], b1r[:, :]))
            ch.link(pool.tensor_tensor(b1r[:, :], b1r[:, :], b1s[:, 1], ALU.subtract))
            pool.tensor_copy(b1s[:, 2], b1r[:, :]).then_inc(k_split, 1)

            pool.wait_ge(k_split, 1)
            for j in range(3):
                pool.dma_start(k_parts[j].rearrange("(c p) m -> p c m", c=KD), k_bf[:, j]).then_inc(k_stored, 16)
            for j in range(3):
                pool.dma_start(b1_parts[j].rearrange("(p n) -> p n", p=P), b1s[:, j]).then_inc(b1_stored, 16)
            pool.wait_ge(k_stored, 48)
            for r in range(6):
                k_stack(pool, 0, r).then_inc(st_k0, 16)

            pool.wait_ge(xn2_ok, NQ)
            pool.tensor_tensor(res[:, :, :], res[:, :, :], b2_b.unsqueeze(1).to_broadcast([P, NT, D]), ALU.add).then_inc(b2_added, 1)

            pool.wait_ge(f_h, 1)
            pool.wait_ge(b1_stored, 48)
            for dst, pattern, first, per_row in ((revi[:, :], [[-1, E]], E, 0), (bl_i, [[1, 24]], 0, 0), (tok, [[P, NT]], 0, 1),
                                                 (lane, [[1, P]], 0, 0), (pad_row, [[1, 1]], T, 1)):
                pool.iota(dst, pattern, base=first, channel_multiplier=per_row,
                          allow_small_or_imprecise_dtypes=True).then_inc(late_consts, 1)

            def gather(b, j):
                pool.indirect_dma_start(out=xg[j], out_offset=None, in_=x_rows[:, :],
                                        in_offset=bass.IndirectOffsetOnAxis(ap=token_in[:, b:b + 1], axis=0)).then_inc(g_ld[j], 16)

            def scatter(b, j):
                pool.wait_ge(g_ys, b + 1)
                pool.indirect_dma_start(out=out_rows, out_offset=bass.IndirectOffsetOnAxis(ap=token_out[:, b:b + 1], axis=0),
                                        in_=ys[j], in_offset=None, bounds_check=T - 1, oob_is_err=False).then_inc(g_st[j], 16)

            def gather_next(b, j):
                pool.wait_ge(g_tr, b - 1)
                pool.wait_ge(g_rs, b - 1)
                gather(b, j)

            for q in range(NQ):
                pool.wait_ge(row_st[q], 32)
            pool.wait_ge(r_slots, 3)
            gather(0, 0)
            gather(1, 1)
            gather_next(2, 0)
            gather_next(3, 1)
            for b in range(NB_LOOP):
                scatter(b, b % 2)
                if b + 4 < NB:
                    gather_next(b + 4, b % 2)
            filled = pool.value_load(n_blocks, min_val=0, max_val=NB)
            for blocks in NB_TAIL:
                with pool.If(filled > blocks[0]):
                    for b in blocks:
                        scatter(b, b % 2)
                        if b + 4 < NB:
                            gather_next(b + 4, b % 2)
                    for b in blocks:
                        pool.wait_ge(g_st[b % 2], 16 * (b // 2 + 1))
            for j in range(2):
                pool.wait_ge(g_st[j], 16 * (NB_LOOP // 2))
                pool.wait_ge(g_ld[j], 16 * ((NB_LOOP + 4) // 2))

        @block.tensor
        def _(pe):
            def bank(i, n=512, p=P):
                return psum[0:p, i, 0:n]

            turn_banks = [(5, 6), (0, 1), (5, 6), (5, 6)]
            qkv_banks = [(7, 5, 6), (2, 3, 4), (7, 5, 6), (7, 5, 6)]

            def turn_x(q):
                pe.wait_ge(xn_ok, q + 1)
                if q >= 2:
                    before = 0 if q == 2 else 2
                    pe.wait_ge(th_ok, 2 * before + 2)
                    pe.wait_ge(v_ok, before + 1)
                for k in range(KD):
                    for t in range(TPC):
                        mm = pe.transpose(psum[:, turn_banks[q][k], t * P:t * P + P], xn1[:, q * TPC + t, k * P:k * P + P], ident[:, :])
                    mm.then_inc(xn_T, 1)

            def qkv(q):
                pe.wait_ge(xT_ok, 2 * q + 2)
                for w in range(2):
                    for k in range(KD):
                        mm = pe.matmul(bank(qkv_banks[q][w]), wqkv[:, w, k, :], xT[q % 2][:, k, :], start=(k == 0), stop=(k == KD - 1))
                    mm.then_inc(qkv_mm, 1)
                for t in range(TPC):
                    for k in range(KD):
                        mm = pe.matmul(psum[:, qkv_banks[q][2], t * P:t * P + P], xT[q % 2][:, k, t * P:t * P + P], wqkv[:, 2, k, :],
                                       start=(k == 0), stop=(k == KD - 1))
                mm.then_inc(qkv_mm, 1)

            def cross_keys(i):
                j, c = i // KD, i % KD
                m0, mn = KCH[j]
                if i == 0:
                    pe.wait_ge(ld_y, 48)
                    pe.wait_ge(th_ok, 2 * NQ)
                    pe.wait_ge(v_ok, NQ)
                if i >= 3:
                    pe.wait_ge(k_evac, i - 2)
                for y in range(2):
                    mm = pe.matmul(bank(5 + i % 3, mn), wk_x[:, y, c * P:c * P + P], yT[:, y, m0:m0 + mn], start=(y == 0), stop=(y == 1))
                mm.then_inc(k_proj, 1)

            def cross_values(t):
                n = P if t < MT - 1 else MLAST
                if t == 0:
                    pe.wait_ge(s_exp, S_PAIRS * NQ)
                if t >= 4:
                    pe.wait_ge(v_evac, t - 3)
                for y in range(2):
                    mm = pe.matmul(bank(t % 4, D, n), yT[:, y, t * P:t * P + n], wv_x[:, y, :], start=(y == 0), stop=(y == 1))
                mm.then_inc(v_proj, 1)

            def scores(u, i):
                n = S_PAIRS * u + i
                if not (isinstance(u, int) and n < 2):
                    pe.wait_ge(s_exp, n - 1)
                if isinstance(u, int) and i % 2 == 0:
                    pe.wait_ge(lo_ok, 4 * (i // 2 + 1))
                for h in range(2):
                    kt = 2 * i + h
                    passes = [(k_, q_, c) for k_, q_ in ((sc_hi, sc_hi), (sc_hi, sc_lo), (sc_lo, sc_hi)) for c in range(2)]
                    for n_, (k_, q_, c) in enumerate(passes):
                        mm = pe.matmul(bank(2 * (i % 2) + h), k_[1][:, c, kt * P:kt * P + P], q_[0][:, c, ds(u * QC, QC)],
                                       start=(n_ == 0), stop=(n_ == len(passes) - 1))
                mm.then_inc(s_mm, 1)

            def pv(u, i):
                n = S_PAIRS * u + i
                pe.wait_ge(s_exp, n + 1)
                if isinstance(u, int) and u == 0 and i % 2 == 0:
                    pe.wait_ge(v_ok, max(i // 2 + 1, 2))
                if i == 0 and not (isinstance(u, int) and u == 0):
                    pe.wait_ge(o_evac, u)
                for h in range(2):
                    kt = 2 * i + h
                    mm = pe.matmul(bank(4), v_s[:, kt, :], pbuf[:, i % 4, h * QC:h * QC + QC], start=(kt == 0), stop=(kt == NT - 1))
                mm.then_inc(s_pv, 1)

            def tail_den(u):
                pe.wait_ge(acc_ok, u + 1)
                pe.matmul(bank(7), ones[:, :], acc1, start=True, stop=True).then_inc(den_mm, 1)

            def tail_wo(u):
                pe.wait_ge(aT_ok, u + 1)
                for t in range(TPC):
                    mm = pe.matmul(psum[:, 6 + t // 2, (t % 2) * D:(t % 2) * D + D], aT[:, t * P:t * P + P], wo_s, start=True, stop=True)
                mm.then_inc(wo_mm, 1)

            def tail_turn(u):
                pe.wait_ge(xn2_ok, u + 1)
                for k in range(KD):
                    for t in range(TPC):
                        mm = pe.transpose(psum[:, 6 + k, t * P:t * P + P], xn2[:, t, k * P:k * P + P], ident[:, :])
                    mm.then_inc(xn2_T, 1)

            def tail_q(u):
                pe.wait_ge(x2T_ok, 2 * u + 2)
                for c in range(KD):
                    for k in range(KD):
                        mm = pe.matmul(bank(5 + c), wq_x[:, k, c * P:c * P + P], xT[0][:, k, :], start=(k == 0), stop=(k == KD - 1))
                    mm.then_inc(q_mm, 1)

            def self_unit(u):
                for i in range(S_PAIRS):
                    scores(u, i)
                    if i:
                        pv(u, i - 1)
                    else:
                        pv(u - 1, S_PAIRS - 1)
                    if i == 1:
                        tail_den(u - 1)
                    if i == 3:
                        tail_wo(u - 1)
                    if i == 5:
                        tail_turn(u - 1)
                    if i == 6:
                        tail_q(u - 1)

            pe.wait_ge(consts, 5)
            pe.wait_ge(ld_wqkv, 16)
            for q in range(2):
                turn_x(q)
                qkv(q)
            pe.wait_ge(xT_ok, 4)
            for i in range(S_PAIRS):
                if i == 1:
                    pe.wait_ge(th_ok, 4)
                scores(0, i)
                if i == 1:
                    turn_x(2)
                if i == 3:
                    pv(0, 2)
                    qkv(3)
                elif i:
                    pv(0, i - 1)
                if i == 1:
                    qkv(2)
                if i == 2:
                    turn_x(3)
                if i >= 5:
                    cross_keys(2 * (i - 5))
                    cross_keys(2 * (i - 5) + 1)
            cross_keys(6)
            cross_keys(7)
            pe.wait_ge(k_evac, 8)
            pe.wait_ge(ld_ws, 80)
            with pe.Fori(1, NQ) as u:
                self_unit(u)
            pv(NQ - 1, S_PAIRS - 1)
            fill = [(0, 3), (3, 6), (6, 10), (10, 13)]
            for step, (t0, t1) in zip((tail_den, tail_wo, tail_turn, tail_q), fill):
                for t in range(t0, t1):
                    cross_values(t)
                step(NQ - 1)

            def c_scores(u, g, qc, t, hf):
                n = P if t < MT - 1 else MLAST
                i = 2 * t + hf
                if i >= 3:
                    pe.wait_ge(c_exp, 2 * MT * u + i - 2)
                elif not (isinstance(u, int) and u == 0):
                    pe.wait_ge(c_exp, 2 * MT * u - (2 * MT - 1 - [24, 25, 23][i]))
                for h in range(2):
                    hh = 2 * hf + h
                    mm = pe.matmul(bank(2 * (i % 3) + h, QC, n), kst[g][:, hh, t * P:t * P + n], qst[g][:, hh, ds(qc * QC, QC)],
                                   start=True, stop=True)
                mm.then_inc(c_mm, 1)

            def c_values(u, g, t):
                n = P if t < MT - 1 else MLAST
                pe.wait_ge(c_exp, 2 * MT * u + 2 * t + 2)
                if t == 0 and not (isinstance(u, int) and u == 0):
                    pe.wait_ge(c_evac, u)
                for h in range(G):
                    hh = g * G + h
                    mm = pe.matmul(psum[32 * h:32 * h + VW, 6, :], vx[0:n, t, hh * VW:(hh + 1) * VW],
                                   p_slot(2 * t + h // 2)[0:n, (h % 2) * QC:(h % 2) * QC + QC], start=(t == 0), stop=(t == MT - 1),
                                   tile_position=(0, 32 * h))
                mm.then_inc(c_pv, 1)

            def c_turn(u):
                pe.wait_ge(c_evac, u + 1)
                if not (isinstance(u, int) and u == 0):
                    pe.wait_ge(c_xo, u)
                for t in range(TPC):
                    mm = pe.transpose(psum[:, 7, t * P:t * P + P], oT[:, t * P:t * P + P], ident[:, :])
                mm.then_inc(c_tr, 1)

            def cross_unit(u, g, qc, first):
                g_before = g if not isinstance(qc, int) else g - 1
                for t in range(MT):
                    c_scores(u, g, qc, t, 0)
                    if t >= 2:
                        c_values(u, g, t - 2)
                    elif not first:
                        c_values(u - 1, g_before, MT - 2 + t)
                    c_scores(u, g, qc, t, 1)
                    if t == 3 and not first:
                        c_turn(u - 1)

            pe.wait_ge(o_clear, 1)
            pe.wait_ge(v_evac, MT)
            pe.wait_ge(st_k0, 96)
            pe.wait_ge(st_q0, 96)
            cross_unit(0, 0, 0, True)
            with pe.Fori(1, NQ) as qc:
                pe.wait_ge(st_q0, 96 * qc + 96)
                cross_unit(qc, 0, qc, False)
            for g in range(1, NG):
                pe.wait_ge(st_ld[g], 12 * 16)
                cross_unit(NQ * g, g, 0, False)
                with pe.Fori(1, NQ) as qc:
                    cross_unit(qc + NQ * g, g, qc, False)
            c_values(NQ * NG - 1, NG - 1, MT - 2)
            c_values(NQ * NG - 1, NG - 1, MT - 1)
            c_turn(NQ * NG - 1)

            pe.wait_ge(bad_ok, 1)
            pe.matmul(psum[:, 7, 0:1], ones[:, :], small[:, 0:1], start=True, stop=True).then_inc(bad_mm, 1)
            pe.wait_ge(flag_ok, 1)
            with pe.If(pe.value_load(again[0:1, 0:1], min_val=0, max_val=P) > 0):
                with pe.Fori(0, NH) as h:
                    with pe.Fori(0, NT) as t:
                        i = h * NT + t
                        pe.wait_ge(m_ld, 12 * 16 * (h + 1))
                        pe.wait_ge(m_out, i + 1)
                        for c, (m0, mn) in enumerate(KCH):
                            mm = pe.matmul(bank(c, 401), gq[:, ds(t * P, P)], gk[:, m0:m0 + 401], start=True, stop=True)
                        mm.then_inc(m_mm, 1)
                        pe.wait_ge(m_exp, 2 * i + 2)
                        for k in range(MT):
                            n = P if k < MT - 1 else MLAST
                            mm = pe.transpose(psum[0:n, 4 + k // 4, (k % 4) * P:(k % 4) * P + P], gp[:, k * P:k * P + n], ident[:, :])
                        mm.then_inc(m_tr, 1)
                        pe.wait_ge(m_pT, 2 * i + 2)
                        for k in range(MT):
                            n = P if k < MT - 1 else MLAST
                            mm = pe.matmul(psum[:, 0, 0:VW], gpT[0:n, k, :], vx[0:n, k, ds(h * VW, VW)], start=(k == 0), stop=(k == MT - 1))
                        mm.then_inc(m_pv, 1)
                pe.wait_ge(m_out, NT * NH + 1)

            def f_turn(q):
                if q == 0:
                    pe.wait_ge(c_exp, 2 * MT * NQ * NG)
                    pe.wait_ge(c_xo, NQ * NG)
                for k in range(KD):
                    if q >= 2:
                        pe.wait_ge(r_xT, 2 * (q - 2) + k + 1)
                    for t in range(TPC):
                        mm = pe.transpose(bank(k)[:, t * P:t * P + P], xo[:, q * TPC + t, k * P:k * P + P], ident[:, :])
                    mm.then_inc(f_tr, 1)

            def f_up(q):
                pe.wait_ge(f_xT, 2 * q + 2)
                for f in range(NF1):
                    i = NF1 * q + f
                    if i >= 3:
                        pe.wait_ge(f_relu, i - 2)
                    for k in range(KD):
                        mm = pe.matmul(bank(2 + i % 3), w1_x[:, k, f * P:f * P + P], xT[q % 2][:, k, :], start=(k == 0), stop=(k == KD - 1))
                    mm.then_inc(f_h, 1)

            def f_down(q):
                pe.wait_ge(f_relu, NF1 * (q + 1))
                if q:
                    pe.wait_ge(f_res, q)
                for t in range(TPC):
                    for f in range(NF1):
                        mm = pe.matmul(psum[:, 6 + t // 2, (t % 2) * D:(t % 2) * D + D], h_x[:, f, t * P:t * P + P], w2_x[:, f, :],
                                       start=(f == 0), stop=(f == NF1 - 1))
                mm.then_inc(f_y, 1)

            def f_router(q):
                pe.wait_ge(xn3_ok, q + 1)
                for k in range(KD):
                    for t in range(TPC):
                        mm = pe.transpose(bank(k)[:, t * P:t * P + P], xn[:, q * TPC + t, k * P:k * P + P], ident[:, :])
                    mm.then_inc(r_tr, 1)
                pe.wait_ge(r_xT, 2 * q + 2)
                if q:
                    pe.wait_ge(r_one, q)
                    if q > 1:
                        pe.wait_ge(r_used, q if q == NQ - 1 else q - 1)
                for t in range(TPC):
                    for k in range(KD):
                        mm = pe.matmul(psum[:, 5, (q * TPC + t) * E:(q * TPC + t + 1) * E], xn3T[:, k, t * P:t * P + P], wr[:, k, :],
                                       start=(k == 0), stop=(k == KD - 1))
                    mm.then_inc(r_lg, 1)

            def f_rank(q):
                pe.wait_ge(r_one, q + 1)
                if q:
                    pe.wait_ge(r_used, q)
                o_q = oneh[:, q * TPC:(q + 1) * TPC, :].rearrange("p t e -> p (t e)")
                pe.matmul(psum[:, 5, P:P + TPC * E], tri[:, :], o_q, start=True, stop=True)
                pe.matmul(psum[:, 5, P + TPC * E:P + 2 * TPC * E], ones[:, :], o_q, start=True, stop=True).then_inc(r_rank, 1)

            for q in range(NQ):
                f_turn(q)
                f_up(q)
                if q:
                    f_router(q - 1)
                if q >= 2:
                    f_rank(q - 2)
                f_down(q)
            f_rank(NQ - 2)
            f_router(NQ - 1)
            f_rank(NQ - 1)

            pe.wait_ge(r_to, 3)
            for t in range(NT):
                mm = pe.matmul(psum[:, 7, 0:72], in_block[:, t, :], to_block[:, t, :, :].rearrange("p w b -> p (w b)"),
                               start=(t == 0), stop=(t == NT - 1))
            mm.then_inc(r_table, 1)

            def expert(b):
                return pe.value_load(bl_e[0:1, ds(b, 1)], min_val=0, max_val=E - 1)

            def g_turn(b, j, half):
                pe.wait_ge(g_ld[j], 16 * (half + 1))
                if not (isinstance(b, int) and b == 0):
                    pe.wait_ge(g_xT, b)
                for k in range(KD):
                    mm = pe.transpose(psum[:, 6, k * P:k * P + P], xg[j][:, k * P:k * P + P], ident[:, :])
                mm.then_inc(g_tr, 1)

            def g_up(b, j):
                e = expert(b)
                pe.wait_ge(g_xT, b + 1)
                if not (isinstance(b, int) and b < 2):
                    pe.wait_ge(g_act, b - 1)
                for n in range(2):
                    pe.matmul(bank(2 * j + n), ones_b[:, :], b1p[:, ds(e * F + n * 512, 512)], start=True, stop=False)
                    for k in range(KD):
                        mm = pe.matmul(bank(2 * j + n), xgT[j][:, k, :], w1v[:, k, ds(e * F + n * 512, 512)], start=False, stop=(k == KD - 1))
                mm.then_inc(g_h, 1)

            def g_hidden(b, j):
                pe.wait_ge(g_act, b + 1)
                if not (isinstance(b, int) and b == 0):
                    pe.wait_ge(g_hTa, b)
                    pe.wait_ge(g_hTd, b)
                for f in range(NF):
                    mm = pe.transpose(psum[:, 4 + f // 4, (f % 4) * P:(f % 4) * P + P], hs[j][:, f * P:f * P + P], ident[:, :])
                mm.then_inc(g_ht, 1)

            def g_down(b, j):
                e = expert(b)
                pe.wait_ge(g_hTa, b + 1)
                pe.wait_ge(g_hTd, b + 1)
                if not (isinstance(b, int) and b == 0):
                    pe.wait_ge(g_sum, b)
                for f in range(NF):
                    mm = pe.matmul(psum[:, 7, 0:D], hT[j][:, f, :], arena[:, ds(e * (NF * D) + f * D, D)], start=(f == 0), stop=(f == NF - 1))
                mm.then_inc(g_y, 1)

            pe.wait_ge(r_blk, 1)
            pe.wait_ge(ld_w1e, 32)
            pe.wait_ge(ld_b1e, 16)
            pe.wait_ge(ld_w2e, 16 * E)
            g_turn(0, 0, 0)
            g_turn(1, 1, 0)
            g_up(0, 0)
            with pe.Fori(0, NB_LOOP // 2) as i:
                for j in range(2):
                    b = 2 * i + j
                    g_hidden(b, j)
                    g_up(b + 1, 1 - j)
                    g_turn(b + 2, j, i + 1)
                    g_down(b, j)
            filled = pe.value_load(n_blocks, min_val=0, max_val=NB)
            for blocks in NB_TAIL:
                with pe.If(filled > blocks[0]):
                    for b in blocks:
                        g_hidden(b, b % 2)
                        if b + 1 < NB:
                            g_up(b + 1, (b + 1) % 2)
                        if b + 2 < NB:
                            g_turn(b + 2, b % 2, (b + 2) // 2)
                        g_down(b, b % 2)

        @block.scalar
        def _(act):
            act.dma_start(cols[:, :], a["cols"]).then_inc(ld_small, 16)
            act.dma_start(rows[:, :], a["rows"].partition_broadcast(P)).then_inc(ld_small, 16)
            act.dma_start(bo_b, a["bo"].partition_broadcast(P)).then_inc(ld_small, 16)
            act.dma_start(b1f[:, :], a["b1"].rearrange("(p n) -> p n", p=P)).then_inc(ld_small, 16)
            act.dma_start(yT, a["yT"].rearrange("(c p) m -> p c m", c=2)).then_inc(ld_y, 16)
            act.dma_start(wk_x, a["xwk"].rearrange("(c p) n -> p c n", c=2)).then_inc(ld_y, 16)
            act.dma_start(wv_x, a["xwv"].rearrange("(c p) n -> p c n", c=2)).then_inc(ld_y, 16)
            act.dma_start(wo_s, a["wo"]).then_inc(ld_ws, 16)
            act.dma_start(wq_x, a["xwq"].rearrange("(c p) n -> p c n", c=KD)).then_inc(ld_ws, 16)
            act.dma_start(w1_x[:, :, :], a["xw1"].rearrange("(c p) n -> p c n", c=KD)).then_inc(ld_ws, 16)
            act.dma_start(w2_x, a["xw2"].rearrange("(c p) n -> p c n", c=NF1)).then_inc(ld_ws, 16)
            act.dma_start(wr[:, :, :], a["wr"].rearrange("(c p) n -> p c n", c=KD)).then_inc(ld_ws, 16)
            def cross_key(i):
                (m0, mn), c = KCH[i // KD], i % KD
                act.wait_ge(k_proj, i + 1)
                act.activation(kf[:, c, m0:m0 + mn], psum[:, 5 + i % 3, 0:mn], ACT.Identity, bias=cols[:, XBK + c:XBK + c + 1],
                               accum_out=ksum[:, c, i // KD:i // KD + 1]).then_inc(k_evac, 1)

            turn_banks = [(5, 6), (0, 1), (5, 6), (5, 6)]
            qk_banks = [(7, 5), (2, 3), (7, 5), (7, 5)]

            def x_turned(q):
                for k in range(KD):
                    act.wait_ge(xn_T, 2 * q + k + 1)
                    if q >= 2:
                        act.wait_ge(qkv_mm, 3 * (q - 1))
                    act.copy(xT[q % 2][:, k, :], psum[:, turn_banks[q][k], :]).then_inc(xT_ok, 1)

            def angles(q):
                for w in range(2):
                    act.wait_ge(qkv_mm, 3 * q + w + 1)
                    if q >= 2:
                        act.wait_ge(lo_ok, 4 * (q - 2) + 2 * w + 2)
                    act.activation(th[q % 2][:, w], psum[:, qk_banks[q][w], :], ACT.Identity, bias=bqk[:, w:w + 1], scale=inv_w[:, 0:1]).then_inc(th_ok, 1)

            def sines(q):
                chunk, th_q, tn_q = ds(q * QC, QC), th[q % 2], tn[q % 2]
                for w in range(2):
                    act.wait_ge(ang_ok, 2 * q + w + 1)
                    act.activation(tn_q[:, w], th_q[:, w], ACT.Abs).then_inc(abs_ok, 1)
                    act.activation(sc_hi[w][:, 1, chunk], th_q[:, w], ACT.Sin).then_inc(act_own, 1)
                    act.wait_ge(abs_ok, 2 * q + w + 1)
                    act.wait_ge(act_own, 4 * q + 2 * w + 1)
                    act.activation(th_q[:, w], th_q[:, w], ACT.Sin).then_inc(sc_ok, 1)
                    act.activation(sc_hi[w][:, 0, chunk], tn_q[:, w], ACT.Sin, bias=half_pi[:, 0:1], scale=-1.0).then_inc(act_own, 1)
                    act.wait_ge(act_own, 4 * q + 2 * w + 2)
                    act.activation(tn_q[:, w], tn_q[:, w], ACT.Sin, bias=half_pi[:, 0:1], scale=-1.0).then_inc(sc_ok, 1)

            act.wait_ge(consts, 5)

            def exp_self(u, i):
                n = S_PAIRS * u + i
                act.wait_ge(s_mm, n + 1)
                first = isinstance(u, int) and u == 0
                if i >= 4:
                    act.wait_ge(s_pv, n - 3)
                    act.wait_ge(s_acc, (S_PAIRS - 1) * u + max(i - 4, 1))
                elif not first:
                    act.wait_ge(s_pv, n - 3)
                    act.wait_ge(s_acc, (S_PAIRS - 1) * (u - 1) + i + 4)
                act.activation(pbuf[:, i % 4, :], psum[:, 2 * (i % 2):2 * (i % 2) + 2, :].rearrange("p b n -> p (b n)"),
                               ACT.Exp, scale=1.0 / math.sqrt(HD)).then_inc(s_exp, 1)

            def tail_xT(u):
                for k in range(KD):
                    act.wait_ge(xn2_T, 2 * u + k + 1)
                    act.copy(xT[0][:, k, :], psum[:, 6 + k, :]).then_inc(x2T_ok, 1)

            def tail_q(u):
                for c in range(KD):
                    act.wait_ge(q_mm, 2 * u + c + 1)
                    if c == 0 and not (isinstance(u, int) and u == 0):
                        act.wait_ge(q_split, u)
                    act.activation(qf[:, c], psum[:, 5 + c, :], ACT.Identity, bias=cols[:, XBQ + c:XBQ + c + 1]).then_inc(q_ok, 1)

            x_turned(0)
            act.wait_ge(col_ok, 2)
            angles(0)
            x_turned(1)
            sines(0)
            angles(1)
            for i in range(S_PAIRS):
                exp_self(0, i)
                if i == 0:
                    sines(1)
                    x_turned(2)
                if i == 1:
                    angles(2)
                if i == 2:
                    sines(2)
                    x_turned(3)
                if i == 3:
                    angles(3)
                if i == 4:
                    sines(3)
                if i >= 6:
                    cross_key(2 * (i - 6))
                    cross_key(2 * (i - 6) + 1)
            for i in range(4, 8):
                cross_key(i)
            with act.Fori(1, NQ) as u:
                for i in range(S_PAIRS):
                    exp_self(u, i)
                    if i == 5:
                        tail_xT(u - 1)
                    if i == 6:
                        tail_q(u - 1)
            def cross_value(t):
                n = P if t < MT - 1 else MLAST
                act.wait_ge(v_proj, t + 1)
                act.copy(vx[0:n, t, :].rearrange("p (h w) -> p h w", w=VW)[:, :, 0:DH],
                         psum[0:n, t % 4, 0:D].rearrange("p (h d) -> p h d", d=DH)).then_inc(v_evac, 1)

            for t in range(10):
                cross_value(t)
            tail_xT(NQ - 1)
            for t in range(10, MT):
                cross_value(t)
            tail_q(NQ - 1)

            def exp_cross(u):
                for i in range(2 * MT):
                    t = i // 2
                    n = P if t < MT - 1 else MLAST
                    act.wait_ge(c_mm, 2 * MT * u + i + 1)
                    if 2 <= t < MT - 1:
                        act.wait_ge(c_pv, MT * u + t - 1)
                    elif not isinstance(u, int):
                        act.wait_ge(c_pv, MT * u if t == MT - 1 else MT * u - 2 + t)
                    act.activation(p_slot(i)[0:n, :], psum[0:n, 2 * (i % 3):2 * (i % 3) + 2, :].rearrange("p b n -> p (b n)"),
                                   ACT.Exp, scale=1.0 / math.sqrt(DH)).then_inc(c_exp, 1)

            exp_cross(0)
            with act.Fori(1, NQ * NG) as u:
                exp_cross(u)

            act.wait_ge(flag_ok, 1)
            with act.If(act.value_load(again[0:1, 0:1], min_val=0, max_val=P) > 0):
                with act.Fori(0, NT * NH) as i:
                    act.wait_ge(m_max, i + 1)
                    sc_m = 1.0 / math.sqrt(DH)
                    act.activation(gp[:, 0:1600].rearrange("p (c n) -> p c n", c=4), psum[:, 0:4, 0:400], ACT.Exp,
                                   bias=small[:, 1:2], scale=sc_m).then_inc(m_exp, 1)
                    act.activation(gp[:, 1600:M], psum[:, 3, 400:401], ACT.Exp, bias=small[:, 1:2], scale=sc_m).then_inc(m_exp, 1)
                    act.wait_ge(m_tr, i + 1)
                    act.copy(gpT[:, 0:MT - 1, :], psum[:, 4:7, :].rearrange("p b (k n) -> p (b k) n", n=P)).then_inc(m_pT, 1)
                    act.copy(gpT[0:MLAST, MT - 1, :], psum[0:MLAST, 7, 0:P]).then_inc(m_pT, 1)

            def xn3_turned(q):
                for k in range(KD):
                    act.wait_ge(r_tr, 2 * q + k + 1)
                    if q:
                        act.wait_ge(r_lg, NT // NQ * q)
                    act.copy(xn3T[:, k, :], psum[:, k, :]).then_inc(r_xT, 1)

            for q in range(NQ):
                for f in range(NF1):
                    i = NF1 * q + f
                    act.wait_ge(f_h, i + 1)
                    if q:
                        act.wait_ge(f_y, q)
                    act.activation(h_x[:, f, :], psum[:, 2 + i % 3, :], ACT.Relu, bias=cols[:, XB1 + f:XB1 + f + 1]).then_inc(f_relu, 1)
                if q:
                    xn3_turned(q - 1)
            xn3_turned(NQ - 1)

            act.wait_ge(r_sub, NQ)
            act.wait_ge(f_y, NQ)
            act.activation(probs, l2, ACT.Exp).then_inc(r_exp, 1)


            def rows_turned(b, j):
                act.wait_ge(g_tr, b + 1)
                if not (isinstance(b, int) and b < 2):
                    act.wait_ge(g_h, b - 1)
                act.copy(xgT[j], psum[:, 6, 0:KD * P].rearrange("p (k n) -> p k n", k=KD)).then_inc(g_xT, 1)

            def gelu(b, j):
                act.wait_ge(g_h, b + 1)
                if not (isinstance(b, int) and b < 2):
                    act.wait_ge(g_ht, b - 1)
                act.activation(hs[j], psum[:, 2 * j:2 * j + 2, :].rearrange("p b n -> p (b n)"), ACT.Gelu).then_inc(g_act, 1)

            def hidden_turned(b, j):
                act.wait_ge(g_ht, b + 1)
                if not (isinstance(b, int) and b < 2):
                    act.wait_ge(g_y, b - 1)
                act.copy(hT[j][:, 0:4, :], psum[:, 4, :].rearrange("p (f n) -> p f n", f=4)).then_inc(g_hTa, 1)

            rows_turned(0, 0)
            rows_turned(1, 1)
            gelu(0, 0)
            hidden_turned(0, 0)
            rows_turned(2, 0)
            gelu(1, 1)
            hidden_turned(1, 1)
            rows_turned(3, 1)
            gelu(2, 0)
            with act.Fori(1, NB_LOOP // 2) as i:
                for j in range(2):
                    b = 2 * i + j
                    hidden_turned(b, j)
                    rows_turned(b + 2, j)
                    gelu(b + 1, 1 - j)
            filled = act.value_load(n_blocks, min_val=0, max_val=NB)
            for blocks in NB_TAIL:
                with act.If(filled > blocks[0]):
                    for b in blocks:
                        hidden_turned(b, b % 2)
                        if b + 2 < NB:
                            rows_turned(b + 2, b % 2)
                        if b + 1 < NB:
                            gelu(b + 1, (b + 1) % 2)

        @block.vector
        def _(dve):
            ch = Chain(dve, dve_own)

            def norm_stats(src, stats, mv, nv, nt, rstd, count):
                ch.inc(dve.memset(nv, 0.0))
                for t in range(count):
                    ch.inc(dve.bn_stats(stats[:, t, :], src[:, t, :]))
                ch.wait()
                ch.inc(dve.memset(nt, 0.0))
                for t in range(count):
                    ch.inc(dve.bn_aggr(mv[:, t, :], stats[:, t, :]))
                ch.wait()
                ch.link(dve.tensor_scalar(nv, mv[:, :, 1], EPS, None, ALU.add))
                ch.link(dve.tensor_scalar(rstd.bitcast(I32), nv.bitcast(I32), -0.5, float(0x5F3759DF), ALU.mult, ALU.add))
                for _ in range(3):
                    ch.link(dve.tensor_tensor(nt, rstd, rstd, ALU.mult))
                    ch.link(dve.tensor_tensor(nt, nt, nv, ALU.mult))
                    ch.link(dve.tensor_scalar(nt, nt, -0.5, 1.5, ALU.mult, ALU.add))
                    ins = dve.tensor_tensor(rstd, rstd, nt, ALU.mult)
                    if _ < 2:
                        ch.link(ins)
                return ins

            def rsqrt_norm(src, dst, signal):
                ch.link(norm_stats(src, stats, mv, nv[:, :], nt1[:, :], rstd[:, :], TPC))
                for t in range(TPC):
                    ins = dve.tensor_scalar(dst[:, t, :], src[:, t, :], mv[:, t, 0:1], rstd[:, t:t + 1], ALU.subtract, ALU.mult)
                    if t < TPC - 1:
                        ch.inc(ins)
                ins.then_inc(signal, 1)

            dve.memset(vx.rearrange("p t (h w) -> p t h w", w=VW)[:, :, :, DH:VW], 1.0).then_inc(ones_ok, 1)
            dve.memset(rmin[:, :, :], 1.0).then_inc(q_stored, 48)

            def norm1(q):
                dve.wait_ge(ld_x[q], 16)
                rsqrt_norm(res[:, q * TPC:(q + 1) * TPC, :], xn1[:, q * TPC:(q + 1) * TPC, :], xn_ok)

            def angles(q):
                for w in range(2):
                    th_q = th[q % 2][:, w]
                    dve.wait_ge(th_ok, 2 * q + w + 1)
                    ch.link(dve.tensor_scalar(turns, th_q, 1.0 / TWO_PI, MAGIC, ALU.mult, ALU.add))
                    ch.link(dve.tensor_scalar(turns, turns, MAGIC, None, ALU.subtract))
                    ch.link(dve.scalar_tensor_tensor(out=th_q, in0=turns, scalar=-C1, in1=th_q, op0=ALU.mult, op1=ALU.add))
                    ch.link(dve.scalar_tensor_tensor(out=th_q, in0=turns, scalar=-C2, in1=th_q, op0=ALU.mult, op1=ALU.add))
                    dve.tensor_scalar(th_q, th_q, PI_IN, -PI_IN, ALU.min, ALU.max).then_inc(ang_ok, 1)

            v_banks = [6, 4, 6, 6]

            def self_values(q):
                dve.wait_ge(qkv_mm, 3 * q + 3)
                dve.tensor_copy(v_s[:, q * TPC:(q + 1) * TPC, :], psum[:, v_banks[q], :].rearrange("p (t n) -> p t n", n=P)).then_inc(v_ok, 1)

            norm1(0)
            dve.wait_ge(ld_small, 64)
            ch.link(dve.tensor_scalar(inv_w[:, 1:2], cols[:, WL:WL + 1], 1e-8, None, ALU.add))
            ch.link(dve.reciprocal(inv_w[:, 0:1], inv_w[:, 1:2]))
            dve.tensor_scalar(bqk[:, 0:1], cols[:, BQ:BQ + 1], inv_w[:, 0:1], cols[:, PH:PH + 1], ALU.mult, ALU.add).then_inc(col_ok, 1)
            dve.tensor_scalar(bqk[:, 1:2], cols[:, BK:BK + 1], inv_w[:, 0:1], cols[:, PH:PH + 1], ALU.mult, ALU.add).then_inc(col_ok, 1)
            norm1(1)
            angles(0)
            self_values(0)
            for q in (2, 3):
                dve.wait_ge(ld_x[q], 16)
            norm_stats(res[:, 2 * TPC:NT, :], stats_late, mv_late, nv_late, nt_late, rstd_late, 2 * TPC).then_inc(norm_ok, 1)
            for q in (1, 2):
                angles(q)
                self_values(q)

            def accumulate(u, i):
                a_ = acc0 if isinstance(u, int) else acc
                dve.wait_ge(s_exp, S_PAIRS * u + i + 1)
                if i == 1:
                    dve.tensor_tensor(a_, pbuf[:, 0, :], pbuf[:, 1, :], ALU.add).then_inc(s_acc, 1)
                else:
                    dve.wait_ge(s_acc, (S_PAIRS - 1) * u + i - 1)
                    dve.tensor_tensor(a_, a_, pbuf[:, i % 4, :], ALU.add).then_inc(s_acc, 1)

            def total(u):
                a_ = acc0 if isinstance(u, int) else acc
                dve.wait_ge(s_acc, (S_PAIRS - 1) * (u + 1))
                dve.tensor_tensor(acc1, a_[:, 0:QC], a_[:, QC:2 * QC], ALU.add).then_inc(acc_ok, 1)
                dve.wait_ge(acc_ok, u + 1)

            def tail_out(u):
                dve.wait_ge(s_pv, S_PAIRS * (u + 1))
                dve.tensor_copy(o_raw, psum[:, 4, :]).then_inc(o_evac, 1)

            def tail_norm(u):
                dve.wait_ge(den_mm, u + 1)
                ch.inc(dve.reciprocal(rden, psum[:, 7, :]))
                ch.wait()
                dve.wait_ge(o_evac, u + 1)
                ch.link(dve.tensor_tensor(aT, o_raw, rden, ALU.mult))
                dve.tensor_scalar(aT, aT, cols[:, BV:BV + 1], None, ALU.add).then_inc(aT_ok, 1)

            def tail_res(u):
                dve.wait_ge(wo_mm, u + 1)
                r = res[:, ds(u * TPC, TPC), :]
                ch.link(dve.tensor_tensor(r.rearrange("p t n -> p (t n)"), r.rearrange("p t n -> p (t n)"),
                                          psum[:, 6:8, :].rearrange("p b n -> p (b n)"), ALU.add))
                rsqrt_norm(r, xn2, xn2_ok)

            def split_q(u):
                dve.wait_ge(q_ok, 2 * u + 2)
                dve.wait_ge(q_stored, 48 * (u + 1))
                ch.link(dve.tensor_copy(q_bf[:, 0], qf))
                ch.link(dve.tensor_tensor(qf, qf, q_bf[:, 0], ALU.subtract))
                ch.link(dve.tensor_copy(q_bf[:, 1], qf))
                ch.link(dve.tensor_tensor(qf, qf, q_bf[:, 1], ALU.subtract))
                dve.tensor_copy(q_bf[:, 2], qf).then_inc(q_split, 1)

            for i in range(1, S_PAIRS):
                accumulate(0, i)
                if i == 2:
                    angles(3)
                    self_values(3)
            dve.wait_ge(lo_ok, 4 * NQ)
            dve.wait_ge(bo_added, NQ)
            total(0)
            with dve.Fori(0, NQ - 1) as v:
                ch.enter(v, TAIL_LINKS)
                tail_out(v)
                for i in range(1, S_PAIRS):
                    accumulate(v + 1, i)
                    if i == 1:
                        tail_norm(v)
                    if i == 3:
                        tail_res(v)
                total(v + 1)
                split_q(v)
                ch.leave(NQ - 1)
            tail_out(NQ - 1)
            tail_norm(NQ - 1)
            tail_res(NQ - 1)
            split_q(NQ - 1)

            dve.wait_ge(q_ok, 2 * NQ)
            dve.memset(psum[:, 6, :], 0.0).then_inc(o_clear, 1)
            for g in range(NG):
                with dve.Fori(0, NQ) as qc:
                    ch.enter(qc, 3)
                    u = qc + NQ * g
                    dve.wait_ge(c_pv, MT * u + MT)
                    dve.tensor_copy(oT, psum[:, 6, :]).then_inc(c_evac, 1)
                    dve.wait_ge(c_tr, u + 1)
                    o_v = psum[:, 7, :].rearrange("p (t h w) -> p t h w", t=TPC, h=G)
                    ch.link(dve.reciprocal(rden_x[:, :, :], o_v[:, :, :, DH]))
                    ch.inc(dve.tensor_tensor(rmin[:, :, :], rmin[:, :, :], rden_x[:, :, :], ALU.min))
                    heads = slice(g * G * DH, (g + 1) * G * DH)
                    ch.link(dve.tensor_tensor(xo[:, ds(qc * TPC, TPC), heads].rearrange("p t (h d) -> p t h d", d=DH),
                                              o_v[:, :, :, 0:DH], rden_x[:, :, :].unsqueeze(3).to_broadcast([P, TPC, G, DH]), ALU.mult))
                    dve.tensor_tensor(xo[:, ds(qc * TPC, TPC), heads], xo[:, ds(qc * TPC, TPC), heads],
                                      bv_b[:, heads].unsqueeze(1).to_broadcast([P, TPC, G * DH]), ALU.add).then_inc(c_xo, 1)
                    ch.leave(NQ)

            ch.wait()
            dve.wait_ge(c_xo, NQ * NG)
            ch.link(dve.tensor_reduce(small[:, 1:2], rmin[:, :, :], AX.XY, ALU.min))
            dve.tensor_scalar(small[:, 0:1], small[:, 1:2], LEAST_RECIPROCAL, None, ALU.is_lt).then_inc(bad_ok, 1)
            dve.wait_ge(bad_mm, 1)
            dve.tensor_copy(again[:, :], psum[:, 7, 0:1]).then_inc(flag_ok, 1)
            dve.wait_ge(flag_ok, 1)
            with dve.If(dve.value_load(again[0:1, 0:1], min_val=0, max_val=P) > 0):
                dve.memset(small[:, 0:1], 0.0).then_inc(m_out, 1)
                with dve.Fori(0, NH) as h:
                    with dve.Fori(0, NT) as t:
                        i = h * NT + t
                        dve.wait_ge(m_out, i + 1)
                        dve.wait_ge(m_mm, i + 1)
                        dve.tensor_reduce(small[:, 0:1], psum[:, 0:4, 0:401], AX.XY, ALU.max).then_inc(m_red, 1)
                        dve.wait_ge(m_red, 2 * i + 1)
                        dve.tensor_scalar(small[:, 1:2], small[:, 0:1], -1.0 / math.sqrt(DH), None, ALU.mult).then_inc(m_max, 1)
                        dve.wait_ge(m_pv, i + 1)
                        dve.reciprocal(rden_x[:, 0, 0:1], psum[:, 0, DH:VW]).then_inc(m_red, 1)
                        dve.wait_ge(m_red, 2 * i + 2)
                        dve.scalar_tensor_tensor(out=duo[:, ds(t * D + h * DH, DH)], in0=psum[:, 0, 0:DH], scalar=rden_x[:, 0, 0:1],
                                                 in1=rows[:, ds(D + h * DH, DH)], op0=ALU.mult, op1=ALU.add).then_inc(m_out, 1)

            dve.wait_ge(b2_added, 1)

            def turned(q):
                for k in range(KD):
                    dve.wait_ge(f_tr, 2 * q + k + 1)
                    if q == 0:
                        dve.wait_ge(q_mm, 2 * NQ)
                    dve.tensor_copy(xT[q % 2][:, k, :], psum[:, k, :]).then_inc(f_xT, 1)

            def choose(q):
                tiles = slice(q * TPC, (q + 1) * TPC)
                dve.wait_ge(r_lg, TPC * (q + 1))
                if q:
                    dve.wait_ge(r_rank, q)
                else:
                    dve.wait_ge(late_consts, 5)
                ch.link(dve.tensor_tensor(lg, psum[:, 5, TPC * E * q:TPC * E * (q + 1)].rearrange("p (t e) -> p t e", e=E),
                                          br_b.unsqueeze(1).to_broadcast([P, TPC, E]), ALU.add))
                ch.link(dve.tensor_reduce(lmax, lg, AX.X, ALU.max))
                lmax_b = lmax.unsqueeze(2).to_broadcast([P, TPC, E])
                revi_b = revi[:, :].unsqueeze(1).to_broadcast([P, TPC, E])
                dve.tensor_tensor(l2[:, tiles, :], lg, lmax_b, ALU.subtract).then_inc(r_sub, 1)
                ch.link(dve.tensor_tensor(oneh[:, tiles, :], lg, lmax_b, ALU.is_equal))
                ch.link(dve.tensor_tensor(oneh[:, tiles, :], oneh[:, tiles, :], revi_b, ALU.mult))
                ch.link(dve.tensor_reduce(top[:, :], oneh[:, tiles, :], AX.X, ALU.max))
                dve.tensor_tensor(oneh[:, tiles, :], revi_b, top[:, :].unsqueeze(2).to_broadcast([P, TPC, E]), ALU.is_equal).then_inc(r_one, 1)
                dve.wait_ge(r_one, q + 1)

            def place(q):
                tiles = slice(q * TPC, (q + 1) * TPC)
                dve.wait_ge(r_rank, q + 1)
                in_bank = lambda i: psum[:, 5, P + TPC * E * i:P + TPC * E * (i + 1)].rearrange("p (t e) -> p t e", e=E)
                for t in range(TPC):
                    ch.link(dve.tensor_tensor(base[:, q * TPC + t + 1, :], base[:, q * TPC + t, :], in_bank(1)[:, t, :], ALU.add))
                dve.tensor_tensor(lg, in_bank(0), base[:, tiles, :], ALU.add).then_inc(r_used, 1)
                dve.wait_ge(r_used, q + 1)
                ch.link(dve.tensor_tensor(lg, lg, oneh[:, tiles, :], ALU.mult))
                ch.link(dve.tensor_reduce(rank[:, tiles], lg, AX.X, ALU.add))
                ch.link(dve.tensor_scalar(full[:, tiles], rank[:, tiles], 1.0 / P, -0.5 + 0.5 / P, ALU.mult, ALU.add))
                ch.link(dve.tensor_scalar(full[:, tiles], full[:, tiles], MAGIC, None, ALU.add))
                ch.link(dve.tensor_scalar(full[:, tiles], full[:, tiles], MAGIC, None, ALU.subtract))
                ch.link(dve.scalar_tensor_tensor(out=rank[:, tiles], in0=full[:, tiles], scalar=-float(P), in1=rank[:, tiles],
                                                 op0=ALU.mult, op1=ALU.add))
                dve.wait_ge(row_st[q // 2], 32)
                dve.wait_ge(r_tr, 2 * (q // 2) + 2)
                ch.inc(dve.tensor_tensor(in_block[:, tiles, :], lane.unsqueeze(1).to_broadcast([P, TPC, P]),
                                         rank[:, tiles].unsqueeze(2).to_broadcast([P, TPC, P]), ALU.is_equal))

            ch.inc(dve.memset(base[:, 0, :], 0.0))
            for i in range(2):
                ch.inc(dve.memset(cum[i], 0.0))
            turned(0)
            for q in range(NQ):
                dve.wait_ge(f_y, q + 1)
                r = res[:, q * TPC:(q + 1) * TPC, :]
                dve.tensor_tensor(r.rearrange("p t n -> p (t n)"), r.rearrange("p t n -> p (t n)"),
                                  psum[:, 6:8, :].rearrange("p b n -> p (b n)"), ALU.add).then_inc(f_res, 1)
                if q + 1 < NQ:
                    turned(q + 1)
                dve.wait_ge(f_res, q + 1)
                rsqrt_norm(r, xn[:, q * TPC:(q + 1) * TPC, :], xn3_ok)
                if q:
                    choose(q - 1)
                if q >= 2:
                    place(q - 2)
            place(NQ - 2)
            choose(NQ - 1)
            place(NQ - 1)

            e_cols = slice(4, 4 + E)
            ch.link(dve.tensor_scalar(nb, base[:, NT, :], 1.0 / P, 0.5 - 0.5 / P, ALU.mult, ALU.add))
            ch.link(dve.tensor_scalar(nb, nb, MAGIC, None, ALU.add))
            ch.link(dve.tensor_scalar(cum[0][:, e_cols], nb, MAGIC, None, ALU.subtract))
            cc = 0
            for s_ in (1, 2, 4):
                ch.link(dve.tensor_tensor(cum[1 - cc][:, e_cols], cum[cc][:, e_cols], cum[cc][:, 4 - s_:4 - s_ + E], ALU.add))
                cc = 1 - cc
            first_block = cum[cc][:, 3:3 + E].unsqueeze(1).to_broadcast([P, NT, E])
            ch.link(dve.tensor_tensor(prod, oneh, first_block, ALU.mult))
            ch.link(dve.tensor_reduce(top_all, prod, AX.X, ALU.add))
            ch.link(dve.tensor_tensor(full[:, :], full[:, :], top_all, ALU.add))
            per_block = lambda x: x.unsqueeze(2).to_broadcast([P, NT, 24])
            dve.tensor_tensor(to_block[:, :, 2, :], bl_i.unsqueeze(1).to_broadcast([P, NT, 24]), per_block(full[:, :]), ALU.is_equal).then_inc(r_to, 1)
            dve.wait_ge(r_to, 1)
            dve.tensor_tensor(to_block[:, :, 0, :], to_block[:, :, 2, :], per_block(tok), ALU.mult).then_inc(r_to, 1)
            dve.wait_ge(r_exp, 1)
            ch.link(dve.tensor_reduce(gate[:, :], probs, AX.X, ALU.add))
            ch.link(dve.reciprocal(gate[:, :], gate[:, :]))
            dve.tensor_tensor(to_block[:, :, 1, :], to_block[:, :, 2, :], per_block(gate[:, :]), ALU.mult).then_inc(r_to, 1)
            ch.link(dve.tensor_tensor(bl_c, bl_i.unsqueeze(2).to_broadcast([P, 24, E]), cum[cc][:, e_cols].unsqueeze(1).to_broadcast([P, 24, E]), ALU.is_ge))
            ch.link(dve.tensor_reduce(bl_f, bl_c[:, :, 0:E - 1], AX.X, ALU.add))
            ch.inc(dve.tensor_copy(n_blocks, cum[cc][0:1, 3 + E:4 + E]))
            ch.wait()
            dve.tensor_copy(bl_e, bl_f).then_inc(r_blk, 1)
            dve.wait_ge(r_table, 1)
            dve.wait_ge(r_blk, 1)
            dve.tensor_copy(token_in, psum[:, 7, 0:24]).then_inc(r_slots, 1)
            ch.inc(dve.tensor_copy(slot_gate, psum[:, 7, 24:48]))
            ch.link(dve.tensor_scalar(bl_f, psum[:, 7, 48:72], -1.0, 1.0, ALU.mult, ALU.add))
            ch.link(dve.tensor_scalar(bl_f, bl_f, pad_row, None, ALU.mult))
            ch.link(dve.tensor_tensor(bl_f, bl_f, psum[:, 7, 0:24], ALU.add))
            dve.tensor_copy(token_out, bl_f).then_inc(r_slots, 2)

            def expert(b):
                return dve.value_load(bl_e[0:1, ds(b, 1)], min_val=0, max_val=E - 1)

            def hidden_turned(b, j):
                dve.wait_ge(g_ht, b + 1)
                dve.tensor_copy(hT[j][:, 4:8, :], psum[:, 5, :].rearrange("p (f n) -> p f n", f=4)).then_inc(g_hTd, 1)

            def residuals(b, j, half):
                dve.wait_ge(g_ld[j], 16 * (half + 1))
                dve.tensor_copy(rs[j], xg[j][:, D:2 * D]).then_inc(g_rs, 1)

            def result(b, j, half):
                e = expert(b)
                dve.wait_ge(g_y, b + 1)
                if not (isinstance(b, int) and b < 2):
                    dve.wait_ge(g_st[j], 16 * half)
                dve.tensor_tensor(ys[j], psum[:, 7, 0:D], b2e[:, ds(e * D, D)], ALU.add).then_inc(g_sum, 1)
                dve.tensor_copy(gate_b, slot_gate[:, ds(b, 1)]).then_inc(g_gate, 1)
                dve.wait_ge(g_sum, b + 1)
                dve.wait_ge(g_gate, b + 1)
                dve.wait_ge(g_rs, b + 1)
                dve.scalar_tensor_tensor(out=ys[j], in0=ys[j], scalar=gate_b, in1=rs[j], op0=ALU.mult, op1=ALU.add).then_inc(g_ys, 1)
                dve.wait_ge(g_ys, b + 1)

            residuals(0, 0, 0)
            residuals(1, 1, 0)
            dve.wait_ge(ld_b2e, 16)
            for b in range(2):
                hidden_turned(b, b % 2)
                result(b, b % 2, 0)
                residuals(b + 2, b % 2, 1)
            with dve.Fori(1, NB_LOOP // 2) as i:
                for j in range(2):
                    b = 2 * i + j
                    hidden_turned(b, j)
                    result(b, j, i)
                    residuals(b + 2, j, i + 1)
            filled = dve.value_load(n_blocks, min_val=0, max_val=NB)
            for blocks in NB_TAIL:
                with dve.If(filled > blocks[0]):
                    for b in blocks:
                        hidden_turned(b, b % 2)
                        result(b, b % 2, b // 2)
                        if b + 2 < NB:
                            residuals(b + 2, b % 2, b // 2 + 1)


def kernel(**inputs):
    import numpy as np
    import concourse.bacc as bacc
    from concourse.bass_utils import run_bass_kernel_spmd

    v = {k: np.ascontiguousarray(x) for k, x in inputs.items()}
    c = lambda x, n: x.reshape(n, P).T
    arrays = {
        "x": v["x"],
        "yT": v["ctx_768"][0].T,
        "wqkv": np.stack([v["L0_attn_Wq"].T, v["L0_attn_Wk"].T, v["L0_attn_Wv"].T]),
        "wo": v["L0_attn_Wo"].T,
        "xwq": v["L0_xattn_Wq"], "xwk": v["L0_xattn_Wk"], "xwv": v["L0_xattn_Wv"], "xw1": v["L0_xattn_W1"], "xw2": v["L0_xattn_W2"],
        "wr": v["L0_ffn_Wr"], "w1": v["L0_ffn_W1"], "w2": v["L0_ffn_W2"],
        "b1": v["L0_ffn_b1"].reshape(-1), "b2": v["L0_ffn_b2"].reshape(-1),
        "cols": np.concatenate([c(v["L0_attn_bq"], 1), c(v["L0_attn_phase_bias"], 1), c(v["L0_attn_wavelengths"], 1), c(v["L0_attn_bk"], 1),
                                c(v["L0_attn_bv"], 1), c(v["L0_xattn_bq"], 2), c(v["L0_xattn_bk"], 2), c(v["L0_xattn_b1"], 4)], axis=1),
        "rows": np.concatenate([v["L0_xattn_b2"], v["L0_xattn_bv"], v["L0_ffn_br"]]), "bo": v["L0_attn_bo"],
    }
    nc = bacc.Bacc("TRN2", target_bir_lowering=False, num_devices=1)
    feeds, args = {}, {}
    for name, x in arrays.items():
        x = np.ascontiguousarray(x)
        feeds[f"in_{name}"] = x
        args[name] = nc.dram_tensor(f"in_{name}", x.shape, mybir.dt.from_np(x.dtype), kind="ExternalInput").ap()
    out = nc.dram_tensor("out_0", (1, T, D), F32, kind="ExternalOutput").ap()
    layer(nc, args, out)
    r = run_bass_kernel_spmd(nc, [feeds], core_ids=[0])
    return r.results[0]["out_0"]
```

```python
from contextlib import ExitStack
import math

import concourse.bass as bass
from concourse import mybir

F32 = mybir.dt.float32
BF16 = mybir.dt.bfloat16
F16 = mybir.dt.float16
I32 = mybir.dt.int32
U32 = mybir.dt.uint32
ALU = mybir.AluOpType
ACT = mybir.ActivationFunctionType
AX = mybir.AxisListType
ds = bass.ds

P = 128
T = 2048
D = 256
KD = D // P
NT = T // P
QC = 512
NQ = T // QC
TPC = QC // P
HD = 128
S_PAIRS = NT // 2
M = 1601
YD = 192
YC = YD // 2
NH = 16
DH = D // NH
G = 4
NG = NH // G
MT = -(-M // P)
MLAST = M - (MT - 1) * P
VW = DH + 1
F1 = 512
NF1 = F1 // P
E = 8
F = 1024
NF = F // P
NB = (T + E * (P - 1)) // P
NB_LOOP = 18
NB_TAIL = [[b] for b in range(NB_LOOP, NB)]
KCH = [(0, 400), (400, 400), (800, 400), (1200, 401)]
PARTS_Q = [0, 0, 0, 1, 1, 2]
PARTS_K = [0, 1, 2, 0, 1, 0]
RS = 6 * DH
EPS = 1e-5
TWO_PI = 2.0 * math.pi
C1 = 6.28125
C2 = TWO_PI - C1
MAGIC = 1.5 * 2.0 ** 23
PI_IN = 3.14159250
TAIL_LINKS = 34
LEAST_RECIPROCAL = 1e-30


class Chain:

    def __init__(self, eng, sem):
        self.eng, self.sem, self.base, self.n = eng, sem, 0, 0

    def inc(self, ins):
        self.n += 1
        ins.then_inc(self.sem, 1)

    def wait(self):
        self.eng.wait_ge(self.sem, self.base + self.n)

    def link(self, ins):
        self.inc(ins)
        self.wait()

    def enter(self, i, per):
        self.saved = (self.base + self.n, per)
        self.base, self.n = i * per + (self.base + self.n), 0

    def leave(self, count):
        start, per = self.saved
        assert self.n == per, (self.n, per)
        self.base, self.n = start + count * per, 0


def layer(nc, a, out):
    ctx = ExitStack()
    with ctx:
        def sb(name, shape, dt=F32):
            return ctx.enter_context(nc.sbuf_tensor(name, shape, dt))

        def sem(name):
            return ctx.enter_context(nc.semaphore(name))

        k_parts = nc.dram_tensor("k_parts", [3, D, M], BF16, kind="Internal").ap()
        q_parts = nc.dram_tensor("q_parts", [3, D, T], BF16, kind="Internal").ap()
        x_rows = nc.dram_tensor("x_rows", [T, 2 * D], F32, kind="Internal").ap()
        out_rows = out.rearrange("b t n -> (b t) n")

        res = sb("res", [P, NT, D])
        w1e = sb("w1e", [P, KD * E * F])
        arena = sb("arena", [P, 16384])
        duo = sb("duo", [P, 4096 + 2048])
        pbuf = sb("pbuf", [P, 4, 1024])
        vbuf = sb("vbuf", [P, 3584])
        ident = sb("ident", [P, P])
        ones = sb("ones", [P, P])
        tri = sb("tri", [P, P])
        cols = sb("cols", [P, 13])
        rows = sb("rows", [P, 2 * D + E])
        b1c = sb("b1c", [P, E * NF])
        lane = sb("lane", [P, P])[:, :]
        w1_x = sb("w1_x", [P, KD, F1])
        wr = sb("wr", [P, KD, E])
        inv_w = sb("inv_w", [P, 2])
        bqk = sb("bqk", [P, 2])
        half_pi = sb("half_pi", [P, 1])
        ksum = sb("ksum", [P, KD, 4])
        kneg = sb("kneg", [P, KD])
        stats = sb("stats", [P, TPC, 6])
        mv = sb("mv", [P, TPC, 2])
        rstd = sb("rstd", [P, TPC])
        nt1 = sb("nt1", [P, TPC])
        nv = sb("nv", [P, TPC])
        rden_x = sb("rden_x", [P, TPC, G])
        rmin = sb("rmin", [P, TPC, G])
        small = sb("small", [P, 2])
        again = sb("again", [P, 1], I32)

        yT = w1e[0:YC, 0:2 * M].rearrange("p (c m) -> p c m", c=2)
        wk_x = w1e[0:YC, 3328:3840].rearrange("p (c n) -> p c n", c=2)
        wv_x = w1e[0:YC, 3840:4352].rearrange("p (c n) -> p c n", c=2)
        wqkv = w1e[:, 4352:5120].rearrange("p (w c n) -> p w c n", w=3, c=KD)
        bo_b = w1e[:, 9984:10240]
        wq_x = w1e[:, 15360:15872].rearrange("p (c n) -> p c n", c=KD)
        wo_s = w1e[:, 15872:16128]
        k_bf = w1e[:, 5120:5120 + 4864].bitcast(BF16)[:, 0:3 * KD * M].rearrange("p (j c m) -> p j c m", j=3, c=KD)
        xo = duo[:, 0:4096].rearrange("p (t n) -> p t n", t=NT)
        kf = duo[:, 0:KD * M].rearrange("p (c m) -> p c m", c=KD)
        w1s = [duo[:, 2048 * b:2048 * b + 2048].rearrange("p (k n) -> p k n", k=KD) for b in range(2)]
        xT = [duo[:, 4096 + 1024 * b:5120 + 1024 * b].rearrange("p (k t) -> p k t", k=KD) for b in range(2)]
        sc_hi = [arena[:, 4096 * w:4096 * w + 2048].bitcast(F16).rearrange("p (c t) -> p c t", c=2) for w in range(2)]
        sc_lo = [arena[:, 4096 * w + 2048:4096 * w + 4096].bitcast(BF16).rearrange("p (c t) -> p c t", c=2) for w in range(2)]
        v_s = arena[:, 8192:10240].rearrange("p (t n) -> p t n", t=NT)
        aT = arena[:, 10240:10752]
        o_raw = arena[:, 10752:11264]
        th, tn = ([arena[:, c:c + 1024].rearrange("p (w n) -> p w n", w=2) for c in places] for places in ((11264, 14336), (12288, 10240)))
        acc0 = w1e[:, 12420:13444]
        stats_late, mv_late = (w1e[:, c:c + 2 * TPC * n].rearrange("p (t n) -> p t n", n=n) for c, n in ((13508, 6), (13556, 2)))
        rstd_late, nt_late, nv_late = (w1e[:, c:c + 2 * TPC] for c in (13572, 13580, 13588))
        acc = arena[:, 11264:12288]
        last_xT = acc.rearrange("p (k t) -> p k t", k=KD)
        acc1 = arena[:, 12288:12800]
        rden = arena[:, 12800:13312]
        turns = arena[:, 13312:13824]
        xn2 = arena[:, 13312:14336].rearrange("p (t n) -> p t n", t=TPC)
        qf = arena[:, 14336:15360].rearrange("p (c n) -> p c n", c=KD)
        w2_x = arena[:, 15360:16384].rearrange("p (f n) -> p f n", f=NF1)
        q_bf = w1e[:, 13824:13824 + 1536].bitcast(BF16).rearrange("p (j c n) -> p j c n", j=3, c=KD)

        def stack(base, width):
            return base[0:RS].bitcast(BF16).rearrange("p (h n) -> p h n", h=G)[:, :, 0:width]

        qst = [stack(w1e[:, 8324:12420], T), stack(arena[:, 4096:8192], T), stack(arena[:, 0:4096], T), stack(arena[:, 4096:8192], T)]
        kst = [stack(w1e[:, 5120:8322], M), stack(arena[:, 11396:14598], M), stack(arena[:, 8192:11394], M), stack(arena[:, 11396:14598], M)]
        gp = pbuf[:, :, :].rearrange("p a n -> p (a n)")[:, 0:M]
        gpT = pbuf[:, 2:4, :].rearrange("p a n -> p (a n)")[:, 0:MT * P].rearrange("p (t n) -> p t n", n=P)
        gq, gk = qst[2][:, 0, :], kst[2][:, 0, :]

        def p_slot(i):
            return pbuf[:, i % 4, :] if i < 2 * MT - 2 else duo[:, 4096 + 1024 * (i % 2):5120 + 1024 * (i % 2)]

        oT = [w1e[:, 12420:12420 + QC]] + [arena[:, 14848:14848 + QC]] * (NG - 1)
        w2e = arena[:, :].rearrange("p (e n) -> p e n", e=E)
        w1v = w1e[:, :].rearrange("p (k n) -> p k n", k=KD)
        xn1 = w1e[:, 5120:9216].rearrange("p (t n) -> p t n", n=D)
        xn = pbuf[:, :, :].rearrange("p a (t n) -> p (a t) n", n=D)
        hT = [pbuf[:, 2 + b, :].rearrange("p (f n) -> p f n", f=NF) for b in range(2)]
        vx = vbuf[:, 0:MT * NH * VW].rearrange("p (t n) -> p t n", t=MT)
        h_x = vbuf[:, 0:NF1 * QC].rearrange("p (f n) -> p f n", f=NF1)
        xn3T = vbuf[:, 2048:3072].rearrange("p (k n) -> p k n", k=KD)
        xgT = [vbuf[:, 2560 + 256 * b:2816 + 256 * b].rearrange("p (k n) -> p k n", k=KD) for b in range(2)]
        flat = res[:, :, :].rearrange("p t n -> p (t n)")
        b2e = flat[:, 0:E * D]
        xg = [flat[:, 2048 + 512 * b:2560 + 512 * b] for b in range(2)]
        rs = [flat[:, 3072 + D * b:3072 + D * b + D] for b in range(2)]
        ys = [flat[:, 3584 + D * b:3584 + D * b + D] for b in range(2)]
        RV = 3072
        l2, oneh = [vbuf[:, RV + P * i:RV + P * i + P].rearrange("p (t e) -> p t e", e=E) for i in range(2)]
        base = vbuf[:, RV + 256:RV + 392].rearrange("p (t e) -> p t e", e=E)
        lg = vbuf[:, RV + 392:RV + 424].rearrange("p (t e) -> p t e", e=E)
        tile_i, bl_i = vbuf[:, RV + 424:RV + 440], vbuf[:, RV + 440:RV + 464]
        cum = [vbuf[:, RV + 464 + 12 * i:RV + 476 + 12 * i] for i in range(2)]
        nb, pad_row, own_row, lmax = vbuf[:, RV + 488:RV + 496], vbuf[:, RV + 496:RV + 497], vbuf[:, RV + 497:RV + 498], vbuf[:, RV + 500:RV + 504]
        in_block = pbuf[:, 0, :].bitcast(BF16).rearrange("p (t n) -> p t n", n=P)
        to_block, gate_to = (vbuf[:, 576 * i:576 * i + 576].bitcast(BF16).rearrange("p (t w b) -> p t w b", w=3, b=24) for i in range(2))
        prod = vbuf[:, 1152:1152 + NT * E].rearrange("p (t e) -> p t e", e=E)
        bl_c = vbuf[:, 1280:1280 + 24 * E].rearrange("p (b e) -> p b e", e=E)
        probs = vbuf[:, 1472:1472 + NT * E].rearrange("p (t e) -> p t e", e=E)
        bl_f = vbuf[:, 1600:1624]
        gate_parts = vbuf[:, 1640:1664].bitcast(BF16).rearrange("p (j t) -> p j t", j=3)
        bl_t = vbuf[:, 1712:1736]
        filled_f, token_f = vbuf[:, 1664:1688], vbuf[:, 1688:1712]
        revi = sb("revi", [P, E])
        gate = sb("gate", [P, NT])
        top = sb("top", [P, TPC])
        top_all = vbuf[:, 1624:1640]
        rank = sb("rank", [P, NT])
        full = sb("full", [P, NT])
        after = lambda i, n: duo[:, 4096 + 24 * i:4096 + 24 * i + n]
        token_in = after(0, 24).bitcast(U32)
        token_out = after(1, 24).bitcast(U32)
        slot_gate = after(2, 24)
        bl_e = after(3, 24).bitcast(I32)
        gate_b, spare = after(4, 1), after(6, 1)
        b1b = [after(7 + b, NF) for b in range(2)]
        n_blocks = after(5, 1).bitcast(I32)[0:1, :]

        psum = ctx.enter_context(nc.psum_tensor("psum", [P, 8, 512], F32))

        ld_y = sem("ld_y"); ld_small = sem("ld_small"); ld_x = [sem(f"ld_x{q}") for q in range(NQ)]
        ld_ws = sem("ld_ws"); ld_wqkv = sem("ld_wqkv"); ld_w1e = sem("ld_w1e"); ld_w2e = sem("ld_w2e"); ld_b2e = sem("ld_b2e")
        consts = sem("consts"); late_consts = sem("late_consts")
        dve_own = sem("dve_own"); pool_own = sem("pool_own"); act_own = sem("act_own")
        k_proj = sem("k_proj"); k_evac = sem("k_evac"); k_split = sem("k_split"); k_stored = sem("k_stored")
        v_proj = sem("v_proj"); v_evac = sem("v_evac"); o_clear = sem("o_clear")
        col_ok = sem("col_ok"); xn_ok = sem("xn_ok"); norm_ok = sem("norm_ok"); xn_T = sem("xn_T"); xT_ok = sem("xT_ok")
        qkv_mm = sem("qkv_mm"); th_ok = sem("th_ok"); lo_ok = sem("lo_ok"); abs_ok = sem("abs_ok"); v_ok = sem("v_ok"); ones_ok = sem("ones_ok"); ang_ok = sem("ang_ok"); sc_ok = sem("sc_ok")
        bo_added = sem("bo_added")
        s_mm = sem("s_mm"); s_exp = sem("s_exp"); s_pv = sem("s_pv"); s_acc = sem("s_acc"); o_evac = sem("o_evac")
        acc_ok = sem("acc_ok"); den_mm = sem("den_mm"); aT_ok = sem("aT_ok"); wo_mm = sem("wo_mm")
        res_half = sem("res_half"); xn2_ok = sem("xn2_ok"); xn2_T = sem("xn2_T"); x2T_ok = sem("x2T_ok"); q_mm = sem("q_mm"); q_ok = sem("q_ok")
        q_split = sem("q_split"); q_stored = sem("q_stored")
        st_k0 = sem("st_k0"); st_q0 = sem("st_q0"); st_ld = [sem(f"st_ld{g}") for g in range(NG)]
        c_mm = sem("c_mm"); c_exp = sem("c_exp"); c_pv = sem("c_pv"); c_evac = sem("c_evac"); c_tr = sem("c_tr"); c_xo = sem("c_xo")
        bad_ok = sem("bad_ok"); bad_mm = sem("bad_mm"); flag_ok = sem("flag_ok")
        m_ld = sem("m_ld"); m_mm = sem("m_mm"); m_max = sem("m_max"); m_exp = sem("m_exp"); m_tr = sem("m_tr")
        m_pT = sem("m_pT"); m_pv = sem("m_pv"); m_out = sem("m_out"); m_red = sem("m_red")
        b2_added = sem("b2_added")
        f_tr = sem("f_tr"); f_xT = sem("f_xT"); f_h = sem("f_h"); f_relu = sem("f_relu"); f_y = sem("f_y"); f_res = sem("f_res")
        xn3_ok = sem("xn3_ok"); r_tr = sem("r_tr"); r_xT = sem("r_xT"); r_lg = sem("r_lg")
        r_sub = sem("r_sub"); r_exp = sem("r_exp"); r_one = sem("r_one"); r_rank = sem("r_rank"); r_used = sem("r_used"); r_blk = sem("r_blk")
        r_to = sem("r_to"); r_table = sem("r_table"); r_slots = sem("r_slots"); row_st = [sem(f"row_st{q}") for q in range(NQ)]
        g_ld = [sem(f"g_ld{b}") for b in range(2)]; g_tr = sem("g_tr"); g_xT = sem("g_xT"); g_h = sem("g_h")
        g_w = sem("g_w"); g_b1 = sem("g_b1"); g_act = sem("g_act"); g_y = sem("g_y"); g_ys = sem("g_ys")
        g_st = [sem(f"g_st{b}") for b in range(2)]
        g_rs = sem("g_rs"); g_sum = sem("g_sum"); g_gate = sem("g_gate")

        block = ctx.enter_context(nc.Block())
        DEN, WO, TURN, QUERIES = (0,), (3, 4), (8, 9), (10, 11)
        down_bank = (7, 4)

        BQ, PH, WL, BV = 0, 1, 2, 4
        BK = 3
        XBQ, XBK, XB1 = 5, 7, 9
        b2_b, bv_b, br_b = rows[:, 0:D], rows[:, D:2 * D], rows[:, 2 * D:]

        def k_stack(eng, g, r):
            return eng.dma_start(kst[g][r * DH:(r + 1) * DH, :, :],
                                 k_parts[PARTS_K[r], g * G * DH:(g + 1) * G * DH, :].rearrange("(h d) m -> d h m", d=DH))

        @block.sync
        def _(sp):
            xv = a["x"].rearrange("b (t p) n -> p (b t) n", p=P)
            for q in range(NQ):
                sp.dma_start(res[:, q * TPC:(q + 1) * TPC, :], xv[:, q * TPC:(q + 1) * TPC, :]).then_inc(ld_x[q], 16)
                if q == 0:
                    sp.dma_start(wqkv, a["wqkv"].rearrange("w (c p) n -> p w c n", c=KD)).then_inc(ld_wqkv, 16)

            def q_stack(g, r, c0, cn, signal):
                sp.dma_start(qst[g][r * DH:(r + 1) * DH, :, c0:c0 + cn],
                             q_parts[PARTS_Q[r], g * G * DH:(g + 1) * G * DH, c0:c0 + cn].rearrange("(h d) t -> d h t", d=DH)
                             ).then_inc(signal, 16)

            for u in range(NQ):
                sp.wait_ge(q_split, u + 1)
                for j in range(3):
                    sp.dma_start(q_parts[j, :, u * QC:u * QC + QC].rearrange("(c p) t -> p c t", c=KD),
                                 q_bf[:, j]).then_inc(q_stored, 16)
                sp.wait_ge(q_stored, 48 * (u + 2))
                if u:
                    sp.wait_ge(st_q0, 96 * u)
                else:
                    sp.wait_ge(k_stored, 48)
                for r in range(6):
                    q_stack(0, r, u * QC, QC, st_q0)
            for g in range(1, NG):
                if g == 1:
                    sp.wait_ge(q_mm, 2 * NQ)
                    sp.wait_ge(q_split, NQ)
                if g == 3:
                    sp.wait_ge(c_mm, 2 * MT * NQ * 2)
                for r in range(6):
                    k_stack(sp, g, r).then_inc(st_ld[g], 16)
                    q_stack(g, r, 0, T, st_ld[g])
                if g == 2:
                    sp.wait_ge(c_mm, 2 * MT * NQ)
                    sp.wait_ge(c_tr, NQ)
                    for k in range(KD):
                        sp.dma_start(w1v[:, k, :].rearrange("p (e f) -> p e f", e=E),
                                     a["w1"][:, k * P:k * P + P, :].rearrange("e p f -> p e f")).then_inc(ld_w1e, 16)
            sp.wait_ge(flag_ok, 1)
            with sp.If(sp.value_load(again[0:1, 0:1], min_val=0, max_val=P) > 0):
                with sp.Fori(0, NH) as h:
                    sp.wait_ge(m_out, NT * h + 1)
                    for r in range(6):
                        sp.dma_start(gk[r * DH:(r + 1) * DH, :], k_parts[PARTS_K[r], ds(h * DH, DH), :]).then_inc(m_ld, 16)
                        sp.dma_start(gq[r * DH:(r + 1) * DH, :], q_parts[PARTS_Q[r], ds(h * DH, DH), :]).then_inc(m_ld, 16)
                sp.wait_ge(m_pv, NT * NH)
            sp.wait_ge(c_mm, 2 * MT * NQ * NG)
            sp.wait_ge(c_tr, NQ * NG)

            def w2(e):
                sp.dma_start(w2e[:, e, :].rearrange("p (f n) -> p f n", f=NF),
                             a["w2"][e].rearrange("(f p) n -> p f n", f=NF)).then_inc(ld_w2e, 16)

            def tokens(q):
                rows_v = x_rows.rearrange("(t p) n -> p t n", p=P)
                tiles = slice(q * TPC, (q + 1) * TPC)
                sp.wait_ge(xn3_ok, q + 1)
                sp.dma_start(rows_v[:, tiles, 0:D], xn[:, tiles, :]).then_inc(row_st[q], 16)
                sp.dma_start(rows_v[:, tiles, D:2 * D], res[:, tiles, :]).then_inc(row_st[q], 16)

            for e in range(E - 1):
                w2(e)
            for q in range(NQ - 1):
                tokens(q)
            tokens(NQ - 1)
            sp.wait_ge(f_y, 2 * NQ)
            w2(E - 1)
            for q in range(NQ):
                sp.wait_ge(row_st[q], 32)
            sp.dma_start(b2e, a["b2"].partition_broadcast(P)).then_inc(ld_b2e, 16)
            sp.wait_ge(ld_b2e, 16)

        @block.gpsimd
        def _(pool):
            ch = Chain(pool, pool_own)
            pool.memset(half_pi[:, :], math.pi / 2).then_inc(consts, 1)
            pool.memset(ones[:, :], 1.0).then_inc(consts, 1)
            ch.inc(pool.memset(ident[:, :], 0.0))
            ch.inc(pool.memset(tri[:, :], 1.0))
            ch.wait()
            pool.affine_select(out=ident[:, :], in_=ident[:, :], compare_op=ALU.not_equal, fill=1.0, base=0,
                               pattern=[[-1, P]], channel_multiplier=1).then_inc(consts, 1)
            pool.affine_select(out=tri[:, :], in_=tri[:, :], compare_op=ALU.is_gt, fill=0.0, base=0,
                               pattern=[[1, P]], channel_multiplier=-1).then_inc(consts, 1)

            def low_parts(q):
                for w in range(2):
                    for c, src in ((1, th[q % 2]), (0, tn[q % 2])):
                        pool.wait_ge(sc_ok, 4 * q + 2 * w + 2 - c)
                        pool.tensor_tensor(sc_lo[w][:, c, q * QC:q * QC + QC], src[:, w], sc_hi[w][:, c, q * QC:q * QC + QC],
                                           ALU.subtract).then_inc(lo_ok, 1)

            def add_bo(q):
                pool.wait_ge(xn_ok, q + 1)
                r = res[:, q * TPC:(q + 1) * TPC, :]
                pool.tensor_tensor(r, r, bo_b.unsqueeze(1).to_broadcast([P, TPC, D]), ALU.add).then_inc(bo_added, 1)

            for q in range(NQ):
                low_parts(q)
            pool.wait_ge(ld_small, 64)
            for q in range(NQ):
                add_bo(q)

            pool.wait_ge(k_evac, 2 * len(KCH))
            ch.link(pool.tensor_tensor(ksum[:, :, 0:2], ksum[:, :, 0:2], ksum[:, :, 2:4], ALU.add))
            ch.link(pool.tensor_tensor(ksum[:, :, 0:1], ksum[:, :, 0:1], ksum[:, :, 1:2], ALU.add))
            ch.link(pool.tensor_scalar(kneg[:, :], ksum[:, :, 0], -1.0 / M, None, ALU.mult))
            for c in range(KD):
                ch.inc(pool.tensor_scalar(kf[:, c], kf[:, c], kneg[:, c:c + 1], None, ALU.add))
            ch.wait()
            pool.wait_ge(xn_T, 2 * NQ)
            ch.link(pool.tensor_copy(k_bf[:, 0], kf[:, :, :]))
            ch.link(pool.tensor_tensor(kf, kf, k_bf[:, 0], ALU.subtract))
            ch.link(pool.tensor_copy(k_bf[:, 1], kf))
            ch.link(pool.tensor_tensor(kf, kf, k_bf[:, 1], ALU.subtract))
            pool.tensor_copy(k_bf[:, 2], kf).then_inc(k_split, 1)

            pool.wait_ge(k_split, 1)
            for j in range(3):
                pool.dma_start(k_parts[j].rearrange("(c p) m -> p c m", c=KD), k_bf[:, j]).then_inc(k_stored, 16)
            pool.wait_ge(k_stored, 48)
            for r in range(6):
                k_stack(pool, 0, r).then_inc(st_k0, 16)

            pool.wait_ge(q_ok, 2 * NQ)
            pool.wait_ge(q_stored, 48 * NQ)
            ch.link(pool.tensor_copy(q_bf[:, 0], qf))
            ch.link(pool.tensor_tensor(qf, qf, q_bf[:, 0], ALU.subtract))
            ch.link(pool.tensor_copy(q_bf[:, 1], qf))
            ch.link(pool.tensor_tensor(qf, qf, q_bf[:, 1], ALU.subtract))
            pool.tensor_copy(q_bf[:, 2], qf).then_inc(q_split, 1)

            pool.wait_ge(xn2_ok, NQ)
            pool.tensor_tensor(res[:, :, :], res[:, :, :], b2_b.unsqueeze(1).to_broadcast([P, NT, D]), ALU.add).then_inc(b2_added, 1)

            pool.wait_ge(f_h, 1)
            for dst, pattern, first, per_row in ((revi[:, :], [[-1, E]], E, 0), (bl_i, [[1, 24]], 0, 0), (tile_i, [[1, NT]], 0, 0),
                                                 (lane, [[1, P]], 0, 0), (pad_row, [[1, 1]], T, 1), (own_row, [[1, 1]], 0, 1)):
                pool.iota(dst, pattern, base=first, channel_multiplier=per_row,
                          allow_small_or_imprecise_dtypes=True).then_inc(late_consts, 1)

            def gather(b, j):
                pool.indirect_dma_start(out=xg[j], out_offset=None, in_=x_rows[:, :],
                                        in_offset=bass.IndirectOffsetOnAxis(ap=token_in[:, b:b + 1], axis=0)).then_inc(g_ld[j], 16)

            def scatter(b, j):
                pool.wait_ge(g_ys, b + 1)
                pool.indirect_dma_start(out=out_rows, out_offset=bass.IndirectOffsetOnAxis(ap=token_out[:, b:b + 1], axis=0),
                                        in_=ys[j], in_offset=None, bounds_check=T - 1, oob_is_err=False).then_inc(g_st[j], 16)

            def gather_next(b, j):
                pool.wait_ge(g_tr, b - 1)
                pool.wait_ge(g_rs, b - 1)
                gather(b, j)

            for q in range(NQ):
                pool.wait_ge(row_st[q], 32)
            pool.wait_ge(r_slots, 1)
            gather(0, 0)
            gather(1, 1)
            gather_next(2, 0)
            gather_next(3, 1)
            pool.wait_ge(r_slots, 3)
            for b in range(NB_LOOP):
                scatter(b, b % 2)
                if b + 4 < NB:
                    gather_next(b + 4, b % 2)
            filled = pool.value_load(n_blocks, min_val=0, max_val=NB)
            for blocks in NB_TAIL:
                with pool.If(filled > blocks[0]):
                    for b in blocks:
                        scatter(b, b % 2)
                        if b + 4 < NB:
                            gather_next(b + 4, b % 2)
                    for b in blocks:
                        pool.wait_ge(g_st[b % 2], 16 * (b // 2 + 1))
                        if b + 4 < NB:
                            pool.wait_ge(g_ld[b % 2], 16 * ((b + 4) // 2 + 1))
            for j in range(2):
                pool.wait_ge(g_st[j], 16 * (NB_LOOP // 2))
                pool.wait_ge(g_ld[j], 16 * ((NB_LOOP + 4) // 2))

        @block.tensor
        def _(pe):
            def bank(i, n=512, p=P):
                return psum[0:p, i, 0:n]

            turn_banks = [(5, 6), (0, 1), (5, 6), (5, 6)]
            qkv_banks = [(7, 5, 6), (2, 3, 4), (7, 5, 6), (7, 5, 6)]

            def turn_x(q):
                pe.wait_ge(xn_ok, q + 1)
                if q >= 2:
                    before = 0 if q == 2 else 2
                    pe.wait_ge(th_ok, 2 * before + 2)
                    pe.wait_ge(v_ok, before + 1)
                for k in range(KD):
                    for t in range(TPC):
                        mm = pe.transpose(psum[:, turn_banks[q][k], t * P:t * P + P], xn1[:, q * TPC + t, k * P:k * P + P], ident[:, :])
                    mm.then_inc(xn_T, 1)

            def qkv(q):
                pe.wait_ge(xT_ok, 2 * q + 2)
                for w in range(2):
                    for k in range(KD):
                        mm = pe.matmul(bank(qkv_banks[q][w]), wqkv[:, w, k, :], xT[q % 2][:, k, :], start=(k == 0), stop=(k == KD - 1))
                    mm.then_inc(qkv_mm, 1)
                for t in range(TPC):
                    for k in range(KD):
                        mm = pe.matmul(psum[:, qkv_banks[q][2], t * P:t * P + P], xT[q % 2][:, k, t * P:t * P + P], wqkv[:, 2, k, :],
                                       start=(k == 0), stop=(k == KD - 1))
                mm.then_inc(qkv_mm, 1)

            def cross_keys(i):
                j, c = i // KD, i % KD
                m0, mn = KCH[j]
                if i == 0:
                    pe.wait_ge(ld_y, 48)
                    pe.wait_ge(th_ok, 2 * NQ)
                    pe.wait_ge(v_ok, NQ)
                if i >= 3:
                    pe.wait_ge(k_evac, i - 2)
                for y in range(2):
                    mm = pe.matmul(bank(5 + i % 3, mn), wk_x[:, y, c * P:c * P + P], yT[:, y, m0:m0 + mn], start=(y == 0), stop=(y == 1))
                mm.then_inc(k_proj, 1)

            def cross_values(t):
                n = P if t < MT - 1 else MLAST
                if t == 0:
                    pe.wait_ge(k_evac, 2 * len(KCH))
                if t >= 3:
                    pe.wait_ge(v_evac, t - 2)
                for y in range(2):
                    mm = pe.matmul(bank(5 + t % 3, D, n), yT[:, y, t * P:t * P + n], wv_x[:, y, :], start=(y == 0), stop=(y == 1))
                mm.then_inc(v_proj, 1)

            def scores(u, i):
                n = S_PAIRS * u + i
                if not (isinstance(u, int) and n < 2):
                    pe.wait_ge(s_exp, n - 1)
                if isinstance(u, int) and i % 2 == 0:
                    pe.wait_ge(lo_ok, 4 * (i // 2 + 1))
                for h in range(2):
                    kt = 2 * i + h
                    passes = [(k_, q_, c) for k_, q_ in ((sc_hi, sc_hi), (sc_hi, sc_lo), (sc_lo, sc_hi)) for c in range(2)]
                    for n_, (k_, q_, c) in enumerate(passes):
                        mm = pe.matmul(bank(2 * (i % 2) + h), k_[1][:, c, kt * P:kt * P + P], q_[0][:, c, ds(u * QC, QC)],
                                       start=(n_ == 0), stop=(n_ == len(passes) - 1))
                mm.then_inc(s_mm, 1)

            def pv(u, i):
                n = S_PAIRS * u + i
                pe.wait_ge(s_exp, n + 1)
                if isinstance(u, int) and u == 0 and i % 2 == 0:
                    pe.wait_ge(v_ok, max(i // 2 + 1, 2))
                if i == 0 and not (isinstance(u, int) and u == 0):
                    pe.wait_ge(o_evac, u)
                for h in range(2):
                    kt = 2 * i + h
                    mm = pe.matmul(bank(4), v_s[:, kt, :], pbuf[:, i % 4, h * QC:h * QC + QC], start=(kt == 0), stop=(kt == NT - 1))
                mm.then_inc(s_pv, 1)

            def tail_den(u):
                pe.wait_ge(acc_ok, u + 1)
                pe.matmul(bank(7), ones[:, :], acc1, start=True, stop=True).then_inc(den_mm, 1)

            def tail_wo(u):
                pe.wait_ge(aT_ok, u + 1)
                for t in range(TPC):
                    mm = pe.matmul(psum[:, 6 + t // 2, (t % 2) * D:(t % 2) * D + D], aT[:, t * P:t * P + P], wo_s, start=True, stop=True)
                mm.then_inc(wo_mm, 1)

            def tail_turn(u):
                pe.wait_ge(xn2_ok, u + 1)
                for k in range(KD):
                    for t in range(TPC):
                        mm = pe.transpose(psum[:, 6 + k, t * P:t * P + P], xn2[:, t, k * P:k * P + P], ident[:, :])
                    mm.then_inc(xn2_T, 1)

            def tail_q(u):
                pe.wait_ge(x2T_ok, 2 * u + 2)
                for c in range(KD):
                    for k in range(KD):
                        mm = pe.matmul(bank(5 + c), wq_x[:, k, c * P:c * P + P], xT[0][:, k, :], start=(k == 0), stop=(k == KD - 1))
                    mm.then_inc(q_mm, 1)

            def last_wo(h):
                if h:
                    pe.wait_ge(res_half, 1)
                else:
                    pe.wait_ge(aT_ok, NQ)
                for t in (2 * h, 2 * h + 1):
                    mm = pe.matmul(psum[:, 7, (t % 2) * D:(t % 2) * D + D], aT[:, t * P:t * P + P], wo_s, start=True, stop=True)
                mm.then_inc(wo_mm, 1)

            def last_turn(k):
                if k:
                    pe.wait_ge(x2T_ok, 2 * NQ - 1)
                else:
                    pe.wait_ge(xn2_ok, NQ)
                for t in range(TPC):
                    mm = pe.transpose(psum[:, 7, t * P:t * P + P], xn2[:, t, k * P:k * P + P], ident[:, :])
                mm.then_inc(xn2_T, 1)

            def last_q(c):
                pe.wait_ge(x2T_ok, 2 * NQ)
                if c:
                    pe.wait_ge(q_ok, 2 * NQ - 1)
                for k in range(KD):
                    mm = pe.matmul(bank(7), wq_x[:, k, c * P:c * P + P], last_xT[:, k, :], start=(k == 0), stop=(k == KD - 1))
                mm.then_inc(q_mm, 1)

            def self_unit(u):
                for i in range(S_PAIRS):
                    scores(u, i)
                    if i:
                        pv(u, i - 1)
                    else:
                        pv(u - 1, S_PAIRS - 1)
                    if i == 1:
                        tail_den(u - 1)
                    if i == 3:
                        tail_wo(u - 1)
                    if i == 5:
                        tail_turn(u - 1)
                    if i == 6:
                        tail_q(u - 1)

            pe.wait_ge(consts, 4)
            pe.wait_ge(ld_wqkv, 16)
            for q in range(2):
                turn_x(q)
                qkv(q)
            pe.wait_ge(xT_ok, 4)
            for i in range(S_PAIRS):
                if i == 1:
                    pe.wait_ge(th_ok, 4)
                scores(0, i)
                if i == 0:
                    turn_x(2)
                if i == 3:
                    pv(0, 2)
                    qkv(3)
                elif i:
                    pv(0, i - 1)
                if i == 1:
                    qkv(2)
                if i == 2:
                    turn_x(3)
                if i >= 5:
                    cross_keys(2 * (i - 5))
                    cross_keys(2 * (i - 5) + 1)
            cross_keys(6)
            cross_keys(7)
            for t in range(MT):
                cross_values(t)
            pe.wait_ge(v_evac, MT)
            pe.wait_ge(ld_ws, 80)
            with pe.Fori(1, NQ) as u:
                self_unit(u)
            pv(NQ - 1, S_PAIRS - 1)
            def c_scores(u, g, qc, t, hf):
                n = P if t < MT - 1 else MLAST
                i = 2 * t + hf
                if isinstance(u, int) and u == 0 and i == 2:
                    pe.wait_ge(o_evac, NQ)
                if i >= 3:
                    pe.wait_ge(c_exp, 2 * MT * u + i - 2)
                elif not (isinstance(u, int) and u == 0):
                    pe.wait_ge(c_exp, 2 * MT * u - (2 * MT - 1 - [24, 25, 23][i]))
                for h in range(2):
                    hh = 2 * hf + h
                    mm = pe.matmul(bank(2 * (i % 3) + h, QC, n), kst[g][:, hh, t * P:t * P + n], qst[g][:, hh, ds(qc * QC, QC)],
                                   start=True, stop=True)
                mm.then_inc(c_mm, 1)

            def c_values(u, g, t):
                n = P if t < MT - 1 else MLAST
                pe.wait_ge(c_exp, 2 * MT * u + 2 * t + 2)
                if t == 0 and isinstance(u, int) and u == 0:
                    pe.wait_ge(o_clear, 1)
                elif t == 0:
                    pe.wait_ge(c_evac, u)
                for h in range(G):
                    hh = g * G + h
                    mm = pe.matmul(psum[32 * h:32 * h + VW, 6, :], vx[0:n, t, hh * VW:(hh + 1) * VW],
                                   p_slot(2 * t + h // 2)[0:n, (h % 2) * QC:(h % 2) * QC + QC], start=(t == 0), stop=(t == MT - 1),
                                   tile_position=(0, 32 * h))
                mm.then_inc(c_pv, 1)

            def c_turn(u, g):
                pe.wait_ge(c_evac, u + 1)
                if not (isinstance(u, int) and u == 0):
                    pe.wait_ge(c_xo, u)
                for t in range(TPC):
                    mm = pe.transpose(psum[:, 7, t * P:t * P + P], oT[g][:, t * P:t * P + P], ident[:, :])
                mm.then_inc(c_tr, 1)

            def cross_unit(u, g, qc, first):
                g_before = g if not isinstance(qc, int) else g - 1
                for t in range(MT):
                    if t == 0 and not first:
                        c_values(u - 1, g_before, MT - 2)
                    c_scores(u, g, qc, t, 0)
                    if t >= 2:
                        c_values(u, g, t - 2)
                    elif t == 1 and not first:
                        c_values(u - 1, g_before, MT - 1)
                    c_scores(u, g, qc, t, 1)
                    if t == 3 and not first:
                        c_turn(u - 1, g_before)
                    if first:
                        last_tail(t)

            def last_tail(t):
                if t in DEN:
                    tail_den(NQ - 1)
                for step, places in ((last_wo, WO), (last_turn, TURN), (last_q, QUERIES)):
                    if t in places:
                        step(places.index(t))

            pe.wait_ge(st_k0, 96)
            pe.wait_ge(st_q0, 96)
            pe.wait_ge(s_exp, S_PAIRS * NQ)
            cross_unit(0, 0, 0, True)
            last_tail(MT)
            pe.wait_ge(q_ok, 2 * NQ)
            with pe.Fori(1, NQ) as qc:
                pe.wait_ge(st_q0, 96 * qc + 96)
                cross_unit(qc, 0, qc, False)
            for g in range(1, NG):
                pe.wait_ge(st_ld[g], 12 * 16)
                cross_unit(NQ * g, g, 0, False)
                with pe.Fori(1, NQ) as qc:
                    cross_unit(qc + NQ * g, g, qc, False)
            c_values(NQ * NG - 1, NG - 1, MT - 2)
            c_values(NQ * NG - 1, NG - 1, MT - 1)
            c_turn(NQ * NG - 1, NG - 1)

            pe.wait_ge(bad_ok, 1)
            pe.matmul(psum[:, 7, 0:1], ones[:, :], small[:, 0:1], start=True, stop=True).then_inc(bad_mm, 1)
            pe.wait_ge(flag_ok, 1)
            with pe.If(pe.value_load(again[0:1, 0:1], min_val=0, max_val=P) > 0):
                with pe.Fori(0, NH) as h:
                    with pe.Fori(0, NT) as t:
                        i = h * NT + t
                        pe.wait_ge(m_ld, 12 * 16 * (h + 1))
                        pe.wait_ge(m_out, i + 1)
                        for c, (m0, mn) in enumerate(KCH):
                            mm = pe.matmul(bank(c, 401), gq[:, ds(t * P, P)], gk[:, m0:m0 + 401], start=True, stop=True)
                        mm.then_inc(m_mm, 1)
                        pe.wait_ge(m_exp, 2 * i + 2)
                        for k in range(MT):
                            n = P if k < MT - 1 else MLAST
                            mm = pe.transpose(psum[0:n, 4 + k // 4, (k % 4) * P:(k % 4) * P + P], gp[:, k * P:k * P + n], ident[:, :])
                        mm.then_inc(m_tr, 1)
                        pe.wait_ge(m_pT, 2 * i + 2)
                        for k in range(MT):
                            n = P if k < MT - 1 else MLAST
                            mm = pe.matmul(psum[:, 0, 0:VW], gpT[0:n, k, :], vx[0:n, k, ds(h * VW, VW)], start=(k == 0), stop=(k == MT - 1))
                        mm.then_inc(m_pv, 1)
                pe.wait_ge(m_out, NT * NH + 1)

            def f_turn(q):
                if q == 0:
                    pe.wait_ge(c_exp, 2 * MT * NQ * NG)
                    pe.wait_ge(c_xo, NQ * NG)
                for k in range(KD):
                    if q >= 2:
                        pe.wait_ge(r_xT, 2 * (q - 2) + k + 1)
                    elif q:
                        pe.wait_ge(f_xT, k + 1)
                    for t in range(TPC):
                        mm = pe.transpose(bank(k)[:, t * P:t * P + P], xo[:, q * TPC + t, k * P:k * P + P], ident[:, :])
                    mm.then_inc(f_tr, 1)

            def f_up(q):
                pe.wait_ge(f_xT, 2 * q + 2)
                for f in range(NF1):
                    i = NF1 * q + f
                    if i >= 3:
                        pe.wait_ge(f_relu, i - 2)
                    for k in range(KD):
                        mm = pe.matmul(bank(2 + i % 3), w1_x[:, k, f * P:f * P + P], xT[q % 2][:, k, :], start=(k == 0), stop=(k == KD - 1))
                    mm.then_inc(f_h, 1)

            def f_down(q):
                pe.wait_ge(f_relu, NF1 * (q + 1))
                for t in range(TPC):
                    if q and t % 2 == 0:
                        pe.wait_ge(f_res, 2 * (q - 1) + t // 2 + 1)
                    for f in range(NF1):
                        mm = pe.matmul(psum[:, 6 + t // 2, (t % 2) * D:(t % 2) * D + D], h_x[:, f, t * P:t * P + P], w2_x[:, f, :],
                                       start=(f == 0), stop=(f == NF1 - 1))
                    if t % 2:
                        mm.then_inc(f_y, 1)
                    if q == NQ - 1 and t == 2:
                        f_rank(NQ - 2)

            def f_turn3(q):
                pe.wait_ge(xn3_ok, q + 1)
                for k in range(KD):
                    for t in range(TPC):
                        mm = pe.transpose(bank(k)[:, t * P:t * P + P], xn[:, q * TPC + t, k * P:k * P + P], ident[:, :])
                    mm.then_inc(r_tr, 1)

            def f_logits(q):
                pe.wait_ge(r_xT, 2 * q + 2)
                if q:
                    pe.wait_ge(r_one, q)
                    if q > 1:
                        pe.wait_ge(r_used, q if q == NQ - 1 else q - 1)
                for t in range(TPC):
                    for k in range(KD):
                        mm = pe.matmul(psum[:, 5, (q * TPC + t) * E:(q * TPC + t + 1) * E], xn3T[:, k, t * P:t * P + P], wr[:, k, :],
                                       start=(k == 0), stop=(k == KD - 1))
                    mm.then_inc(r_lg, 1)

            def f_rank(q):
                pe.wait_ge(r_one, q + 1)
                if q:
                    pe.wait_ge(r_used, q)
                o_q = oneh[:, q * TPC:(q + 1) * TPC, :].rearrange("p t e -> p (t e)")
                pe.matmul(psum[:, 5, P:P + TPC * E], tri[:, :], o_q, start=True, stop=True)
                pe.matmul(psum[:, 5, P + TPC * E:P + 2 * TPC * E], ones[:, :], o_q, start=True, stop=True).then_inc(r_rank, 1)

            f_turn(0)
            for q in range(NQ):
                f_up(q)
                if q:
                    f_turn3(q - 1)
                if q == NQ - 1:
                    f_logits(q - 1)
                    f_rank(q - 2)
                f_down(q)
                if q + 1 < NQ:
                    f_turn(q + 1)
                    if q:
                        f_logits(q - 1)
                    if q >= 2:
                        f_rank(q - 2)
            f_turn3(NQ - 1)
            f_logits(NQ - 1)
            f_rank(NQ - 1)

            def table(i, dst, values):
                pe.wait_ge(r_to, 3 * (i + 1))
                for t in range(NT):
                    mm = pe.matmul(dst, in_block[:, t, :], values[:, t, :, :].rearrange("p w b -> p (w b)"),
                                   start=(t == 0), stop=(t == NT - 1))
                mm.then_inc(r_table, 1)

            table(0, psum[:, 7, 0:72], to_block)

            def expert(b):
                return pe.value_load(bl_e[0:1, ds(b, 1)], min_val=0, max_val=E - 1)

            def g_turn(b, j, half):
                pe.wait_ge(g_ld[j], 16 * (half + 1))
                if not (isinstance(b, int) and b == 0):
                    pe.wait_ge(g_xT, b)
                for k in range(KD):
                    mm = pe.transpose(psum[:, 6, k * P:k * P + P], xg[j][:, k * P:k * P + P], ident[:, :])
                mm.then_inc(g_tr, 1)

            def g_up(b, j):
                pe.wait_ge(g_xT, b + 1)
                pe.wait_ge(g_w, b + 1)
                if not (isinstance(b, int) and b < 2):
                    pe.wait_ge(g_act, b - 1)
                for f in range(NF):
                    for k in range(KD):
                        mm = pe.matmul(psum[:, 2 * j + f // 4, (f % 4) * P:(f % 4) * P + P], w1s[j][:, k, f * P:f * P + P], xgT[j][:, k, :],
                                       start=(k == 0), stop=(k == KD - 1))
                mm.then_inc(g_h, 1)

            def g_down(b, j):
                e = expert(b)
                pe.wait_ge(g_act, b + 1)
                if not (isinstance(b, int) and b < 2):
                    pe.wait_ge(g_sum, b - 1)
                for f in range(NF):
                    mm = pe.matmul(bank(down_bank[j], D), hT[j][:, f, :], arena[:, ds(e * (NF * D) + f * D, D)], start=(f == 0), stop=(f == NF - 1))
                mm.then_inc(g_y, 1)

            pe.wait_ge(r_blk, 1)
            pe.wait_ge(ld_w2e, 16 * E)
            g_turn(0, 0, 0)
            g_turn(1, 1, 0)
            g_up(0, 0)
            table(1, psum[:, 5, 256:328], gate_to)
            for b in range(2):
                g_up(b + 1, 1 - b)
                g_turn(b + 2, b, 1)
                g_down(b, b)
            with pe.Fori(1, NB_LOOP // 2) as i:
                for j in range(2):
                    b = 2 * i + j
                    g_up(b + 1, 1 - j)
                    g_turn(b + 2, j, i + 1)
                    g_down(b, j)
            filled = pe.value_load(n_blocks, min_val=0, max_val=NB)
            for blocks in NB_TAIL:
                with pe.If(filled > blocks[0]):
                    for b in blocks:
                        if b + 1 < NB:
                            g_up(b + 1, (b + 1) % 2)
                        if b + 2 < NB:
                            g_turn(b + 2, b % 2, (b + 2) // 2)
                        g_down(b, b % 2)

        @block.scalar
        def _(act):
            act.dma_start(cols[:, :], a["cols"]).then_inc(ld_small, 16)
            act.dma_start(rows[:, :], a["rows"].partition_broadcast(P)).then_inc(ld_small, 16)
            act.dma_start(bo_b, a["bo"].partition_broadcast(P)).then_inc(ld_small, 16)
            act.dma_start(b1c[:, :], a["b1"]).then_inc(ld_small, 16)
            act.dma_start(yT, a["yT"].rearrange("(c p) m -> p c m", c=2)).then_inc(ld_y, 16)
            act.dma_start(wk_x, a["xwk"].rearrange("(c p) n -> p c n", c=2)).then_inc(ld_y, 16)
            act.dma_start(wv_x, a["xwv"].rearrange("(c p) n -> p c n", c=2)).then_inc(ld_y, 16)
            act.dma_start(wo_s, a["wo"]).then_inc(ld_ws, 16)
            act.dma_start(wq_x, a["xwq"].rearrange("(c p) n -> p c n", c=KD)).then_inc(ld_ws, 16)
            act.dma_start(w1_x[:, :, :], a["xw1"].rearrange("(c p) n -> p c n", c=KD)).then_inc(ld_ws, 16)
            act.dma_start(w2_x, a["xw2"].rearrange("(c p) n -> p c n", c=NF1)).then_inc(ld_ws, 16)
            act.dma_start(wr[:, :, :], a["wr"].rearrange("(c p) n -> p c n", c=KD)).then_inc(ld_ws, 16)
            def cross_key(i):
                (m0, mn), c = KCH[i // KD], i % KD
                act.wait_ge(k_proj, i + 1)
                act.activation(kf[:, c, m0:m0 + mn], psum[:, 5 + i % 3, 0:mn], ACT.Identity, bias=cols[:, XBK + c:XBK + c + 1],
                               accum_out=ksum[:, c, i // KD:i // KD + 1]).then_inc(k_evac, 1)

            turn_banks = [(5, 6), (0, 1), (5, 6), (5, 6)]
            qk_banks = [(7, 5), (2, 3), (7, 5), (7, 5)]

            def x_turned(q):
                for k in range(KD):
                    act.wait_ge(xn_T, 2 * q + k + 1)
                    if q >= 2:
                        act.wait_ge(qkv_mm, 3 * (q - 1))
                    act.copy(xT[q % 2][:, k, :], psum[:, turn_banks[q][k], :]).then_inc(xT_ok, 1)

            def angles(q):
                for w in range(2):
                    act.wait_ge(qkv_mm, 3 * q + w + 1)
                    if q >= 2:
                        act.wait_ge(lo_ok, 4 * (q - 2) + 2 * w + 2)
                    act.activation(th[q % 2][:, w], psum[:, qk_banks[q][w], :], ACT.Identity, bias=bqk[:, w:w + 1], scale=inv_w[:, 0:1]).then_inc(th_ok, 1)

            def sines(q):
                chunk, th_q, tn_q = ds(q * QC, QC), th[q % 2], tn[q % 2]
                for w in range(2):
                    act.wait_ge(ang_ok, 2 * q + w + 1)
                    act.activation(tn_q[:, w], th_q[:, w], ACT.Abs).then_inc(abs_ok, 1)
                    act.activation(sc_hi[w][:, 1, chunk], th_q[:, w], ACT.Sin).then_inc(act_own, 1)
                    act.wait_ge(abs_ok, 2 * q + w + 1)
                    act.wait_ge(act_own, 4 * q + 2 * w + 1)
                    act.activation(th_q[:, w], th_q[:, w], ACT.Sin).then_inc(sc_ok, 1)
                    act.activation(sc_hi[w][:, 0, chunk], tn_q[:, w], ACT.Sin, bias=half_pi[:, 0:1], scale=-1.0).then_inc(act_own, 1)
                    act.wait_ge(act_own, 4 * q + 2 * w + 2)
                    act.activation(tn_q[:, w], tn_q[:, w], ACT.Sin, bias=half_pi[:, 0:1], scale=-1.0).then_inc(sc_ok, 1)

            act.wait_ge(consts, 4)

            def exp_self(u, i):
                n = S_PAIRS * u + i
                act.wait_ge(s_mm, n + 1)
                first = isinstance(u, int) and u == 0
                if i >= 4:
                    act.wait_ge(s_pv, n - 3)
                    act.wait_ge(s_acc, (S_PAIRS - 1) * u + max(i - 4, 1))
                elif not first:
                    act.wait_ge(s_pv, n - 3)
                    act.wait_ge(s_acc, (S_PAIRS - 1) * (u - 1) + i + 4)
                act.activation(pbuf[:, i % 4, :], psum[:, 2 * (i % 2):2 * (i % 2) + 2, :].rearrange("p b n -> p (b n)"),
                               ACT.Exp, scale=1.0 / math.sqrt(HD)).then_inc(s_exp, 1)

            def tail_xT(u):
                for k in range(KD):
                    act.wait_ge(xn2_T, 2 * u + k + 1)
                    act.copy(xT[0][:, k, :], psum[:, 6 + k, :]).then_inc(x2T_ok, 1)

            def tail_q(u):
                for c in range(KD):
                    act.wait_ge(q_mm, 2 * u + c + 1)
                    if c == 0 and not (isinstance(u, int) and u == 0):
                        act.wait_ge(q_split, u)
                    act.activation(qf[:, c], psum[:, 5 + c, :], ACT.Identity, bias=cols[:, XBQ + c:XBQ + c + 1]).then_inc(q_ok, 1)

            x_turned(0)
            act.wait_ge(col_ok, 2)
            angles(0)
            x_turned(1)
            sines(0)
            angles(1)
            for i in range(S_PAIRS):
                exp_self(0, i)
                if i == 0:
                    x_turned(2)
                    sines(1)
                if i == 1:
                    angles(2)
                if i == 2:
                    x_turned(3)
                    sines(2)
                if i == 3:
                    angles(3)
                if i == 4:
                    sines(3)
                if i >= 6:
                    cross_key(2 * (i - 6))
                    cross_key(2 * (i - 6) + 1)
            for i in range(4, 8):
                cross_key(i)

            def cross_value(t):
                n = P if t < MT - 1 else MLAST
                act.wait_ge(v_proj, t + 1)
                act.copy(vx[0:n, t, :].rearrange("p (h w) -> p h w", w=VW)[:, :, 0:DH],
                         psum[0:n, 5 + t % 3, 0:D].rearrange("p (h d) -> p h d", d=DH)).then_inc(v_evac, 1)

            for t in range(MT):
                cross_value(t)
            with act.Fori(1, NQ) as u:
                for i in range(S_PAIRS):
                    exp_self(u, i)
                    if i == 5:
                        tail_xT(u - 1)
                    if i == 6:
                        tail_q(u - 1)
            act.wait_ge(s_pv, S_PAIRS * NQ)
            act.wait_ge(aT_ok, NQ - 1)
            act.copy(o_raw, psum[:, 4, :]).then_inc(o_evac, 1)

            def exp_cross(u):
                for i in range(2 * MT):
                    t = i // 2
                    n = P if t < MT - 1 else MLAST
                    pair = 2 * (i % 3)
                    act.wait_ge(c_mm, 2 * MT * u + i + 1)
                    if isinstance(u, int) and i == 0:
                        act.wait_ge(s_pv, S_PAIRS * NQ)
                        act.wait_ge(s_acc, (S_PAIRS - 1) * NQ)
                    if 2 <= t < MT - 1:
                        act.wait_ge(c_pv, MT * u + t - 1)
                    elif not isinstance(u, int):
                        act.wait_ge(c_pv, MT * u if t == MT - 1 else MT * u - 2 + t)
                    act.activation(p_slot(i)[0:n, :], psum[0:n, pair:pair + 2, :].rearrange("p b n -> p (b n)"),
                                   ACT.Exp, scale=1.0 / math.sqrt(DH)).then_inc(c_exp, 1)
                    if isinstance(u, int) and i % 2:
                        if t in TURN:
                            k = TURN.index(t)
                            act.wait_ge(xn2_T, 2 * NQ - 1 + k)
                            act.copy(last_xT[:, k, :], psum[:, 7, :]).then_inc(x2T_ok, 1)
                        for c in range(KD):
                            if t == min(QUERIES[c], MT - 1):
                                act.wait_ge(q_mm, 2 * NQ - 1 + c)
                                if c == 0:
                                    act.wait_ge(q_split, NQ - 1)
                                act.activation(qf[:, c], psum[:, 7, :], ACT.Identity, bias=cols[:, XBQ + c:XBQ + c + 1]).then_inc(q_ok, 1)

            exp_cross(0)
            with act.Fori(1, NQ * NG) as u:
                exp_cross(u)

            act.wait_ge(flag_ok, 1)
            with act.If(act.value_load(again[0:1, 0:1], min_val=0, max_val=P) > 0):
                with act.Fori(0, NT * NH) as i:
                    act.wait_ge(m_max, i + 1)
                    sc_m = 1.0 / math.sqrt(DH)
                    act.activation(gp[:, 0:1600].rearrange("p (c n) -> p c n", c=4), psum[:, 0:4, 0:400], ACT.Exp,
                                   bias=small[:, 1:2], scale=sc_m).then_inc(m_exp, 1)
                    act.activation(gp[:, 1600:M], psum[:, 3, 400:401], ACT.Exp, bias=small[:, 1:2], scale=sc_m).then_inc(m_exp, 1)
                    act.wait_ge(m_tr, i + 1)
                    act.copy(gpT[:, 0:MT - 1, :], psum[:, 4:7, :].rearrange("p b (k n) -> p (b k) n", n=P)).then_inc(m_pT, 1)
                    act.copy(gpT[0:MLAST, MT - 1, :], psum[0:MLAST, 7, 0:P]).then_inc(m_pT, 1)

            def xn3_turned(q):
                for k in range(KD):
                    act.wait_ge(r_tr, 2 * q + k + 1)
                    if q:
                        act.wait_ge(r_lg, NT // NQ * q)
                    act.copy(xn3T[:, k, :], psum[:, k, :]).then_inc(r_xT, 1)

            def turned(q):
                for k in range(KD):
                    act.wait_ge(f_tr, 2 * q + k + 1)
                    act.copy(xT[q % 2][:, k, :], psum[:, k, :]).then_inc(f_xT, 1)

            turned(0)
            for q in range(NQ):
                for f in range(NF1):
                    i = NF1 * q + f
                    act.wait_ge(f_h, i + 1)
                    if q:
                        act.wait_ge(f_y, 2 * q)
                    act.activation(h_x[:, f, :], psum[:, 2 + i % 3, :], ACT.Relu, bias=cols[:, XB1 + f:XB1 + f + 1]).then_inc(f_relu, 1)
                if q:
                    xn3_turned(q - 1)
                if q + 1 < NQ:
                    turned(q + 1)
            xn3_turned(NQ - 1)

            act.wait_ge(r_sub, NQ)
            act.wait_ge(f_y, 2 * NQ)
            act.activation(probs, l2, ACT.Exp).then_inc(r_exp, 1)
            act.activation(spare, half_pi[:, :], ACT.Gelu)


            def rows_turned(b, j):
                act.wait_ge(g_tr, b + 1)
                if not (isinstance(b, int) and b < 2):
                    act.wait_ge(g_h, b - 1)
                act.copy(xgT[j], psum[:, 6, 0:KD * P].rearrange("p (k n) -> p k n", k=KD)).then_inc(g_xT, 1)

            def gelu(b, j):
                act.wait_ge(g_h, b + 1)
                if not (isinstance(b, int) and b < 2):
                    act.wait_ge(g_y, b - 1)
                act.wait_ge(g_b1, b + 1)
                for f in range(NF):
                    ins = act.activation(hT[j][:, f, :], psum[:, 2 * j + f // 4, (f % 4) * P:(f % 4) * P + P], ACT.Gelu, bias=b1b[j][:, f:f + 1])
                ins.then_inc(g_act, 1)

            rows_turned(0, 0)
            rows_turned(1, 1)
            gelu(0, 0)
            for b in range(2):
                gelu(b + 1, 1 - b)
                rows_turned(b + 2, b)
            with act.Fori(1, NB_LOOP // 2) as i:
                for j in range(2):
                    b = 2 * i + j
                    gelu(b + 1, 1 - j)
                    rows_turned(b + 2, j)
            filled = act.value_load(n_blocks, min_val=0, max_val=NB)
            for blocks in NB_TAIL:
                with act.If(filled > blocks[0]):
                    for b in blocks:
                        if b + 1 < NB:
                            gelu(b + 1, (b + 1) % 2)
                        if b + 2 < NB:
                            rows_turned(b + 2, b % 2)

        @block.vector
        def _(dve):
            ch = Chain(dve, dve_own)

            def norm_stats(src, stats, mv, nv, nt, rstd, count, before_third=None):
                ch.inc(dve.memset(nv, 0.0))
                for t in range(count):
                    if t == 2 and before_third:
                        before_third()
                    ch.inc(dve.bn_stats(stats[:, t, :], src[:, t, :]))
                ch.wait()
                ch.inc(dve.memset(nt, 0.0))
                for t in range(count):
                    ch.inc(dve.bn_aggr(mv[:, t, :], stats[:, t, :]))
                ch.wait()
                ch.link(dve.tensor_scalar(nv, mv[:, :, 1], EPS, None, ALU.add))
                ch.link(dve.tensor_scalar(rstd.bitcast(I32), nv.bitcast(I32), -0.5, float(0x5F3759DF), ALU.mult, ALU.add))
                for step in range(3):
                    ch.link(dve.tensor_tensor(nt, rstd, rstd, ALU.mult))
                    ch.link(dve.tensor_tensor(nt, nt, nv, ALU.mult))
                    ch.link(dve.tensor_scalar(nt, nt, -0.5, 1.5, ALU.mult, ALU.add))
                    ins = dve.tensor_tensor(rstd, rstd, nt, ALU.mult)
                    if step < 2:
                        ch.link(ins)
                return ins

            def rsqrt_norm(src, dst, signal, before_third=None):
                ch.link(norm_stats(src, stats, mv, nv[:, :], nt1[:, :], rstd[:, :], TPC, before_third))
                for t in range(TPC):
                    ins = dve.tensor_scalar(dst[:, t, :], src[:, t, :], mv[:, t, 0:1], rstd[:, t:t + 1], ALU.subtract, ALU.mult)
                    if t < TPC - 1:
                        ch.inc(ins)
                ins.then_inc(signal, 1)

            dve.memset(vx.rearrange("p t (h w) -> p t h w", w=VW)[:, :, :, DH:VW], 1.0).then_inc(ones_ok, 1)
            dve.memset(rmin[:, :, :], 1.0).then_inc(q_stored, 48)

            def norm1(q):
                dve.wait_ge(ld_x[q], 16)
                rsqrt_norm(res[:, q * TPC:(q + 1) * TPC, :], xn1[:, q * TPC:(q + 1) * TPC, :], xn_ok)

            def angles(q):
                for w in range(2):
                    th_q = th[q % 2][:, w]
                    dve.wait_ge(th_ok, 2 * q + w + 1)
                    ch.link(dve.tensor_scalar(turns, th_q, 1.0 / TWO_PI, MAGIC, ALU.mult, ALU.add))
                    ch.link(dve.tensor_scalar(turns, turns, MAGIC, None, ALU.subtract))
                    ch.link(dve.scalar_tensor_tensor(out=th_q, in0=turns, scalar=-C1, in1=th_q, op0=ALU.mult, op1=ALU.add))
                    ch.link(dve.scalar_tensor_tensor(out=th_q, in0=turns, scalar=-C2, in1=th_q, op0=ALU.mult, op1=ALU.add))
                    dve.tensor_scalar(th_q, th_q, PI_IN, -PI_IN, ALU.min, ALU.max).then_inc(ang_ok, 1)
                    if w == 0:
                        self_values(q)

            v_banks = [6, 4, 6, 6]

            def self_values(q):
                dve.wait_ge(qkv_mm, 3 * q + 3)
                dve.tensor_copy(v_s[:, q * TPC:(q + 1) * TPC, :], psum[:, v_banks[q], :].rearrange("p (t n) -> p t n", n=P)).then_inc(v_ok, 1)

            norm1(0)
            dve.wait_ge(ld_small, 64)
            ch.link(dve.tensor_scalar(inv_w[:, 1:2], cols[:, WL:WL + 1], 1e-8, None, ALU.add))
            ch.link(dve.reciprocal(inv_w[:, 0:1], inv_w[:, 1:2]))
            dve.tensor_scalar(bqk[:, 0:1], cols[:, BQ:BQ + 1], inv_w[:, 0:1], cols[:, PH:PH + 1], ALU.mult, ALU.add).then_inc(col_ok, 1)
            dve.tensor_scalar(bqk[:, 1:2], cols[:, BK:BK + 1], inv_w[:, 0:1], cols[:, PH:PH + 1], ALU.mult, ALU.add).then_inc(col_ok, 1)
            norm1(1)
            angles(0)

            def norm_late(q):
                for t in range(q * TPC, (q + 1) * TPC):
                    late = t - 2 * TPC
                    ins = dve.tensor_scalar(xn1[:, t, :], res[:, t, :], mv_late[:, late, 0:1], rstd_late[:, late:late + 1], ALU.subtract, ALU.mult)
                ins.then_inc(xn_ok, 1)

            for q in (2, 3):
                dve.wait_ge(ld_x[q], 16)
            norm_stats(res[:, 2 * TPC:NT, :], stats_late, mv_late, nv_late, nt_late, rstd_late, 2 * TPC).then_inc(norm_ok, 1)
            dve.wait_ge(norm_ok, 1)
            norm_late(2)
            angles(1)
            norm_late(3)
            angles(2)

            def accumulate(u, i):
                a_ = acc0 if isinstance(u, int) else acc
                dve.wait_ge(s_exp, S_PAIRS * u + i + 1)
                if i == 1:
                    dve.tensor_tensor(a_, pbuf[:, 0, :], pbuf[:, 1, :], ALU.add).then_inc(s_acc, 1)
                else:
                    dve.wait_ge(s_acc, (S_PAIRS - 1) * u + i - 1)
                    dve.tensor_tensor(a_, a_, pbuf[:, i % 4, :], ALU.add).then_inc(s_acc, 1)

            def total(u):
                a_ = acc0 if isinstance(u, int) else acc
                dve.wait_ge(s_acc, (S_PAIRS - 1) * (u + 1))
                dve.tensor_tensor(acc1, a_[:, 0:QC], a_[:, QC:2 * QC], ALU.add).then_inc(acc_ok, 1)
                dve.wait_ge(acc_ok, u + 1)

            def tail_out(u):
                dve.wait_ge(s_pv, S_PAIRS * (u + 1))
                dve.tensor_copy(o_raw, psum[:, 4, :]).then_inc(o_evac, 1)

            def tail_norm(u):
                dve.wait_ge(den_mm, u + 1)
                ch.inc(dve.reciprocal(rden, psum[:, 7, :]))
                ch.wait()
                dve.wait_ge(o_evac, u + 1)
                ch.link(dve.tensor_tensor(aT, o_raw, rden, ALU.mult))
                dve.tensor_scalar(aT, aT, cols[:, BV:BV + 1], None, ALU.add).then_inc(aT_ok, 1)

            def tail_res(u):
                dve.wait_ge(wo_mm, u + 1)
                r = res[:, ds(u * TPC, TPC), :]
                ch.link(dve.tensor_tensor(r.rearrange("p t n -> p (t n)"), r.rearrange("p t n -> p (t n)"),
                                          psum[:, 6:8, :].rearrange("p b n -> p (b n)"), ALU.add))
                rsqrt_norm(r, xn2, xn2_ok)

            def last_res():
                r = res[:, (NQ - 1) * TPC:NQ * TPC, :]
                for h in range(2):
                    dve.wait_ge(wo_mm, NQ + h)
                    half = r[:, 2 * h:2 * h + 2, :].rearrange("p t n -> p (t n)")
                    dve.tensor_tensor(half, half, psum[:, 7, :], ALU.add).then_inc(res_half, 1)
                dve.wait_ge(res_half, 2)
                rsqrt_norm(r, xn2, xn2_ok)

            def split_q(u):
                dve.wait_ge(q_ok, 2 * u + 2)
                dve.wait_ge(q_stored, 48 * (u + 1))
                ch.link(dve.tensor_copy(q_bf[:, 0], qf))
                ch.link(dve.tensor_tensor(qf, qf, q_bf[:, 0], ALU.subtract))
                ch.link(dve.tensor_copy(q_bf[:, 1], qf))
                ch.link(dve.tensor_tensor(qf, qf, q_bf[:, 1], ALU.subtract))
                dve.tensor_copy(q_bf[:, 2], qf).then_inc(q_split, 1)

            for i in range(1, S_PAIRS):
                accumulate(0, i)
                if i == 2:
                    angles(3)
            dve.wait_ge(lo_ok, 4 * NQ)
            dve.wait_ge(bo_added, NQ)
            total(0)
            with dve.Fori(0, NQ - 1) as v:
                ch.enter(v, TAIL_LINKS)
                tail_out(v)
                for i in range(1, S_PAIRS):
                    accumulate(v + 1, i)
                    if i == 1:
                        tail_norm(v)
                    if i == 3:
                        tail_res(v)
                total(v + 1)
                split_q(v)
                ch.leave(NQ - 1)
            dve.memset(psum[:, 6, :], 0.0).then_inc(o_clear, 1)
            tail_norm(NQ - 1)
            last_res()

            for g in range(NG):
                with dve.Fori(0, NQ) as qc:
                    ch.enter(qc, 3)
                    u = qc + NQ * g
                    dve.wait_ge(c_pv, MT * u + MT)
                    dve.tensor_copy(oT[g], psum[:, 6, :]).then_inc(c_evac, 1)
                    dve.wait_ge(c_tr, u + 1)
                    o_v = psum[:, 7, :].rearrange("p (t h w) -> p t h w", t=TPC, h=G)
                    ch.link(dve.reciprocal(rden_x[:, :, :], o_v[:, :, :, DH]))
                    ch.inc(dve.tensor_tensor(rmin[:, :, :], rmin[:, :, :], rden_x[:, :, :], ALU.min))
                    heads = slice(g * G * DH, (g + 1) * G * DH)
                    ch.link(dve.tensor_tensor(xo[:, ds(qc * TPC, TPC), heads].rearrange("p t (h d) -> p t h d", d=DH),
                                              o_v[:, :, :, 0:DH], rden_x[:, :, :].unsqueeze(3).to_broadcast([P, TPC, G, DH]), ALU.mult))
                    dve.tensor_tensor(xo[:, ds(qc * TPC, TPC), heads], xo[:, ds(qc * TPC, TPC), heads],
                                      bv_b[:, heads].unsqueeze(1).to_broadcast([P, TPC, G * DH]), ALU.add).then_inc(c_xo, 1)
                    ch.leave(NQ)

            ch.wait()
            dve.wait_ge(c_xo, NQ * NG)
            ch.link(dve.tensor_reduce(small[:, 1:2], rmin[:, :, :], AX.XY, ALU.min))
            dve.tensor_scalar(small[:, 0:1], small[:, 1:2], LEAST_RECIPROCAL, None, ALU.is_lt).then_inc(bad_ok, 1)
            dve.wait_ge(bad_mm, 1)
            dve.tensor_copy(again[:, :], psum[:, 7, 0:1]).then_inc(flag_ok, 1)
            dve.wait_ge(flag_ok, 1)
            with dve.If(dve.value_load(again[0:1, 0:1], min_val=0, max_val=P) > 0):
                dve.memset(small[:, 0:1], 0.0).then_inc(m_out, 1)
                with dve.Fori(0, NH) as h:
                    with dve.Fori(0, NT) as t:
                        i = h * NT + t
                        dve.wait_ge(m_out, i + 1)
                        dve.wait_ge(m_mm, i + 1)
                        dve.tensor_reduce(small[:, 0:1], psum[:, 0:4, 0:401], AX.XY, ALU.max).then_inc(m_red, 1)
                        dve.wait_ge(m_red, 2 * i + 1)
                        dve.tensor_scalar(small[:, 1:2], small[:, 0:1], -1.0 / math.sqrt(DH), None, ALU.mult).then_inc(m_max, 1)
                        dve.wait_ge(m_pv, i + 1)
                        dve.reciprocal(rden_x[:, 0, 0:1], psum[:, 0, DH:VW]).then_inc(m_red, 1)
                        dve.wait_ge(m_red, 2 * i + 2)
                        dve.scalar_tensor_tensor(out=duo[:, ds(t * D + h * DH, DH)], in0=psum[:, 0, 0:DH], scalar=rden_x[:, 0, 0:1],
                                                 in1=rows[:, ds(D + h * DH, DH)], op0=ALU.mult, op1=ALU.add).then_inc(m_out, 1)

            dve.wait_ge(b2_added, 1)

            def choose(q):
                tiles = slice(q * TPC, (q + 1) * TPC)
                dve.wait_ge(r_lg, TPC * (q + 1))
                if q:
                    dve.wait_ge(r_rank, q)
                else:
                    dve.wait_ge(late_consts, 6)
                ch.link(dve.tensor_tensor(lg, psum[:, 5, TPC * E * q:TPC * E * (q + 1)].rearrange("p (t e) -> p t e", e=E),
                                          br_b.unsqueeze(1).to_broadcast([P, TPC, E]), ALU.add))
                ch.link(dve.tensor_reduce(lmax, lg, AX.X, ALU.max))
                lmax_b = lmax.unsqueeze(2).to_broadcast([P, TPC, E])
                revi_b = revi[:, :].unsqueeze(1).to_broadcast([P, TPC, E])
                dve.tensor_tensor(l2[:, tiles, :], lg, lmax_b, ALU.subtract).then_inc(r_sub, 1)
                ch.link(dve.tensor_tensor(oneh[:, tiles, :], lg, lmax_b, ALU.is_equal))
                ch.link(dve.tensor_tensor(oneh[:, tiles, :], oneh[:, tiles, :], revi_b, ALU.mult))
                ch.link(dve.tensor_reduce(top[:, :], oneh[:, tiles, :], AX.X, ALU.max))
                dve.tensor_tensor(oneh[:, tiles, :], revi_b, top[:, :].unsqueeze(2).to_broadcast([P, TPC, E]), ALU.is_equal).then_inc(r_one, 1)
                dve.wait_ge(r_one, q + 1)

            def place(q):
                tiles = slice(q * TPC, (q + 1) * TPC)
                dve.wait_ge(r_rank, q + 1)
                in_bank = lambda i: psum[:, 5, P + TPC * E * i:P + TPC * E * (i + 1)].rearrange("p (t e) -> p t e", e=E)
                for t in range(TPC):
                    ch.link(dve.tensor_tensor(base[:, q * TPC + t + 1, :], base[:, q * TPC + t, :], in_bank(1)[:, t, :], ALU.add))
                dve.tensor_tensor(lg, in_bank(0), base[:, tiles, :], ALU.add).then_inc(r_used, 1)
                dve.wait_ge(r_used, q + 1)
                ch.link(dve.tensor_tensor(lg, lg, oneh[:, tiles, :], ALU.mult))
                ch.link(dve.tensor_reduce(rank[:, tiles], lg, AX.X, ALU.add))
                ch.link(dve.tensor_scalar(full[:, tiles], rank[:, tiles], 1.0 / P, -0.5 + 0.5 / P, ALU.mult, ALU.add))
                ch.link(dve.tensor_scalar(full[:, tiles], full[:, tiles], MAGIC, None, ALU.add))
                ch.link(dve.tensor_scalar(full[:, tiles], full[:, tiles], MAGIC, None, ALU.subtract))
                ch.link(dve.scalar_tensor_tensor(out=rank[:, tiles], in0=full[:, tiles], scalar=-float(P), in1=rank[:, tiles],
                                                 op0=ALU.mult, op1=ALU.add))
                dve.wait_ge(row_st[0], 32)
                ch.inc(dve.tensor_tensor(in_block[:, tiles, :], lane.unsqueeze(1).to_broadcast([P, TPC, P]),
                                         rank[:, tiles].unsqueeze(2).to_broadcast([P, TPC, P]), ALU.is_equal))

            ch.inc(dve.memset(base[:, 0, :], 0.0))
            for i in range(2):
                ch.inc(dve.memset(cum[i], 0.0))
            for q in range(NQ):
                if q == NQ - 1:
                    choose(q - 1)
                    place(q - 2)
                r = res[:, q * TPC:(q + 1) * TPC, :]

                def add(h):
                    dve.wait_ge(f_y, 2 * q + h + 1)
                    half = r[:, 2 * h:2 * h + 2, :].rearrange("p t n -> p (t n)")
                    dve.tensor_tensor(half, half, psum[:, 6 + h, :], ALU.add).then_inc(f_res, 1)
                    dve.wait_ge(f_res, 2 * q + h + 1)

                add(0)
                rsqrt_norm(r, xn[:, q * TPC:(q + 1) * TPC, :], xn3_ok, lambda: add(1))
                if 0 < q < NQ - 1:
                    choose(q - 1)
                    if q >= 2:
                        place(q - 2)
            place(NQ - 2)
            choose(NQ - 1)
            place(NQ - 1)

            e_cols = slice(4, 4 + E)
            ch.link(dve.tensor_scalar(nb, base[:, NT, :], 1.0 / P, 0.5 - 0.5 / P, ALU.mult, ALU.add))
            ch.link(dve.tensor_scalar(nb, nb, MAGIC, None, ALU.add))
            ch.link(dve.tensor_scalar(cum[0][:, e_cols], nb, MAGIC, None, ALU.subtract))
            cc = 0
            for s_ in (1, 2, 4):
                ch.link(dve.tensor_tensor(cum[1 - cc][:, e_cols], cum[cc][:, e_cols], cum[cc][:, 4 - s_:4 - s_ + E], ALU.add))
                cc = 1 - cc
            first_block = cum[cc][:, 3:3 + E].unsqueeze(1).to_broadcast([P, NT, E])
            ch.link(dve.tensor_tensor(prod, oneh, first_block, ALU.mult))
            ch.link(dve.tensor_reduce(top_all, prod, AX.X, ALU.add))
            ch.link(dve.tensor_tensor(full[:, :], full[:, :], top_all, ALU.add))
            per_block = lambda x: x.unsqueeze(2).to_broadcast([P, NT, 24])
            dve.tensor_tensor(to_block[:, :, 2, :], bl_i.unsqueeze(1).to_broadcast([P, NT, 24]), per_block(full[:, :]), ALU.is_equal).then_inc(r_to, 1)
            dve.wait_ge(r_to, 1)
            dve.tensor_scalar(to_block[:, :, 0, :], to_block[:, :, 2, :], own_row, None, ALU.mult).then_inc(r_to, 1)
            dve.tensor_tensor(to_block[:, :, 1, :], to_block[:, :, 2, :], per_block(tile_i), ALU.mult).then_inc(r_to, 1)
            ch.link(dve.tensor_tensor(bl_c, bl_i.unsqueeze(2).to_broadcast([P, 24, E]), cum[cc][:, e_cols].unsqueeze(1).to_broadcast([P, 24, E]), ALU.is_ge))
            ch.inc(dve.tensor_copy(n_blocks, cum[cc][0:1, 3 + E:4 + E]))
            ch.link(dve.tensor_reduce(bl_f, bl_c[:, :, 0:E - 1], AX.X, ALU.add))
            dve.tensor_copy(bl_e, bl_f).then_inc(r_blk, 1)
            dve.wait_ge(r_table, 1)
            ch.link(dve.tensor_copy(bl_t, psum[:, 7, 0:24]))
            ch.link(dve.scalar_tensor_tensor(out=token_f, in0=psum[:, 7, 24:48], scalar=float(P), in1=bl_t, op0=ALU.mult, op1=ALU.add))
            dve.tensor_copy(token_in, token_f).then_inc(r_slots, 1)
            ch.link(dve.tensor_scalar(filled_f, psum[:, 7, 48:72], -1.0, 1.0, ALU.mult, ALU.add))
            ch.link(dve.tensor_scalar(filled_f, filled_f, pad_row, None, ALU.mult))
            ch.link(dve.tensor_tensor(filled_f, filled_f, token_f, ALU.add))
            dve.tensor_copy(token_out, filled_f).then_inc(r_slots, 2)
            def expert(b):
                return dve.value_load(bl_e[0:1, ds(b, 1)], min_val=0, max_val=E - 1)

            def weights(b, j):
                e = expert(b)
                if not (isinstance(b, int) and b < 2):
                    dve.wait_ge(g_h, b - 1)
                    dve.wait_ge(g_act, b - 1)
                dve.tensor_copy(w1s[j], w1v[:, :, ds(e * F, F)]).then_inc(g_w, 1)
                dve.tensor_copy(b1b[j], b1c[:, ds(e * NF, NF)]).then_inc(g_b1, 1)

            dve.wait_ge(r_blk, 1)
            dve.wait_ge(ld_w1e, 32)
            weights(0, 0)
            dve.wait_ge(r_exp, 1)
            ch.link(dve.tensor_reduce(gate[:, :], probs, AX.X, ALU.add))
            ch.link(dve.reciprocal(gate[:, :], gate[:, :]))
            for j in range(3):
                ch.link(dve.tensor_copy(gate_parts[:, j], gate[:, :]))
                if j < 2:
                    ch.inc(dve.tensor_tensor(gate[:, :], gate[:, :], gate_parts[:, j], ALU.subtract))
                dve.tensor_tensor(gate_to[:, :, j, :], to_block[:, :, 2, :], per_block(gate_parts[:, j]), ALU.mult).then_inc(r_to, 1)
                ch.wait()

            def residuals(b, j, half):
                dve.wait_ge(g_ld[j], 16 * (half + 1))
                dve.tensor_copy(rs[j], xg[j][:, D:2 * D]).then_inc(g_rs, 1)

            def result(b, j, half):
                e = expert(b)
                dve.wait_ge(g_y, b + 1)
                if not (isinstance(b, int) and b < 2):
                    dve.wait_ge(g_st[j], 16 * half)
                dve.tensor_tensor(ys[j], psum[:, down_bank[j], 0:D], b2e[:, ds(e * D, D)], ALU.add).then_inc(g_sum, 1)
                dve.tensor_copy(gate_b, slot_gate[:, ds(b, 1)]).then_inc(g_gate, 1)
                dve.wait_ge(g_sum, b + 1)
                dve.wait_ge(g_gate, b + 1)
                dve.wait_ge(g_rs, b + 1)
                dve.scalar_tensor_tensor(out=ys[j], in0=ys[j], scalar=gate_b, in1=rs[j], op0=ALU.mult, op1=ALU.add).then_inc(g_ys, 1)
                dve.wait_ge(g_ys, b + 1)

            residuals(0, 0, 0)
            weights(1, 1)
            residuals(1, 1, 0)
            dve.wait_ge(r_table, 2)
            ch.link(dve.tensor_copy(slot_gate, psum[:, 5, 304:328]))
            ch.link(dve.tensor_tensor(slot_gate, slot_gate, psum[:, 5, 280:304], ALU.add))
            dve.tensor_tensor(slot_gate, slot_gate, psum[:, 5, 256:280], ALU.add).then_inc(r_slots, 1)
            dve.wait_ge(r_slots, 4)
            dve.wait_ge(ld_b2e, 16)
            for b in range(2):
                weights(b + 2, b)
                result(b, b, 0)
                residuals(b + 2, b, 1)
            with dve.Fori(1, NB_LOOP // 2) as i:
                for j in range(2):
                    b = 2 * i + j
                    weights(b + 2, j)
                    result(b, j, i)
                    residuals(b + 2, j, i + 1)
            filled = dve.value_load(n_blocks, min_val=0, max_val=NB)
            for blocks in NB_TAIL:
                with dve.If(filled > blocks[0]):
                    for b in blocks:
                        if b + 2 < NB:
                            weights(b + 2, b % 2)
                        result(b, b % 2, b // 2)
                        if b + 2 < NB:
                            residuals(b + 2, b % 2, b // 2 + 1)


def kernel(**inputs):
    import numpy as np
    import concourse.bacc as bacc
    from concourse.bass_utils import run_bass_kernel_spmd

    v = {k: np.ascontiguousarray(x) for k, x in inputs.items()}
    c = lambda x, n: x.reshape(n, P).T
    arrays = {
        "x": v["x"],
        "yT": v["ctx_768"][0].T,
        "wqkv": np.stack([v["L0_attn_Wq"].T, v["L0_attn_Wk"].T, v["L0_attn_Wv"].T]),
        "wo": v["L0_attn_Wo"].T,
        "xwq": v["L0_xattn_Wq"], "xwk": v["L0_xattn_Wk"], "xwv": v["L0_xattn_Wv"], "xw1": v["L0_xattn_W1"], "xw2": v["L0_xattn_W2"],
        "wr": v["L0_ffn_Wr"], "w1": v["L0_ffn_W1"], "w2": v["L0_ffn_W2"],
        "b1": c(v["L0_ffn_b1"], E * NF), "b2": v["L0_ffn_b2"].reshape(-1),
        "cols": np.concatenate([c(v["L0_attn_bq"], 1), c(v["L0_attn_phase_bias"], 1), c(v["L0_attn_wavelengths"], 1), c(v["L0_attn_bk"], 1),
                                c(v["L0_attn_bv"], 1), c(v["L0_xattn_bq"], 2), c(v["L0_xattn_bk"], 2), c(v["L0_xattn_b1"], 4)], axis=1),
        "rows": np.concatenate([v["L0_xattn_b2"], v["L0_xattn_bv"], v["L0_ffn_br"]]), "bo": v["L0_attn_bo"],
    }
    nc = bacc.Bacc("TRN2", target_bir_lowering=False, num_devices=1)
    feeds, args = {}, {}
    for name, x in arrays.items():
        x = np.ascontiguousarray(x)
        feeds[f"in_{name}"] = x
        args[name] = nc.dram_tensor(f"in_{name}", x.shape, mybir.dt.from_np(x.dtype), kind="ExternalInput").ap()
    out = nc.dram_tensor("out_0", (1, T, D), F32, kind="ExternalOutput").ap()
    layer(nc, args, out)
    r = run_bass_kernel_spmd(nc, [feeds], core_ids=[0])
    return r.results[0]["out_0"]
```
